# Optimizing a Trainium2 kernel written in Bass

```python
import numpy as np
import jax
import jax.numpy as jnp

def _softmax(x, axis=-1):
    return jax.nn.softmax(x, axis=axis)

def _gelu(x):
    return jax.nn.gelu(x, approximate=True)

def _silu(x):
    return jax.nn.silu(x)

def _sigmoid(x):
    return jax.nn.sigmoid(x)

def _layernorm(x, axis=-1, eps=1e-05):
    m = jnp.mean(x, axis=axis, keepdims=True)
    v = jnp.var(x, axis=axis, keepdims=True)
    return (x - m) / jnp.sqrt(v + eps)

def _scatter_add(tgt, idx, src, axis=0):
    return tgt.at[idx].add(src)

def _segment_sum(src, seg, n):
    return jax.ops.segment_sum(src, seg, n)
kernel_name = 'mk_recurrent_d1_jaxref_r4_876766'

def setup_inputs(seed: int=0):
    np.random.seed(seed)
    _w = jnp.asarray

    def _L0_attn_setup():
        import jax, jax.numpy as jnp
        import numpy as np
        DIM = 256
        HEADS = 16
        HEAD_DIM = DIM // HEADS
        SCALE = HEAD_DIM ** (-0.5)

        def apply_rope(x, theta=10000.0):
            n, d = (x.shape[2], x.shape[3])
            seq = jnp.arange(n, dtype=jnp.float32)
            inv = 1.0 / theta ** (jnp.arange(0, d, 2, dtype=jnp.float32) / d)
            freqs = seq[:, None] * inv[None, :]
            cos = jnp.cos(freqs)[None, None]
            sin = jnp.sin(freqs)[None, None]
            x1, x2 = jnp.split(x, 2, axis=-1)
            return jnp.concatenate([x1 * cos - x2 * sin, x1 * sin + x2 * cos], axis=-1)
        key = jax.random.key(seed)
        ks = jax.random.split(key, 7)
        s = DIM ** (-0.5)
        return {'x': jax.random.normal(ks[0], (2, 512, DIM), dtype=jnp.float32), 'Wqkv': jax.random.normal(ks[1], (3 * DIM, DIM), dtype=jnp.float32) * s, 'bqkv': jax.random.normal(ks[2], (3 * DIM,), dtype=jnp.float32) * 0.02, 'Wpre': jax.random.normal(ks[3], (HEADS, HEADS), dtype=jnp.float32) * HEADS ** (-0.5), 'Wpost': jax.random.normal(ks[4], (HEADS, HEADS), dtype=jnp.float32) * HEADS ** (-0.5), 'Wout': jax.random.normal(ks[5], (DIM, DIM), dtype=jnp.float32) * s, 'bout': jax.random.normal(ks[6], (DIM,), dtype=jnp.float32) * 0.02}
    _L0_attn_in = _L0_attn_setup()

    def _L0_ffn_setup():
        import jax, jax.numpy as jnp
        import numpy as np
        DIM = 256
        DEPTH = 2
        HEADS = 8
        DIM_HEAD = 64
        WINDOW = 128
        INNER = HEADS * DIM_HEAD
        HID = int(DIM * 4 * 2 / 3)
        B, N = (2, 2048)
        QK_SCALE = 8.0

        def shift_token(t):
            t1, t2 = jnp.split(t, 2, axis=-1)
            t2 = jnp.pad(t2, ((0, 0), (1, 0), (0, 0)))[:, :-1]
            return jnp.concatenate([t1, t2], axis=-1)

        def l2norm(t):
            return t / jnp.clip(jnp.linalg.norm(t, axis=-1, keepdims=True), 1e-12)

        def rotate_half(x):
            x1, x2 = jnp.split(x, 2, axis=-1)
            return jnp.concatenate([-x2, x1], axis=-1)

        def rotary_xpos(q, k):
            n = q.shape[-2]
            half_idx = jnp.arange(0, DIM_HEAD, 2, dtype=jnp.float32)
            inv_freq = 1.0 / 10000.0 ** (half_idx / DIM_HEAD)
            t = jnp.arange(n, dtype=jnp.float32)
            freqs = t[:, None] * inv_freq[None, :]
            freqs = jnp.concatenate([freqs, freqs], axis=-1)
            base = (half_idx + 0.4 * DIM_HEAD) / (1.4 * DIM_HEAD)
            power = (t - n // 2) / float(WINDOW // 2)
            scale = base[None, :] ** power[:, None]
            scale = jnp.concatenate([scale, scale], axis=-1)
            cos, sin = (jnp.cos(freqs), jnp.sin(freqs))
            q = q * cos * scale + rotate_half(q) * sin * scale
            k = k * cos / scale + rotate_half(k) * sin / scale
            return (q, k)

        def local_attention(q, k, v):
            b, h, n, d = q.shape
            w = n // WINDOW
            bq = q.reshape(b, h, w, WINDOW, d) * QK_SCALE
            bk = k.reshape(b, h, w, WINDOW, d)
            bv = v.reshape(b, h, w, WINDOW, d)

            def look_around(t):
                p = jnp.pad(t, ((0, 0), (0, 0), (1, 0), (0, 0), (0, 0)))
                return jnp.concatenate([p[:, :, :w], p[:, :, 1:]], axis=3)
            bk, bv = (look_around(bk), look_around(bv))
            bt = jnp.arange(n).reshape(w, WINDOW)
            btp = jnp.pad(bt, ((1, 0), (0, 0)), constant_values=-1)
            btk = jnp.concatenate([btp[:w], btp[1:]], axis=1)
            sim = jnp.einsum('bhwid,bhwjd->bhwij', bq, bk)
            i = bt[:, :, None]
            j = btk[:, None, :]
            mask = (i < j) | (i > j + WINDOW) | (j == -1)
            sim = jnp.where(mask, -jnp.finfo(sim.dtype).max, sim)
            attn = jax.nn.softmax(sim, axis=-1)
            out = jnp.einsum('bhwij,bhwjd->bhwid', attn, bv)
            return out.reshape(b, h, n, d)

        def _layer(x, wqkv, qs, ksc, wo, lg, lb, w1, b1, w2, b2):
            b, n, _ = x.shape
            h = shift_token(x)
            qkv = h @ wqkv
            q, k, v = jnp.split(qkv, 3, axis=-1)
            to_heads = lambda t: t.reshape(b, n, HEADS, DIM_HEAD).transpose(0, 2, 1, 3)
            q, k, v = (to_heads(q), to_heads(k), to_heads(v))
            q = l2norm(q) * qs
            k = l2norm(k) * ksc
            q, k = rotary_xpos(q, k)
            o = local_attention(q, k, v)
            o = o.transpose(0, 2, 1, 3).reshape(b, n, INNER)
            x = x + o @ wo
            h = shift_token(x)
            mu = h.mean(-1, keepdims=True)
            var = h.var(-1, keepdims=True)
            h = (h - mu) / jnp.sqrt(var + 1e-05) * lg + lb
            h = h @ w1 + b1
            a, g = jnp.split(h, 2, axis=-1)
            h = a * jax.nn.gelu(g, approximate=False)
            x = x + h @ w2 + b2
            return x
        key = jax.random.key(seed)
        ks = jax.random.split(key, 6)
        return {'x': jax.random.normal(ks[0], (B, N, DIM), jnp.float32), 'wqkv': jax.random.normal(ks[1], (DEPTH, DIM, 3 * INNER), jnp.float32) * 0.02, 'q_scale': jnp.ones((DEPTH, DIM_HEAD), jnp.float32), 'k_scale': jnp.ones((DEPTH, DIM_HEAD), jnp.float32), 'wo': jax.random.normal(ks[2], (DEPTH, INNER, DIM), jnp.float32) * 0.02, 'ln_g': jnp.ones((DEPTH, DIM), jnp.float32), 'ln_b': jnp.zeros((DEPTH, DIM), jnp.float32), 'w1': jax.random.normal(ks[3], (DEPTH, DIM, 2 * HID), jnp.float32) * 0.02, 'b1': jnp.zeros((DEPTH, 2 * HID), jnp.float32), 'w2': jax.random.normal(ks[4], (DEPTH, HID, DIM), jnp.float32) * 0.02, 'b2': jnp.zeros((DEPTH, DIM), jnp.float32)}
    _L0_ffn_in = _L0_ffn_setup()
    _d = {'L0_attn_x': _L0_attn_in['x'], 'L0_attn_Wqkv': _L0_attn_in['Wqkv'], 'L0_attn_bqkv': _L0_attn_in['bqkv'], 'L0_attn_Wpre': _L0_attn_in['Wpre'], 'L0_attn_Wpost': _L0_attn_in['Wpost'], 'L0_attn_Wout': _L0_attn_in['Wout'], 'L0_attn_bout': _L0_attn_in['bout'], 'L0_ffn_wqkv': _L0_ffn_in['wqkv'], 'L0_ffn_q_scale': _L0_ffn_in['q_scale'], 'L0_ffn_k_scale': _L0_ffn_in['k_scale'], 'L0_ffn_wo': _L0_ffn_in['wo'], 'L0_ffn_ln_g': _L0_ffn_in['ln_g'], 'L0_ffn_ln_b': _L0_ffn_in['ln_b'], 'L0_ffn_w1': _L0_ffn_in['w1'], 'L0_ffn_b1': _L0_ffn_in['b1'], 'L0_ffn_w2': _L0_ffn_in['w2'], 'L0_ffn_b2': _L0_ffn_in['b2']}
    _x0 = _d['L0_attn_x']
    _d['L0_attn_x'] = jax.random.normal(jax.random.fold_in(jax.random.key(seed), 1), (16, 512, 256), dtype=_x0.dtype)
    del _x0
    return _d

def reference(L0_attn_x, L0_attn_Wqkv, L0_attn_bqkv, L0_attn_Wpre, L0_attn_Wpost, L0_attn_Wout, L0_attn_bout, L0_ffn_wqkv, L0_ffn_q_scale, L0_ffn_k_scale, L0_ffn_wo, L0_ffn_ln_g, L0_ffn_ln_b, L0_ffn_w1, L0_ffn_b1, L0_ffn_w2, L0_ffn_b2):

    def _L0_attn_ref(x, Wqkv, bqkv, Wpre, Wpost, Wout, bout):
        import jax, jax.numpy as jnp
        import numpy as np
        DIM = 256
        HEADS = 16
        HEAD_DIM = DIM // HEADS
        SCALE = HEAD_DIM ** (-0.5)

        def apply_rope(x, theta=10000.0):
            n, d = (x.shape[2], x.shape[3])
            seq = jnp.arange(n, dtype=jnp.float32)
            inv = 1.0 / theta ** (jnp.arange(0, d, 2, dtype=jnp.float32) / d)
            freqs = seq[:, None] * inv[None, :]
            cos = jnp.cos(freqs)[None, None]
            sin = jnp.sin(freqs)[None, None]
            x1, x2 = jnp.split(x, 2, axis=-1)
            return jnp.concatenate([x1 * cos - x2 * sin, x1 * sin + x2 * cos], axis=-1)
        b, n, _ = x.shape
        qkv = x @ Wqkv.T + bqkv
        q, k, v = jnp.split(qkv, 3, axis=-1)
        reshape = lambda t: t.reshape(b, n, HEADS, HEAD_DIM).transpose(0, 2, 1, 3)
        q, k, v = (reshape(q), reshape(k), reshape(v))
        q = apply_rope(q)
        k = apply_rope(k)
        logits = jnp.einsum('bhid,bhjd->bhij', q, k) * SCALE
        logits = jnp.einsum('bhij,gh->bgij', logits, Wpre)
        attn = jax.nn.softmax(logits, axis=-1)
        attn = jnp.einsum('bhij,gh->bgij', attn, Wpost)
        out = jnp.einsum('bhij,bhjd->bhid', attn, v)
        out = out.transpose(0, 2, 1, 3).reshape(b, n, DIM)
        return out @ Wout.T + bout

    def _L0_ffn_ref(x, wqkv, q_scale, k_scale, wo, ln_g, ln_b, w1, b1, w2, b2):
        import jax, jax.numpy as jnp
        import numpy as np
        DIM = 256
        DEPTH = 2
        HEADS = 8
        DIM_HEAD = 64
        WINDOW = 128
        INNER = HEADS * DIM_HEAD
        HID = int(DIM * 4 * 2 / 3)
        B, N = (2, 2048)
        QK_SCALE = 8.0

        def shift_token(t):
            t1, t2 = jnp.split(t, 2, axis=-1)
            t2 = jnp.pad(t2, ((0, 0), (1, 0), (0, 0)))[:, :-1]
            return jnp.concatenate([t1, t2], axis=-1)

        def l2norm(t):
            return t / jnp.clip(jnp.linalg.norm(t, axis=-1, keepdims=True), 1e-12)

        def rotate_half(x):
            x1, x2 = jnp.split(x, 2, axis=-1)
            return jnp.concatenate([-x2, x1], axis=-1)

        def rotary_xpos(q, k):
            n = q.shape[-2]
            half_idx = jnp.arange(0, DIM_HEAD, 2, dtype=jnp.float32)
            inv_freq = 1.0 / 10000.0 ** (half_idx / DIM_HEAD)
            t = jnp.arange(n, dtype=jnp.float32)
            freqs = t[:, None] * inv_freq[None, :]
            freqs = jnp.concatenate([freqs, freqs], axis=-1)
            base = (half_idx + 0.4 * DIM_HEAD) / (1.4 * DIM_HEAD)
            power = (t - n // 2) / float(WINDOW // 2)
            scale = base[None, :] ** power[:, None]
            scale = jnp.concatenate([scale, scale], axis=-1)
            cos, sin = (jnp.cos(freqs), jnp.sin(freqs))
            q = q * cos * scale + rotate_half(q) * sin * scale
            k = k * cos / scale + rotate_half(k) * sin / scale
            return (q, k)

        def local_attention(q, k, v):
            b, h, n, d = q.shape
            w = n // WINDOW
            bq = q.reshape(b, h, w, WINDOW, d) * QK_SCALE
            bk = k.reshape(b, h, w, WINDOW, d)
            bv = v.reshape(b, h, w, WINDOW, d)

            def look_around(t):
                p = jnp.pad(t, ((0, 0), (0, 0), (1, 0), (0, 0), (0, 0)))
                return jnp.concatenate([p[:, :, :w], p[:, :, 1:]], axis=3)
            bk, bv = (look_around(bk), look_around(bv))
            bt = jnp.arange(n).reshape(w, WINDOW)
            btp = jnp.pad(bt, ((1, 0), (0, 0)), constant_values=-1)
            btk = jnp.concatenate([btp[:w], btp[1:]], axis=1)
            sim = jnp.einsum('bhwid,bhwjd->bhwij', bq, bk)
            i = bt[:, :, None]
            j = btk[:, None, :]
            mask = (i < j) | (i > j + WINDOW) | (j == -1)
            sim = jnp.where(mask, -jnp.finfo(sim.dtype).max, sim)
            attn = jax.nn.softmax(sim, axis=-1)
            out = jnp.einsum('bhwij,bhwjd->bhwid', attn, bv)
            return out.reshape(b, h, n, d)

        def _layer(x, wqkv, qs, ksc, wo, lg, lb, w1, b1, w2, b2):
            b, n, _ = x.shape
            h = shift_token(x)
            qkv = h @ wqkv
            q, k, v = jnp.split(qkv, 3, axis=-1)
            to_heads = lambda t: t.reshape(b, n, HEADS, DIM_HEAD).transpose(0, 2, 1, 3)
            q, k, v = (to_heads(q), to_heads(k), to_heads(v))
            q = l2norm(q) * qs
            k = l2norm(k) * ksc
            q, k = rotary_xpos(q, k)
            o = local_attention(q, k, v)
            o = o.transpose(0, 2, 1, 3).reshape(b, n, INNER)
            x = x + o @ wo
            h = shift_token(x)
            mu = h.mean(-1, keepdims=True)
            var = h.var(-1, keepdims=True)
            h = (h - mu) / jnp.sqrt(var + 1e-05) * lg + lb
            h = h @ w1 + b1
            a, g = jnp.split(h, 2, axis=-1)
            h = a * jax.nn.gelu(g, approximate=False)
            x = x + h @ w2 + b2
            return x
        for l in range(DEPTH):
            x = _layer(x, wqkv[l], q_scale[l], k_scale[l], wo[l], ln_g[l], ln_b[l], w1[l], b1[l], w2[l], b2[l])
        return x
    x = L0_attn_x
    xn = _layernorm(x, axis=-1)
    s = _L0_attn_ref(xn, L0_attn_Wqkv, L0_attn_bqkv, L0_attn_Wpre, L0_attn_Wpost, L0_attn_Wout, L0_attn_bout)
    g = _silu(_L0_ffn_ref(xn, L0_ffn_wqkv, L0_ffn_q_scale, L0_ffn_k_scale, L0_ffn_wo, L0_ffn_ln_g, L0_ffn_ln_b, L0_ffn_w1, L0_ffn_b1, L0_ffn_w2, L0_ffn_b2))
    x = x + s * g
    return x

_drawn_inputs = setup_inputs


def setup_inputs(seed=0):
    import zlib

    import numpy as np

    out = dict(_drawn_inputs(seed))
    spreads = {'L0_ffn_q_scale': (1.0, 0.6),
     'L0_ffn_k_scale': (1.0, 0.6),
     'L0_ffn_ln_g': (1.0, 0.6),
     'L0_ffn_ln_b': (0.0, 0.8),
     'L0_ffn_b1': (0.0, 0.8),
     'L0_ffn_b2': (0.0, 0.8)}
    factors = {'L0_attn_bqkv': 5.864,
     'L0_attn_bout': 4.439,
     'L0_ffn_wqkv': 8.0,
     'L0_ffn_wo': 8.0,
     'L0_ffn_w1': 8.0,
     'L0_ffn_w2': 8.0}
    for name, (base, spread) in spreads.items():
        noise = np.random.default_rng([zlib.crc32(name.encode()), seed]).standard_normal(out[name].shape)
        drawn = base * np.exp(spread * noise) if base else spread * noise
        out[name] = jnp.asarray(drawn.astype(out[name].dtype))
    for name, factor in factors.items():
        out[name] = (out[name] * factor).astype(out[name].dtype)
    return out
```

```python
from contextlib import ExitStack

import numpy as np

import concourse.bass as bass
from concourse import mybir

ALU = mybir.AluOpType
ACT = mybir.ActivationFunctionType
AX = mybir.AxisListType
F32 = mybir.dt.float32
BF16 = mybir.dt.bfloat16

P = 128
B, N, D = 16, 512, 256
TW = N // P
KC = D // P

GH, GD = 16, 16
HALF = GD // 2
RI = P // GH
TILES = N // RI
CT = 8
ET = 4
CI = CT * RI
CHUNKS = TILES // CT
LAG = 2
PB = LAG + 1
GR = 4
PAD = 32

LAYERS = 2
H, HD = 8, 64
INNER = H * HD
HID = D * 4 * 2 // 3
HC = -(-HID // P)
QUADS = 2
MASKED = -1e30
LEAST = -87.5


def hidden_rows(c):
    return min(P, HID - c * P)


def step_order():
    head = [("norm",), ("x_turn", 0), ("talk_qk",), ("talk_v",), ("expand", 0)]
    talk = []
    for n in range(TILES):
        talk.append([("scores", n)])
        if n % ET == 0 and n // ET + 1 < TILES // ET:
            talk[-1].append(("expand", n // ET + 1))
        if n % CT == LAG and n >= CT:
            talk[-1].append(("values", n // CT - 1))
        if n >= LAG:
            talk[-1].append(("mix", n - LAG))
        if n % (2 * CT) == 5 and n >= CT:
            talk[-1].append(("project", n // (2 * CT) - 1))
    for n in range(TILES - LAG, TILES):
        talk.append([("mix", n)])
    talk.append([("values", CHUNKS - 1)])
    talk.append([("project", TW - 1)])

    gate = []
    for l in range(LAYERS):
        if l:
            gate.append([("x_turn", l)])
        for t in range(TW):
            gate.append([("qkv", l, t)])
            if t:
                gate.append([("q_turn", l, t - 1)])
                gate.append([("k_turn", l, t - 1)])
        gate.append([("q_turn", l, TW - 1)])
        gate.append([("k_turn", l, TW - 1)])
        units = TW * QUADS
        for u in range(units + 3):
            if u < units:
                gate.append([("local_scores", l, u)])
            if 1 <= u <= units:
                gate.append([("p_turn", l, u - 1)])
            if 2 <= u <= units + 1:
                gate[-1].append(("local_values", l, u - 2))
            if u >= 3 and u % QUADS == 1:
                gate.append([("o_turn", l, u // QUADS - 1)])
            if u >= 4 and u % QUADS == 0:
                gate.append([("out_proj", l, u // QUADS - 2)])
        gate += [[("half_turn", l)], [("shift_turn", l)], [("h_turn", l)]]
        gate += [[("up", l, c)] for c in range(HC)]
        gate += [[("down", l, t)] for t in range(TW)]

    order, done = list(head), 0
    for i, steps in enumerate(talk):
        order += steps
        upto = (i + 1) * len(gate) // len(talk)
        for g in gate[done:upto]:
            order += g
        done = upto
    order.append(("gated",))
    return order


def banks_of(step):
    kind = step[0]
    if kind == "scores":
        return [f"S{step[1] % 2}"]
    if kind in ("mix", "project"):
        return ["M"]
    if kind in ("values", "local_values"):
        return ["V"]
    if kind == "talk_qk":
        return ["S0", "S1", "M", "V"]
    if kind == "talk_v":
        return ["S0", "S1"]
    if kind == "up":
        return ["F0", "F1"] if step[2] % 2 == 0 else ["F2", "F3"]
    if kind == "down":
        return [f"F{step[2]}"]
    return {
        "x_turn": ["F0", "F1"], "qkv": ["F0", "F1", "F2"], "q_turn": ["F3"], "k_turn": ["F3"],
        "local_scores": ["F0", "F1"], "p_turn": ["F2", "F3"], "o_turn": ["F2"], "out_proj": ["F3"],
        "half_turn": ["F0"], "shift_turn": ["F1"], "h_turn": ["F2", "F3"],
    }.get(kind, [])


BANKS = ["S0", "S1", "M", "V", "F0", "F1", "F2", "F3"]


def gate_network_kernel(nc, a, out):
    order = step_order()
    filling, fillings = {}, {k: 0 for k in BANKS}
    for step in order:
        for k in banks_of(step):
            fillings[k] += 1
            filling[step, k] = fillings[k]

    with ExitStack() as ctx:
        def sb(name, shape, dt=F32):
            return ctx.enter_context(nc.sbuf_tensor(name, [P, *shape], dt))

        ident = sb("ident", [P])
        ident_bf = sb("ident_bf", [P], BF16)
        mask_bf = sb("mask_bf", [2, 2 * P], BF16)
        rope_cos = sb("rope_cos", [N])
        rope_sin = sb("rope_sin", [N])
        delta = sb("delta", [RI])
        w_qk = sb("w_qk", [KC, 4, P])
        b_qk = sb("b_qk", [4])
        w_v = sb("w_v", [KC, D])
        b_v = sb("b_v", [D])
        w_pre = sb("w_pre", [GH])
        w_post = sb("w_post", [GH])
        w_out = sb("w_out", [GR, D])
        b_out = sb("b_out", [D])
        mixer = sb("mixer", [GH, RI])
        rot = [sb(f"rot{l}", [4, TW, HD]) for l in range(LAYERS)]
        w_qkv = sb("w_qkv", [KC, 3 * INNER])
        w_o = [sb(f"w_o{l}", [INNER // P, D]) for l in range(LAYERS)]
        w_1 = sb("w_1", [KC, 2 * HID])
        w_2 = [sb(f"w_2{l}", [HC, D]) for l in range(LAYERS)]
        b_1 = [sb(f"b_1{l}", [2 * HC]) for l in range(LAYERS)]
        b_2 = [sb(f"b_2{l}", [D]) for l in range(LAYERS)]
        ln_w = [sb(f"ln_w{l}", [2 * KC]) for l in range(LAYERS)]
        minus_half = sb("minus_half", [2 * H])
        one = sb("one", [1])
        opener = sb("opener", [1])
        eps = sb("eps", [TW])

        x_in = sb("x_in", [TW, D])
        x_keep = sb("x_keep", [TW, D])
        x_tok = sb("x_tok", [TW, D])
        xT = sb("xT", [KC, N + 1])
        stats = sb("stats", [TW, 2, 6])
        mean_var = sb("mean_var", [TW, 2])
        var_eps = sb("var_eps", [TW])
        rstd = sb("rstd", [TW])
        q_rope = sb("q_rope", [2, N])
        k_rope = sb("k_rope", [2, N])
        v_pad = sb("v_pad", [TW, GH, PAD])
        q_mix = sb("q_mix", [2, 2, ET, P])
        neg_max = sb("neg_max", [2])
        row_sum = sb("row_sum", [PB])
        row_inv = sb("row_inv", [2])
        probs = sb("probs", [PB, N])
        mixer_n = sb("mixer_n", [2, P])
        mixed = sb("mixed", [TW, GH, CI])
        before = mixed[:].rearrange("p j g i -> p (j g i)").rearrange("p (a n) -> p a n", n=N)
        raw_qk, t_q, t_k = before[:, 0:4], before[:, 4:6], before[:, 6:8]
        oT = sb("oT", [GR, P])
        s_tok = sb("s_tok", [TW, D])

        shared = sb("shared", [8, INNER])
        sq = shared[:, 0:2]
        rot_a, rot_b, qk_tok = shared[:, 2:4], shared[:, 4:6], shared[:, 6:8]
        x_mid_b, h_tok = (shared[:, j:j + 2].rearrange("p a (b f) -> p (a b) f", f=D) for j in (0, 2))
        hT, gelu = shared[:, 4:6], shared[:, 6:8]
        norms = sb("norms", [2 * H])
        norms_c = sb("norms_c", [2 * H])
        inv_norms = sb("inv_norms", [2 * H])
        att = sb("att", [3 * 4, N])
        qT = att[:, 0:4, :]
        kT = att[:, 4:8, :]
        v_loc = att[:, 8:12, :]
        hidden = att[:, 0:HC, :]
        l_max = sb("l_max", [2, 4])
        l_sum = sb("l_sum", [2, 4])
        l_inv = sb("l_inv", [2, 4])
        l_probs = sb("l_probs", [2, 4, 2 * P])
        pT = sb("pT", [2, 4, P])
        o_tok = sb("o_tok", [H, HD])
        o_locT = sb("o_locT", [4, P])
        x_mid = sb("x_mid", [TW, D])
        midT = sb("midT", [N + 1])
        o_fin = sb("o_fin", [TW, D])
        setup = l_probs[:].rearrange("p a h k -> p (a h k)")
        xpos = setup[:, 0:4 * TW * HD].rearrange("p (j t d) -> p j t d", j=4, t=TW)
        mask = setup[:, (4 * TW + 4 * LAYERS) * HD:]
        scales = [setup[:, (4 * TW + 4 * l) * HD:(4 * TW + 4 * l + 4) * HD].rearrange("p (j d) -> p j d", j=4)
                  for l in range(LAYERS)]

        bank = {k: ctx.enter_context(nc.psum_tensor(f"bank_{k}", [P, 512], F32)) for k in BANKS}

        per = {}

        def sem(name, count):
            h = ctx.enter_context(nc.semaphore(name))
            per[id(h)] = count
            return h

        filled = {k: sem(f"filled_{k}", fillings[k]) for k in BANKS}
        emptied = {k: sem(f"emptied_{k}", fillings[k]) for k in BANKS}
        QL = TW * QUADS * LAYERS
        WL = TW * LAYERS
        loads = sem("loads", 0)
        tables = sem("tables", 0)
        pads = sem("pads", 0)
        x_loaded = sem("x_loaded", 16)
        qkv_loaded = sem("qkv_loaded", 16 * LAYERS)
        w_1_loaded = sem("w_1_loaded", 16 * LAYERS)
        x_kept = sem("x_kept", 1)
        stats_done = sem("stats_done", TW + LAYERS * 2 * TW)
        aggr_done = sem("aggr_done", 1 + LAYERS)
        eps_done = sem("eps_done", 1 + LAYERS)
        rstd_done = sem("rstd_done", 1 + LAYERS)
        x_ready = sem("x_ready", TW)
        raw_ready = sem("raw_ready", 4)
        k_parts = sem("k_parts", 2)
        k_roped = sem("k_roped", 1)
        q_parts = sem("q_parts", 2)
        q_roped = sem("q_roped", 1)
        q_mixed = sem("q_mixed", 2 * TILES // ET)
        max_done = sem("max_done", TILES)
        inv_done = sem("inv_done", TILES)
        mixer_done = sem("mixer_done", TILES)
        s_done = sem("s_done", TW)
        norm_done = sem("norm_done", 2 * WL)
        rot_done = sem("rot_done", 2 * WL)
        clip_done = sem("clip_done", WL)
        inv_norm_done = sem("inv_norm_done", WL)
        rot_added = sem("rot_added", 2 * WL)
        qk_ready = sem("qk_ready", 2 * WL)
        l_max_done = sem("l_max_done", QL)
        l_inv_done = sem("l_inv_done", QL)
        mid_b_ready = sem("mid_b_ready", LAYERS)
        h_ready = sem("h_ready", LAYERS * TW)
        gelu_done = sem("gelu_done", LAYERS * HC)
        bounded = sem("bounded", 1)
        exp_done = sem("exp_done", 1)
        one_plus = sem("one_plus", 1)
        sig_done = sem("sig_done", 1)
        silu_done = sem("silu_done", 1)
        gated_done = sem("gated_done", 1)
        o_ready = sem("o_ready", 1)
        stored = sem("stored", 16)

        once = [
            (ident[:], a["ident"]), (mask, a["mask"]),
            (rope_cos[:], a["rope_cos"]), (rope_sin[:], a["rope_sin"]), (delta[:], a["delta"]),
            (w_qk[:], a["w_qk"]), (b_qk[:], a["b_qk"]), (w_v[:], a["w_v"]), (b_v[:], a["b_v"]),
            (w_pre[:], a["w_pre"]), (w_post[:], a["w_post"]), (w_out[:], a["w_out"]),
            (b_out[:], a["b_out"]), (xpos, a["xpos"]),
        ]
        for l in range(LAYERS):
            once += [
                (scales[l], a["scales"][l]), (w_o[l][:], a["w_o"][l]),
                (w_2[l][:], a["w_2"][l]), (b_1[l][:], a["b_1"][l]),
                (b_2[l][:], a["b_2"][l]), (ln_w[l][:], a["ln_w"][l]),
            ]
        LOADED = 16 * len(once)
        TABLES = 4 + 4 * LAYERS

        class Counts:
            def __init__(self):
                self.b, self.first = 0, True

            def past(self, k):
                return k > 0 or not self.first

            def at(self, sem, k):
                return self.b * per[id(sem)] + k

            def fill(self, step, k, ago=0):
                return self.b * fillings[k] + filling[step, k] - ago * fillings[k]

            def run(self, eng, body):
                body()
                self.first = False
                with eng.Fori(1, B) as b:
                    self.b = b
                    body()

        def window_before(l, t):
            return (l, t - 1) if t else ((l - 1) % LAYERS, TW - 1)

        def unit_before(l, u, by):
            n = (TW * QUADS * l + u - by) % (LAYERS * TW * QUADS)
            return n // (TW * QUADS), n % (TW * QUADS)

        def stream_ready(eng, now, l):
            if l == 0:
                eng.wait_ge(x_ready, now.at(x_ready, TW))
            else:
                for t in range(TW):
                    eng.wait_ge(emptied[f"F{t}"], now.fill(("down", l - 1, t), f"F{t}"))

        def store_mixed(eng, copy, now, n):
            c, m = n // CT, n % CT
            if c:
                eng.wait_ge(filled["V"], now.fill(("values", c - 1), "V"))
            else:
                eng.wait_ge(q_roped, now.at(q_roped, 1))
                eng.wait_ge(k_roped, now.at(k_roped, 1))
            copy(mixed[:, :, :, m * RI:(m + 1) * RI],
                 bank["M"][:].rearrange("p (j g i) -> p j g i", j=TW, g=GH)).then_inc(emptied["M"], 1)

        block = ctx.enter_context(nc.Block())

        @block.sync
        def _(sp):
            now = Counts()
            for dst, src in once:
                sp.dma_start(dst, src).then_inc(loads, 16)
            sp.dma_start(w_qkv[:], a["w_qkv"][0]).then_inc(qkv_loaded, 16)
            sp.dma_start(w_1[:], a["w_1"][0]).then_inc(w_1_loaded, 16)

            def body():
                for l in range(LAYERS):
                    sp.wait_ge(filled["F2"], now.fill(("qkv", l, TW - 1), "F2"))
                    sp.dma_start(w_qkv[:], a["w_qkv"][(l + 1) % LAYERS]).then_inc(qkv_loaded, 16)
                    sp.wait_ge(filled[banks_of(("up", l, HC - 1))[1]], now.fill(("up", l, HC - 1), banks_of(("up", l, HC - 1))[1]))
                    sp.dma_start(w_1[:], a["w_1"][(l + 1) % LAYERS]).then_inc(w_1_loaded, 16)

            now.run(sp, body)
            sp.wait_ge(x_loaded, 16 * (B + 1))
            sp.wait_ge(qkv_loaded, 16 * (LAYERS * B + 1))
            sp.wait_ge(w_1_loaded, 16 * (LAYERS * B + 1))
            sp.wait_ge(stored, 16 * B)

        @block.tensor
        def _(pe):
            now = Counts()
            mm = nc.tensor.matmul
            turn = nc.tensor.transpose
            pe.wait_ge(loads, LOADED)
            pe.wait_ge(tables, TABLES)
            pe.wait_ge(pads, 6)

            def x_turn(step, l):
                stream_ready(pe, now, l)
                for c in range(KC):
                    if now.past(filling[step, f"F{c}"] - 1):
                        pe.wait_ge(emptied[f"F{c}"], now.fill(step, f"F{c}") - 1)
                    for t in range(TW):
                        last = turn(bank[f"F{c}"][:, t * P:(t + 1) * P], x_tok[:, t, c * P:(c + 1) * P], ident[:])
                    last.then_inc(filled[f"F{c}"], 1)

            def talk_qk(step):
                for c in range(KC):
                    pe.wait_ge(emptied[f"F{c}"], now.fill(("x_turn", 0), f"F{c}"))
                for j, k in enumerate(["S0", "S1", "M", "V"]):
                    if now.past(filling[step, k] - 1):
                        pe.wait_ge(emptied[k], now.fill(step, k) - 1)
                    for c in range(KC):
                        last = mm(bank[k][:], w_qk[:, c, j, :], xT[:, c, 1:N + 1], start=(c == 0), stop=(c == KC - 1))
                    last.then_inc(filled[k], 1)

            def talk_v(step):
                for t in range(TW):
                    k = f"S{t // 2}"
                    if t % 2 == 0:
                        if now.past(filling[step, k] - 1):
                            pe.wait_ge(emptied[k], now.fill(step, k) - 1)
                    for c in range(KC):
                        last = mm(bank[k][:, (t % 2) * D:(t % 2 + 1) * D], xT[:, c, 1 + t * P:1 + (t + 1) * P],
                                  w_v[:, c, :], start=(c == 0), stop=(c == KC - 1))
                    if t % 2:
                        last.then_inc(filled[k], 1)

            def scores(step, n):
                k = f"S{n % 2}"
                if n == 0:
                    pe.wait_ge(k_roped, now.at(k_roped, 1))
                if n % ET == 0:
                    pe.wait_ge(q_mixed, now.at(q_mixed, 2 * (n // ET + 1)))
                if now.past(filling[step, k] - 1):
                    pe.wait_ge(emptied[k], now.fill(step, k) - 1)
                for s in range(2):
                    last = mm(bank[k][:], q_mix[:, (n // ET) % 2, s, n % ET, :], k_rope[:, s, :],
                              start=(s == 0), stop=(s == 1))
                last.then_inc(filled[k], 1)

            def mix(step, n):
                pe.wait_ge(mixer_done, now.at(mixer_done, n + 1))
                if now.past(filling[step, "M"] - 1):
                    pe.wait_ge(emptied["M"], now.fill(step, "M") - 1)
                for j in range(TW):
                    last = mm(bank["M"][:, j * P:(j + 1) * P], probs[:, n % PB, j * P:(j + 1) * P],
                              mixer_n[:, n % 2, :], start=True, stop=True)
                last.then_inc(filled["M"], 1)

            def values(step, c):
                pe.wait_ge(emptied["M"], now.fill(("mix", (c + 1) * CT - 1), "M"))
                for j in range(2):
                    pe.wait_ge(emptied[f"S{j}"], now.fill(("talk_v",), f"S{j}"))
                if now.past(filling[step, "V"] - 1):
                    pe.wait_ge(emptied["V"], now.fill(step, "V") - 1)
                for r in range(GH // GR):
                    for j in range(TW):
                        for q in range(GR):
                            g = GR * r + q
                            last = mm(bank["V"][PAD * q:PAD * (q + 1), r * CI:(r + 1) * CI], v_pad[:, j, g, :],
                                      mixed[:, j, g, :], start=(j == 0), stop=(j == TW - 1))
                last.then_inc(filled["V"], 1)

            def project(step, t):
                pe.wait_ge(emptied["V"], now.fill(("values", 2 * t + 1), "V"))
                if now.past(filling[step, "M"] - 1):
                    pe.wait_ge(emptied["M"], now.fill(step, "M") - 1)
                for r in range(GH // GR):
                    last = mm(bank["M"][:, 0:D], oT[:, r, :], w_out[:, r, :], start=(r == 0), stop=(r == GH // GR - 1))
                last.then_inc(filled["M"], 1)

            def qkv(step, l, t):
                for c in range(KC):
                    pe.wait_ge(emptied[f"F{c}"], now.fill(("x_turn", l), f"F{c}"))
                pe.wait_ge(qkv_loaded, now.at(qkv_loaded, 16 * (l + 1)))
                for j in range(3):
                    k = f"F{j}"
                    if now.past(filling[step, k] - 1):
                        pe.wait_ge(emptied[k], now.fill(step, k) - 1)
                    for c in range(KC):
                        at = 1 - c + t * P
                        last = mm(bank[k][:], xT[:, c, at:at + P], w_qkv[:, c, j * INNER:(j + 1) * INNER],
                                  start=(c == 0), stop=(c == KC - 1))
                    last.then_inc(filled[k], 1)

            def qk_turn(step, l, t, j):
                pe.wait_ge(qk_ready, now.at(qk_ready, 2 * (TW * l + t) + j + 1))
                if now.past(filling[step, "F3"] - 1):
                    pe.wait_ge(emptied["F3"], now.fill(step, "F3") - 1)
                for c in range(4):
                    last = turn(bank["F3"][:, c * P:(c + 1) * P], qk_tok[:, j, c * P:(c + 1) * P], ident[:])
                last.then_inc(filled["F3"], 1)

            def local_scores(step, l, u):
                t, quad = u // QUADS, u % QUADS
                pe.wait_ge(emptied["F3"], now.fill(("k_turn", l, TW - 1), "F3"))
                for parity in range(2):
                    k = f"F{parity}"
                    if now.past(filling[step, k] - 1):
                        pe.wait_ge(emptied[k], now.fill(step, k) - 1)
                    mm(bank[k][:], ident_bf[:], mask_bf[:].rearrange("p a j -> p (a j)"), start=True, stop=False,
                       skip_group_check=True)
                    for pair in range(2):
                        hp = 2 * quad + pair
                        lo = P if t == 0 else 0
                        rows = slice(HD * parity, HD * (parity + 1))
                        last = mm(bank[k][:, pair * 2 * P + lo:(pair + 1) * 2 * P],
                                  qT[rows, hp, t * P:(t + 1) * P],
                                  kT[rows, hp, (t - 1) * P + lo:(t + 1) * P],
                                  start=False, stop=(pair == 1), skip_group_check=True)
                    last.then_inc(filled[k], 1)

            def p_turn(step, l, u):
                for parity in range(2):
                    pe.wait_ge(emptied[f"F{parity}"], now.fill(("local_scores", l, u), f"F{parity}"))
                lo = 1 if u // QUADS == 0 else 0
                for pair in range(2):
                    k = f"F{2 + pair}"
                    if now.past(filling[step, k] - 1):
                        pe.wait_ge(emptied[k], now.fill(step, k) - 1)
                    for parity in range(2):
                        for j in range(lo, 2):
                            last = turn(bank[k][:, (2 * parity + j) * P:(2 * parity + j + 1) * P],
                                        l_probs[:, u % 2, 2 * parity + pair, j * P:(j + 1) * P], ident[:])
                    last.then_inc(filled[k], 1)

            def local_values(step, l, u):
                t, quad = u // QUADS, u % QUADS
                for pair in range(2):
                    pe.wait_ge(emptied[f"F{2 + pair}"], now.fill(("p_turn", l, u), f"F{2 + pair}"))
                if now.past(filling[step, "V"] - 1):
                    pe.wait_ge(emptied["V"], now.fill(step, "V") - 1)
                lo = 1 if t == 0 else 0
                for pair in range(2):
                    for parity in range(2):
                        h = 4 * quad + 2 * pair + parity
                        for j in range(lo, 2):
                            last = mm(bank["V"][:, (2 * pair + parity) * HD:(2 * pair + parity + 1) * HD],
                                      pT[:, pair, 2 * parity + j, :], v_loc[:, t - 1 + j, h * HD:(h + 1) * HD],
                                      start=(j == lo), stop=(j == 1))
                last.then_inc(filled["V"], 1)

            def o_turn(step, l, t):
                pe.wait_ge(emptied["V"], now.fill(("local_values", l, QUADS * t + QUADS - 1), "V"))
                if now.past(filling[step, "F2"] - 1):
                    pe.wait_ge(emptied["F2"], now.fill(step, "F2") - 1)
                flat = o_tok[:].rearrange("p h d -> p (h d)")
                for c in range(4):
                    last = turn(bank["F2"][:, c * P:(c + 1) * P], flat[:, c * P:(c + 1) * P], ident[:])
                last.then_inc(filled["F2"], 1)

            def out_proj(step, l, t):
                pe.wait_ge(emptied["F2"], now.fill(("o_turn", l, t), "F2"))
                if now.past(filling[step, "F3"] - 1):
                    pe.wait_ge(emptied["F3"], now.fill(step, "F3") - 1)
                for c in range(4):
                    last = mm(bank["F3"][:, 0:D], o_locT[:, c, :], w_o[l][:, c, :], start=(c == 0), stop=(c == 3))
                last.then_inc(filled["F3"], 1)

            def half_turn(step, l):
                pe.wait_ge(emptied["F3"], now.fill(("out_proj", l, TW - 1), "F3"))
                if now.past(filling[step, "F0"] - 1):
                    pe.wait_ge(emptied["F0"], now.fill(step, "F0") - 1)
                for t in range(TW):
                    last = turn(bank["F0"][:, t * P:(t + 1) * P], x_mid[:, t, P:D], ident[:])
                last.then_inc(filled["F0"], 1)

            def shift_turn(step, l):
                pe.wait_ge(emptied["F0"], now.fill(("half_turn", l), "F0"))
                if now.past(filling[step, "F1"] - 1):
                    pe.wait_ge(emptied["F1"], now.fill(step, "F1") - 1)
                for t in range(TW):
                    last = turn(bank["F1"][:, t * P:(t + 1) * P], midT[:, t * P:(t + 1) * P], ident[:])
                last.then_inc(filled["F1"], 1)

            def h_turn(step, l):
                pe.wait_ge(h_ready, now.at(h_ready, TW * (l + 1)))
                pe.wait_ge(emptied["F1"], now.fill(("shift_turn", l), "F1"))
                for c in range(KC):
                    k = f"F{2 + c}"
                    if now.past(filling[step, k] - 1):
                        pe.wait_ge(emptied[k], now.fill(step, k) - 1)
                    for t in range(TW):
                        last = turn(bank[k][:, t * P:(t + 1) * P], h_tok[:, t, c * P:(c + 1) * P], ident[:])
                    last.then_inc(filled[k], 1)

            def up(step, l, i):
                for c in range(KC):
                    pe.wait_ge(emptied[f"F{2 + c}"], now.fill(("h_turn", l), f"F{2 + c}"))
                pe.wait_ge(w_1_loaded, now.at(w_1_loaded, 16 * (l + 1)))
                m = hidden_rows(i)
                for j, k in enumerate(banks_of(step)):
                    if now.past(filling[step, k] - 1):
                        pe.wait_ge(emptied[k], now.fill(step, k) - 1)
                    for c in range(KC):
                        at = j * HID + i * P
                        last = mm(bank[k][0:m, :], w_1[:, c, at:at + m], hT[:, c, :], start=(c == 0), stop=(c == KC - 1))
                    last.then_inc(filled[k], 1)

            def down(step, l, t):
                pe.wait_ge(emptied[banks_of(("up", l, HC - 1))[0]], now.fill(("up", l, HC - 1), banks_of(("up", l, HC - 1))[0]))
                k = f"F{t}"
                if now.past(filling[step, k] - 1):
                    pe.wait_ge(emptied[k], now.fill(step, k) - 1)
                for i in range(HC):
                    m = hidden_rows(i)
                    last = mm(bank[k][:, 0:D], hidden[0:m, i, t * P:(t + 1) * P], w_2[l][0:m, i, :],
                              start=(i == 0), stop=(i == HC - 1))
                last.then_inc(filled[k], 1)

            steps = {
                "x_turn": x_turn, "talk_qk": talk_qk, "talk_v": talk_v, "scores": scores, "mix": mix,
                "values": values, "project": project, "qkv": qkv,
                "q_turn": lambda step, l, t: qk_turn(step, l, t, 0),
                "k_turn": lambda step, l, t: qk_turn(step, l, t, 1),
                "local_scores": local_scores, "p_turn": p_turn, "local_values": local_values,
                "o_turn": o_turn, "out_proj": out_proj, "half_turn": half_turn, "shift_turn": shift_turn,
                "h_turn": h_turn, "up": up, "down": down,
            }

            def body():
                for step in order:
                    if step[0] in steps:
                        steps[step[0]](step, *step[1:])

            now.run(pe, body)

        @block.scalar
        def _(act):
            now = Counts()
            fn = nc.scalar.activation
            act.wait_ge(loads, LOADED)

            def x_turn(step, l):
                if now.past(not (not l)):
                    act.wait_ge(filled["F2"], now.fill(("qkv", (l - 1) % LAYERS, TW - 1), "F2", ago=not l))
                if l:
                    act.wait_ge(filled["S1"], now.fill(("talk_v",), "S1"))
                for c in range(KC):
                    k = f"F{c}"
                    act.wait_ge(filled[k], now.fill(step, k))
                    fn(xT[:, c, 1:N + 1], bank[k][:], ACT.Copy).then_inc(emptied[k], 1)

            def talk_qk(step):
                if not now.first:
                    act.wait_ge(filled["V"], now.fill(("values", CHUNKS - 1), "V", ago=1))
                for j, k in enumerate(["S0", "S1", "M", "V"]):
                    act.wait_ge(filled[k], now.fill(step, k))
                    fn(raw_qk[:, j, :], bank[k][:], ACT.Identity, bias=b_qk[:, j:j + 1]).then_inc(emptied[k], 1)

            def scores(step, n):
                k = f"S{n % 2}"
                act.wait_ge(max_done, now.at(max_done, n + 1))
                if n >= PB:
                    act.wait_ge(filled["M"], now.fill(("mix", n - PB), "M"))
                elif not now.first:
                    act.wait_ge(filled["M"], now.fill(("mix", TILES - 1), "M", ago=1))
                fn(probs[:, n % PB, :], bank[k][:], ACT.Exp, bias=neg_max[:, n % 2:n % 2 + 1],
                   accum_out=row_sum[:, n % PB:n % PB + 1]).then_inc(emptied[k], 1)

            def mix(step, n):
                if n % 2:
                    return
                act.wait_ge(filled["M"], now.fill(step, "M"))
                store_mixed(act, nc.scalar.copy, now, n)

            def values(step, c):
                act.wait_ge(filled["V"], now.fill(step, "V"))
                if c % 2 == 0:
                    if now.past(not (c < 2)):
                        act.wait_ge(filled["M"], now.fill(("project", (c // 2 - 1) % TW), "M", ago=c < 2))
                at = (c % 2) * CI
                fn(oT[:, :, at:at + CI], bank["V"][:, 0:GR * CI].rearrange("p (r i) -> p r i", r=GR), ACT.Copy)\
                    .then_inc(emptied["V"], 1)

            def qkv(step, l, t):
                w = TW * l + t
                for j in range(2):
                    if now.past(2 * (w - 1) + j + 1):
                        act.wait_ge(norm_done, now.at(norm_done, 2 * (w - 1) + j + 1))
                    act.wait_ge(rot_done, now.at(rot_done, 2 * w + j + 1))
                    fn(sq[:, j, :], bank[f"F{j}"][:], ACT.Square).then_inc(emptied[f"F{j}"], 1)
                if t == 0:
                    if now.past(not (not l)):
                        act.wait_ge(filled["V"], now.fill(("local_values", (l - 1) % LAYERS, TW * QUADS - 1), "V", ago=not l))
                act.wait_ge(filled["F2"], now.fill(step, "F2"))
                fn(v_loc[:, t, :], bank["F2"][:], ACT.Copy).then_inc(emptied["F2"], 1)

            def q_turn(step, l, t):
                if t == 0:
                    if now.past(not (not l)):
                        act.wait_ge(filled["F3"], now.fill(("down", (l - 1) % LAYERS, TW - 1), "F3", ago=not l))
                act.wait_ge(filled["F3"], now.fill(step, "F3"))
                fn(qT[:, :, t * P:(t + 1) * P], bank["F3"][:].rearrange("p (c i) -> p c i", c=4), ACT.Copy)\
                    .then_inc(emptied["F3"], 1)

            def local_scores(step, l, u):
                n = TW * QUADS * l + u
                lo = P if u // QUADS == 0 else 0
                act.wait_ge(l_max_done, now.at(l_max_done, n + 1))
                if now.past(not (n < 2)):
                    act.wait_ge(filled["F3"], now.fill(("p_turn", *unit_before(l, u, 2)), "F3", ago=n < 2))
                if now.past(n - 1):
                    act.wait_ge(l_inv_done, now.at(l_inv_done, n - 1))
                for parity in range(2):
                    for pair in range(2):
                        j = 2 * parity + pair
                        ins = fn(l_probs[:, u % 2, j, lo:], bank[f"F{parity}"][:, pair * 2 * P + lo:(pair + 1) * 2 * P],
                                 ACT.Exp, bias=l_max[:, u % 2, j:j + 1], accum_out=l_sum[:, u % 2, j:j + 1])
                    ins.then_inc(emptied[f"F{parity}"], 1)

            def p_turn(step, l, u):
                act.wait_ge(filled["F3"], now.fill(step, "F3"))
                if now.past(not (not l and not u)):
                    act.wait_ge(filled["V"], now.fill(("local_values", *unit_before(l, u, 1)), "V", ago=not l and not u))
                lo = 1 if u // QUADS == 0 else 0
                fn(pT[:, 1, :, :].rearrange("p (a j) i -> p a j i", a=2)[:, :, lo:, :],
                   bank["F3"][:].rearrange("p (a j i) -> p a j i", a=2, j=2)[:, :, lo:, :], ACT.Copy)\
                    .then_inc(emptied["F3"], 1)

            def o_turn(step, l, t):
                act.wait_ge(filled["F2"], now.fill(step, "F2"))
                if now.past(not (not l and not t)):
                    act.wait_ge(filled["F3"], now.fill(("out_proj", *window_before(l, t)), "F3", ago=not l and not t))
                fn(o_locT[:], bank["F2"][:].rearrange("p (c i) -> p c i", c=4), ACT.Copy).then_inc(emptied["F2"], 1)

            def half_turn(step, l):
                act.wait_ge(filled["F0"], now.fill(step, "F0"))
                if now.past(not (not l)):
                    act.wait_ge(filled["F1"], now.fill(("shift_turn", (l - 1) % LAYERS), "F1", ago=not l))
                fn(midT[:, 1:N + 1], bank["F0"][:], ACT.Copy).then_inc(emptied["F0"], 1)

            def h_turn(step, l):
                act.wait_ge(rot_added, now.at(rot_added, 2 * TW * (l + 1)))
                for c in range(KC):
                    k = f"F{2 + c}"
                    act.wait_ge(filled[k], now.fill(step, k))
                    fn(hT[:, c, :], bank[k][:], ACT.Identity, bias=ln_w[l][:, KC + c:KC + c + 1],
                       scale=ln_w[l][:, c:c + 1]).then_inc(emptied[k], 1)

            def up(step, l, i):
                k = banks_of(step)[1]
                m = hidden_rows(i)
                act.wait_ge(filled[k], now.fill(step, k))
                if i >= 2:
                    act.wait_ge(emptied[banks_of(("up", l, i - 2))[0]], now.fill(("up", l, i - 2), banks_of(("up", l, i - 2))[0]))
                else:
                    act.wait_ge(filled["F3"], now.fill(("k_turn", l, TW - 1), "F3"))
                fn(gelu[0:m, i % 2, :], bank[k][0:m, :], ACT.Gelu, bias=b_1[l][0:m, HC + i:HC + i + 1])\
                    .then_inc(emptied[k], 1)

            def gated(step):
                act.wait_ge(bounded, now.at(bounded, 1))
                fn(o_fin[:], o_fin[:], ACT.Exp, scale=-1.0).then_inc(exp_done, 1)

            steps = {
                "x_turn": x_turn, "talk_qk": talk_qk, "scores": scores, "mix": mix, "values": values, "qkv": qkv,
                "q_turn": q_turn, "local_scores": local_scores, "p_turn": p_turn, "o_turn": o_turn,
                "half_turn": half_turn, "h_turn": h_turn, "up": up, "gated": gated,
            }

            def body():
                for step in order:
                    if step[0] in steps:
                        steps[step[0]](step, *step[1:])

            now.run(act, body)

        @block.vector
        def _(dve):
            now = Counts()
            v = nc.vector
            v.memset(xT[:, :, 0:1], 0.0).then_inc(pads, 1)
            v.memset(midT[:, 0:1], 0.0).then_inc(pads, 1)
            v.memset(v_pad[:], 0.0).then_inc(pads, 1)
            v.memset(minus_half[:], -0.5).then_inc(pads, 1)
            v.memset(one[:], 1.0).then_inc(pads, 1)
            v.memset(eps[:], 1e-5).then_inc(pads, 1)
            dve.wait_ge(pads, 6)
            dve.wait_ge(loads, LOADED)
            v.tensor_copy(mask_bf[:].rearrange("p a j -> p (a j)"), mask).then_inc(tables, 1)
            v.tensor_copy(ident_bf[:], ident[:]).then_inc(tables, 1)
            v.tensor_scalar(w_pre[:], w_pre[:], float(GD) ** -0.5, None, ALU.mult).then_inc(tables, 1)
            v.tensor_tensor(mixer[:], w_post[:, :, None].to_broadcast([P, GH, RI]),
                            delta[:, None, :].to_broadcast([P, GH, RI]), ALU.mult).then_inc(tables, 1)
            for l in range(LAYERS):
                for j in range(4):
                    v.tensor_tensor(rot[l][:, j], xpos[:, j], scales[l][:, j, None, :].to_broadcast([P, TW, HD]),
                                    ALU.mult).then_inc(tables, 1)
            dve.wait_ge(tables, TABLES)

            def norm(step):
                dve.wait_ge(x_loaded, now.at(x_loaded, 16))
                if now.past(0):
                    dve.wait_ge(aggr_done, now.at(aggr_done, 0))
                for t in range(TW):
                    v.bn_stats(stats[:, t, 0, :], x_in[:, t, :]).then_inc(stats_done, 1)
                dve.wait_ge(stats_done, now.at(stats_done, TW))
                v.memset(opener[:], 0.0)
                for t in range(TW):
                    ins = v.bn_aggr(mean_var[:, t, :], stats[:, t, 0, :])
                ins.then_inc(aggr_done, 1)
                dve.wait_ge(rstd_done, now.at(rstd_done, 1))
                if now.past(0):
                    dve.wait_ge(silu_done, now.at(silu_done, 0))
                for t in range(TW):
                    v.tensor_scalar(x_tok[:, t, :], x_in[:, t, :], mean_var[:, t, 0:1], rstd[:, t:t + 1],
                                    ALU.subtract, ALU.mult).then_inc(x_ready, 1)

            def talk_qk(step):
                dve.wait_ge(emptied["V"], now.at(emptied["V"], filling[step, "V"]))
                if not now.first:
                    dve.wait_ge(filled["S1"], now.fill(("scores", TILES - 1), "S1", ago=1))
                v.tensor_tensor(k_rope[:], raw_qk[:, 2:4, :], rope_cos[:, None, :].to_broadcast([P, 2, N]),
                                ALU.mult).then_inc(k_parts, 1)
                v.tensor_tensor(t_k, raw_qk[:, 2:4, :][:, ::-1, :], rope_sin[:, None, :].to_broadcast([P, 2, N]),
                                ALU.mult).then_inc(k_parts, 1)
                dve.wait_ge(k_parts, now.at(k_parts, 2))
                v.tensor_tensor(k_rope[:, 0], k_rope[:, 0], t_k[:, 0], ALU.subtract)
                v.tensor_tensor(k_rope[:, 1], k_rope[:, 1], t_k[:, 1], ALU.add).then_inc(k_roped, 1)

            def talk_v(step):
                if not now.first:
                    dve.wait_ge(filled["V"], now.fill(("values", CHUNKS - 1), "V", ago=1))
                for t in range(TW):
                    k = f"S{t // 2}"
                    if t % 2 == 0:
                        dve.wait_ge(filled[k], now.fill(step, k))
                    ins = v.tensor_tensor(v_pad[:, t, :, 0:GD],
                                          bank[k][:, (t % 2) * D:(t % 2 + 1) * D].rearrange("p (g d) -> p g d", d=GD),
                                          b_v[:].rearrange("p (g d) -> p g d", d=GD), ALU.add)
                    if t % 2:
                        ins.then_inc(emptied[k], 1)

            def mixers(n):
                k = f"S{n % 2}"
                dve.wait_ge(emptied[k], now.fill(("scores", n), k))
                if now.past(n - 1):
                    dve.wait_ge(mixer_done, now.at(mixer_done, n - 1))
                v.reciprocal(row_inv[:, n % 2:n % 2 + 1], row_sum[:, n % PB:n % PB + 1]).then_inc(inv_done, 1)
                if now.past(not (n < 2)):
                    dve.wait_ge(filled["M"], now.fill(("mix", (n - 2) % TILES), "M", ago=n < 2))
                dve.wait_ge(inv_done, now.at(inv_done, n + 1))
                v.tensor_scalar(mixer_n[:, n % 2, :], mixer[:].rearrange("p g i -> p (g i)"),
                                row_inv[:, n % 2:n % 2 + 1], None, ALU.mult).then_inc(mixer_done, 1)

            def scores(step, n):
                k = f"S{n % 2}"
                dve.wait_ge(filled[k], now.fill(step, k))
                if now.past(not (n < 2)):
                    dve.wait_ge(emptied[k], now.fill(("scores", (n - 2) % TILES), k, ago=n < 2))
                v.tensor_reduce(neg_max[:, n % 2:n % 2 + 1], bank[k][:], AX.X, ALU.max, negate=True)\
                    .then_inc(max_done, 1)
                if n:
                    mixers(n - 1)

            def mix(step, n):
                if n == TILES - LAG:
                    mixers(TILES - 1)
                if n % 2:
                    dve.wait_ge(filled["M"], now.fill(step, "M"))
                    store_mixed(dve, v.tensor_copy, now, n)

            def project(step, t):
                dve.wait_ge(filled["M"], now.fill(step, "M"))
                if t == 0:
                    if now.past(0):
                        dve.wait_ge(gated_done, now.at(gated_done, 0))
                v.tensor_tensor(s_tok[:, t, :], bank["M"][:, 0:D], b_out[:], ALU.add).then_inc(emptied["M"], 1)

            def qkv(step, l, t):
                w = TW * l + t
                if now.past(2 * w):
                    dve.wait_ge(rot_added, now.at(rot_added, 2 * w))
                for j in range(2):
                    dve.wait_ge(filled[f"F{j}"], now.fill(step, f"F{j}"))
                    src = bank[f"F{j}"][:].rearrange("p (h s d) -> p h s d", h=H, s=2)
                    for k, (dst, x) in enumerate([(rot_a, src), (rot_b, src[:, :, ::-1, :])]):
                        tab = rot[l][:, 2 * j + k, t, :].rearrange("p (s d) -> p s d", s=2)
                        ins = v.tensor_tensor(dst[:, j, :].rearrange("p (h s d) -> p h s d", h=H, s=2), x,
                                              tab[:, None, :, :].to_broadcast([P, H, 2, HD // 2]), ALU.mult)
                    ins.then_inc(rot_done, 1)
                if now.past(w):
                    dve.wait_ge(clip_done, now.at(clip_done, w))
                for j in range(2):
                    dve.wait_ge(emptied[f"F{j}"], now.fill(step, f"F{j}"))
                    v.tensor_reduce(norms[:, j * H:(j + 1) * H], sq[:, j, :].rearrange("p (h d) -> p h d", h=H),
                                    AX.X, ALU.add).then_inc(norm_done, 1)
                dve.wait_ge(norm_done, now.at(norm_done, 2 * w + 2))
                if now.past(w):
                    dve.wait_ge(inv_norm_done, now.at(inv_norm_done, w))
                v.tensor_scalar(norms_c[:], norms[:], 1e-24, None, ALU.max).then_inc(clip_done, 1)

            def k_turn(step, l, t):
                if t == 0:
                    if now.past(not (not l)):
                        dve.wait_ge(filled["F3"], now.fill(("down", (l - 1) % LAYERS, TW - 1), "F3", ago=not l))
                dve.wait_ge(filled["F3"], now.fill(step, "F3"))
                v.tensor_copy(kT[:, :, t * P:(t + 1) * P], bank["F3"][:].rearrange("p (c i) -> p c i", c=4))\
                    .then_inc(emptied["F3"], 1)

            def local_scores(step, l, u):
                n = TW * QUADS * l + u
                lo = P if u // QUADS == 0 else 0
                if now.past(not (n < 2)):
                    dve.wait_ge(emptied["F1"], now.fill(("local_scores", *unit_before(l, u, 2)), "F1", ago=n < 2))
                for parity in range(2):
                    k = f"F{parity}"
                    dve.wait_ge(filled[k], now.fill(step, k))
                    ins = v.tensor_reduce(l_max[:, u % 2, 2 * parity:2 * parity + 2],
                                          bank[k][:].rearrange("p (a j) -> p a j", a=2)[:, :, lo:], AX.X, ALU.max,
                                          negate=True)
                ins.then_inc(l_max_done, 1)

            def p_turn(step, l, u):
                n = TW * QUADS * l + u
                lo = 1 if u // QUADS == 0 else 0
                if now.past(not (not l and not u)):
                    dve.wait_ge(filled["V"], now.fill(("local_values", *unit_before(l, u, 1)), "V", ago=not l and not u))
                dve.wait_ge(filled["F2"], now.fill(step, "F2"))
                v.tensor_copy(pT[:, 0, :, :].rearrange("p (a j) i -> p a j i", a=2)[:, :, lo:, :],
                              bank["F2"][:].rearrange("p (a j i) -> p a j i", a=2, j=2)[:, :, lo:, :])\
                    .then_inc(emptied["F2"], 1)
                dve.wait_ge(emptied["F1"], now.fill(("local_scores", l, u), "F1"))
                if now.past(not (n < 2)):
                    dve.wait_ge(emptied["V"], now.fill(("local_values", *unit_before(l, u, 2)), "V", ago=n < 2))
                v.reciprocal(l_inv[:, u % 2, :], l_sum[:, u % 2, :]).then_inc(l_inv_done, 1)

            def local_values(step, l, u):
                t, quad = u // QUADS, u % QUADS
                dve.wait_ge(filled["V"], now.fill(step, "V"))
                dve.wait_ge(l_inv_done, now.at(l_inv_done, TW * QUADS * l + u + 1))
                if quad == 0:
                    if now.past(not (not l and not t)):
                        dve.wait_ge(filled["F2"], now.fill(("o_turn", *window_before(l, t)), "F2", ago=not l and not t))
                v.tensor_tensor(
                    o_tok[:, 4 * quad:4 * quad + 4, :].rearrange("p (a b) d -> p a b d", a=2),
                    bank["V"][:, 0:4 * HD].rearrange("p (a b d) -> p a b d", a=2, b=2),
                    l_inv[:, u % 2, :].rearrange("p (b a) -> p a b", b=2)[:, :, :, None].to_broadcast([P, 2, 2, HD]),
                    ALU.mult).then_inc(emptied["V"], 1)

            def out_proj(step, l, t):
                dve.wait_ge(filled["F3"], now.fill(step, "F3"))
                if t == 0:
                    if now.past(l):
                        dve.wait_ge(mid_b_ready, now.at(mid_b_ready, l))
                    if now.past(TW * l):
                        dve.wait_ge(h_ready, now.at(h_ready, TW * l))
                v.tensor_tensor(x_mid[:, t, :], bank["F3"][:, 0:D], x_tok[:, t, :], ALU.add)\
                    .then_inc(emptied["F3"], 1)

            def shift_turn(step, l):
                dve.wait_ge(filled["F1"], now.fill(step, "F1"))
                dve.wait_ge(emptied["F3"], now.fill(("out_proj", l, TW - 1), "F3"))
                base = TW + 2 * TW * l
                dve.wait_ge(aggr_done, now.at(aggr_done, 1 + l))
                for t in range(TW):
                    v.bn_stats(stats[:, t, 0, :], x_mid[:, t, 0:P]).then_inc(stats_done, 1)
                    v.bn_stats(stats[:, t, 1, :], bank["F1"][:, t * P:(t + 1) * P]).then_inc(stats_done, 1)
                dve.wait_ge(stats_done, now.at(stats_done, base + 2 * TW))
                dve.wait_ge(eps_done, now.at(eps_done, 1 + l))
                v.memset(opener[:], 0.0)
                for t in range(TW):
                    ins = v.bn_aggr(mean_var[:, t, :], stats[:, t, :, :].rearrange("p a s -> p (a s)"))
                ins.then_inc(aggr_done, 1)
                dve.wait_ge(rstd_done, now.at(rstd_done, 2 + l))
                dve.wait_ge(rot_added, now.at(rot_added, 2 * TW * (l + 1)))
                dve.wait_ge(qk_ready, now.at(qk_ready, 2 * TW * (l + 1)))
                for t in range(TW):
                    v.tensor_scalar(h_tok[:, t, 0:P], x_mid[:, t, 0:P], mean_var[:, t, 0:1], rstd[:, t:t + 1],
                                    ALU.subtract, ALU.mult).then_inc(h_ready, 1)
                for t in range(TW):
                    ins = v.tensor_scalar(h_tok[:, t, P:D], bank["F1"][:, t * P:(t + 1) * P], mean_var[:, t, 0:1],
                                          rstd[:, t:t + 1], ALU.subtract, ALU.mult)
                ins.then_inc(emptied["F1"], 1)

            def up(step, l, i):
                ka, kg = banks_of(step)
                m = hidden_rows(i)
                dve.wait_ge(filled[ka], now.fill(step, ka))
                dve.wait_ge(emptied[kg], now.fill(step, kg))
                v.scalar_tensor_tensor(hidden[0:m, i, :], bank[ka][0:m, :], b_1[l][0:m, i:i + 1], gelu[0:m, i % 2, :],
                                       op0=ALU.add, op1=ALU.mult).then_inc(emptied[ka], 1)

            def down(step, l, t):
                k = f"F{t}"
                dve.wait_ge(filled[k], now.fill(step, k))
                dve.wait_ge(mid_b_ready, now.at(mid_b_ready, l + 1))
                v.tensor_tensor(x_tok[:, t, :], bank[k][:, 0:D], x_mid_b[:, t, :], ALU.add)\
                    .then_inc(emptied[k], 1)

            def gated(step):
                stream_ready(dve, now, LAYERS)
                if now.past(0):
                    dve.wait_ge(stored, now.at(stored, 0))
                v.tensor_scalar(o_fin[:], x_tok[:], LEAST, None, ALU.max).then_inc(bounded, 1)
                dve.wait_ge(exp_done, now.at(exp_done, 1))
                v.tensor_scalar(o_fin[:], o_fin[:], 1.0, None, ALU.add).then_inc(one_plus, 1)
                dve.wait_ge(one_plus, now.at(one_plus, 1))
                v.reciprocal(h_tok, o_fin[:]).then_inc(sig_done, 1)

            steps = {
                "norm": norm, "talk_qk": talk_qk, "talk_v": talk_v, "scores": scores, "mix": mix, "project": project,
                "qkv": qkv, "k_turn": k_turn, "local_scores": local_scores, "p_turn": p_turn,
                "local_values": local_values, "out_proj": out_proj, "shift_turn": shift_turn, "up": up, "down": down,
                "gated": gated,
            }

            def body():
                for step in order:
                    if step[0] in steps:
                        steps[step[0]](step, *step[1:])

            now.run(dve, body)

        @block.gpsimd
        def _(pool):
            now = Counts()
            g = nc.gpsimd
            pool.dma_start(x_in[:], a["x"][0]).then_inc(x_loaded, 16)
            pool.wait_ge(pads, 6)
            pool.wait_ge(loads, LOADED)
            pool.wait_ge(tables, TABLES)

            def inverse_std(n):
                pool.wait_ge(aggr_done, now.at(aggr_done, n))
                g.tensor_tensor(var_eps[:], mean_var[:, :, 1], eps[:], ALU.add).then_inc(eps_done, 1)
                pool.wait_ge(eps_done, now.at(eps_done, n))
                if n == 1:
                    if not now.first:
                        pool.wait_ge(emptied["F1"], now.fill(("shift_turn", LAYERS - 1), "F1", ago=1))
                elif n == 2:
                    pool.wait_ge(x_ready, now.at(x_ready, TW))
                else:
                    pool.wait_ge(emptied["F1"], now.fill(("shift_turn", n - 3), "F1"))
                g.tensor_tensor(rstd[:], var_eps[:], minus_half[:, 0:TW], ALU.pow).then_inc(rstd_done, 1)

            def norm(step):
                pool.wait_ge(x_loaded, now.at(x_loaded, 16))
                if now.past(0):
                    pool.wait_ge(o_ready, now.at(o_ready, 0))
                g.tensor_tensor(x_keep[:], x_in[:], one[:, :, None].to_broadcast([P, TW, D]), ALU.mult)\
                    .then_inc(x_kept, 1)
                inverse_std(1)

            def talk_qk(step):
                pool.wait_ge(x_kept, now.at(x_kept, 1))
                pool.wait_ge(x_ready, now.at(x_ready, TW))
                pool.dma_start(x_in[:], a["x_next"][bass.ds(now.b + 1, 1)].rearrange("a p t f -> (a p) t f"))\
                    .then_inc(x_loaded, 16)
                pool.wait_ge(emptied["S1"], now.fill(step, "S1"))
                if now.past(0):
                    pool.wait_ge(q_mixed, now.at(q_mixed, 0))
                g.tensor_tensor(q_rope[:], raw_qk[:, 0:2, :], rope_cos[:, None, :].to_broadcast([P, 2, N]),
                                ALU.mult).then_inc(q_parts, 1)
                for s in range(2):
                    ins = g.tensor_tensor(t_q[:, s, :], raw_qk[:, 1 - s, :], rope_sin[:], ALU.mult)
                ins.then_inc(q_parts, 1)
                pool.wait_ge(q_parts, now.at(q_parts, 2))
                g.tensor_tensor(q_rope[:, 0], q_rope[:, 0], t_q[:, 0], ALU.subtract)
                g.tensor_tensor(q_rope[:, 1], q_rope[:, 1], t_q[:, 1], ALU.add).then_inc(q_roped, 1)

            def expand(step, c):
                pool.wait_ge(q_roped, now.at(q_roped, 1))
                n = (c - 2) * ET + ET - 1
                if now.past(not (n < 0)):
                    pool.wait_ge(filled[f"S{n % 2}"], now.fill(("scores", n % TILES), f"S{n % 2}", ago=n < 0))
                shape = [P, ET, GH, RI]
                for s in range(2):
                    q = q_rope[:, s, c * ET * RI:(c + 1) * ET * RI].rearrange("p (m i) -> p m i", m=ET)
                    g.tensor_tensor(q_mix[:, c % 2, s].rearrange("p m (g i) -> p m g i", g=GH),
                                    q[:, :, None, :].to_broadcast(shape),
                                    w_pre[:, None, :, None].to_broadcast(shape), ALU.mult).then_inc(q_mixed, 1)

            def qkv(step, l, t):
                w = TW * l + t
                if now.past(not (not w)):
                    pool.wait_ge(filled["F3"], now.fill(("k_turn", *window_before(l, t)), "F3", ago=not w))
                if not t:
                    c = ("up", (l - 1) % LAYERS, HC - 1)
                    if now.past(not (not l)):
                        pool.wait_ge(emptied[banks_of(c)[0]], now.fill(c, banks_of(c)[0], ago=not l))
                for j in range(2):
                    pool.wait_ge(rot_done, now.at(rot_done, 2 * w + j + 1))
                    g.tensor_tensor(qk_tok[:, j, :], rot_a[:, j, :], rot_b[:, j, :], ALU.add).then_inc(rot_added, 1)
                pool.wait_ge(clip_done, now.at(clip_done, w + 1))
                if now.past(2 * w):
                    pool.wait_ge(qk_ready, now.at(qk_ready, 2 * w))
                g.tensor_tensor(inv_norms[:], norms_c[:], minus_half[:], ALU.pow).then_inc(inv_norm_done, 1)
                pool.wait_ge(inv_norm_done, now.at(inv_norm_done, w + 1))
                pool.wait_ge(rot_added, now.at(rot_added, 2 * w + 2))
                for j in range(2):
                    g.tensor_tensor(qk_tok[:, j, :].rearrange("p (h d) -> p h d", h=H),
                                    qk_tok[:, j, :].rearrange("p (h d) -> p h d", h=H),
                                    inv_norms[:, j * H:(j + 1) * H, None].to_broadcast([P, H, HD]), ALU.mult)\
                        .then_inc(qk_ready, 1)

            def half_turn(step, l):
                pool.wait_ge(emptied["F3"], now.fill(("out_proj", l, TW - 1), "F3"))
                g.tensor_tensor(x_mid_b, x_mid[:], b_2[l][:, None, :].to_broadcast([P, TW, D]), ALU.add)\
                    .then_inc(mid_b_ready, 1)

            def shift_turn(step, l):
                inverse_std(2 + l)

            def gated(step):
                pool.wait_ge(sig_done, now.at(sig_done, 1))
                pool.wait_ge(emptied["M"], now.fill(("project", TW - 1), "M"))
                g.tensor_tensor(h_tok, h_tok, x_tok[:], ALU.mult).then_inc(silu_done, 1)
                pool.wait_ge(silu_done, now.at(silu_done, 1))
                g.tensor_tensor(s_tok[:], s_tok[:], h_tok, ALU.mult).then_inc(gated_done, 1)
                pool.wait_ge(gated_done, now.at(gated_done, 1))
                g.tensor_tensor(o_fin[:], s_tok[:], x_keep[:], ALU.add).then_inc(o_ready, 1)
                pool.wait_ge(o_ready, now.at(o_ready, 1))
                pool.dma_start(out[bass.ds(now.b, 1)].rearrange("a (t p) f -> (a p) t f", p=P), o_fin[:])\
                    .then_inc(stored, 16)

            steps = {
                "norm": norm, "talk_qk": talk_qk, "expand": expand, "qkv": qkv, "half_turn": half_turn,
                "shift_turn": shift_turn, "gated": gated,
            }

            def body():
                for step in order:
                    if step[0] in steps:
                        steps[step[0]](step, *step[1:])

            now.run(pool, body)


def shape_constants():
    f = np.float32
    c = {"ident": np.eye(P, dtype=f)}
    i, j = np.arange(P)[:, None], np.arange(P)[None, :]
    prev, cur = np.where(i > j, MASKED, 0.0), np.where(i < j, MASKED, 0.0)
    c["mask"] = np.tile(np.concatenate([prev, cur], 1), (1, 2)).astype(f)
    c["delta"] = (np.arange(P)[:, None] % RI == np.arange(RI)[None, :]).astype(f)
    inv = f(1.0) / f(10000.0) ** (np.arange(0, GD, 2, dtype=f) / f(GD))
    fr = (np.arange(N, dtype=f)[:, None] * inv[None, :]).astype(f)
    cos, sin = np.tile(np.cos(fr).T, (GH, 1)), np.tile(np.sin(fr).T, (GH, 1))
    c["rope_cos"] = cos.astype(f)
    c["rope_sin"] = sin.astype(f)
    half = np.arange(0, HD, 2, dtype=f)
    inv = f(1.0) / f(10000.0) ** (half / f(HD))
    t = np.arange(N, dtype=f)
    fr = (t[:, None] * inv[None, :]).astype(f)
    base = (half + f(0.4 * HD)) / f(1.4 * HD)
    power = (t - N // 2) / f(P // 2)
    sc = (base[None, :] ** power[:, None]).astype(f)
    two = lambda x: np.concatenate([x, x], 1)
    cos, sin, sc = two(np.cos(fr)), two(np.sin(fr)), two(sc)
    sin[:, :HD // 2] *= -1
    tab = np.stack([cos * sc * f(8), sin * sc * f(8), cos / sc, sin / sc]).astype(f)
    c["xpos"] = np.ascontiguousarray(tab.reshape(4, TW, P, HD).transpose(2, 0, 1, 3))
    return c


def laid_out(i):
    i = {k: np.asarray(v) for k, v in i.items()}
    bc = lambda x: np.ascontiguousarray(np.broadcast_to(x, (P, *x.shape)))
    kp = lambda w: np.ascontiguousarray(w.reshape(-1, P, w.shape[-1]).transpose(1, 0, 2))
    o = {}
    x = i["L0_attn_x"].reshape(B, TW, P, D).transpose(0, 2, 1, 3)
    o["x_next"] = np.ascontiguousarray(np.concatenate([x, x[:1]]))
    w = i["L0_attn_Wqkv"]
    qk = w[:2 * D].reshape(2, GH, 2, HALF, KC, P).transpose(5, 4, 0, 2, 1, 3)
    o["w_qk"] = np.ascontiguousarray(qk.reshape(P, KC, 4, P))
    bias = i["L0_attn_bqkv"]
    o["b_qk"] = np.ascontiguousarray(bias[:2 * D].reshape(2, GH, 2, HALF).transpose(1, 3, 0, 2).reshape(P, 4))
    o["w_v"] = kp(w[2 * D:].T)
    o["b_v"] = bc(bias[2 * D:])
    o["w_pre"] = np.repeat(i["L0_attn_Wpre"].T, RI, axis=0)
    o["w_post"] = np.repeat(i["L0_attn_Wpost"].T, RI, axis=0)
    wo = np.zeros((GR, PAD, GH // GR, D), w.dtype)
    wo[:, :GD] = i["L0_attn_Wout"].T.reshape(GH // GR, GR, GD, D).transpose(1, 2, 0, 3)
    o["w_out"] = wo.reshape(P, GH // GR, D)
    o["b_out"] = bc(i["L0_attn_bout"])
    qs, ks = i["L0_ffn_q_scale"], i["L0_ffn_k_scale"]
    sw = lambda s: np.concatenate([s[:, HD // 2:], s[:, :HD // 2]], 1)
    sc = np.stack([qs, sw(qs), ks, sw(ks)], 1)
    o["scales"] = np.ascontiguousarray(np.broadcast_to(sc[:, None], (LAYERS, P, 4, HD)))
    per = lambda f: np.stack([f(l) for l in range(LAYERS)])
    o["w_qkv"] = per(lambda l: kp(i["L0_ffn_wqkv"][l]))
    o["w_o"] = per(lambda l: kp(i["L0_ffn_wo"][l]))
    o["w_1"] = per(lambda l: kp(i["L0_ffn_w1"][l]))

    def padded(v):
        z = np.zeros((HC * P, *v.shape[1:]), v.dtype)
        z[:HID] = v
        return z
    o["w_2"] = per(lambda l: kp(padded(i["L0_ffn_w2"][l])))
    b1 = i["L0_ffn_b1"]
    o["b_1"] = per(lambda l: np.concatenate([padded(b1[l][:HID]).reshape(HC, P).T, padded(b1[l][HID:]).reshape(HC, P).T], 1))
    o["b_2"] = per(lambda l: bc(i["L0_ffn_b2"][l]))
    o["ln_w"] = per(lambda l: np.concatenate([i["L0_ffn_ln_g"][l].reshape(KC, P).T, i["L0_ffn_ln_b"][l].reshape(KC, P).T], 1))
    return {k: np.ascontiguousarray(v) for k, v in o.items()}


def kernel(**inputs):
    import concourse.bacc as bacc
    from concourse.bass_utils import run_bass_kernel_spmd

    arrays = {**laid_out(inputs), **shape_constants()}
    nc = bacc.Bacc("TRN2", target_bir_lowering=False, num_devices=1)
    a = {k: nc.dram_tensor(f"in_{k}", v.shape, mybir.dt.from_np(v.dtype), kind="ExternalInput").ap()
         for k, v in arrays.items()}
    a["x"] = a["x_next"]
    out = nc.dram_tensor("out_y", (B, N, D), F32, kind="ExternalOutput").ap()
    gate_network_kernel(nc, a, out)
    r = run_bass_kernel_spmd(nc, [{f"in_{k}": v for k, v in arrays.items()}], core_ids=[0])
    return r.results[0]["out_y"]
```

```python
from contextlib import ExitStack

import numpy as np

import concourse.bass as bass
from concourse import mybir

ALU = mybir.AluOpType
ACT = mybir.ActivationFunctionType
AX = mybir.AxisListType
F32 = mybir.dt.float32
BF16 = mybir.dt.bfloat16

P = 128
B, N, D = 16, 512, 256
TW = N // P
KC = D // P

GH, GD = 16, 16
HALF = GD // 2
RI = P // GH
TILES = N // RI
CT = 8
ET = 4
CI = CT * RI
CHUNKS = TILES // CT
LAG = 2
PB = LAG + 1
GR = 4
PAD = 32

LAYERS = 2
H, HD = 8, 64
INNER = H * HD
HID = D * 4 * 2 // 3
HC = -(-HID // P)
QUADS = 2
MASKED = -1e30
LEAST = -87.5


def hidden_rows(c):
    return min(P, HID - c * P)


AHEAD = [("norm",), ("scale",), ("x_turn", 0)]
BEHIND = [("gated",)]


def step_order():
    head = [("talk_qk",), ("talk_v",), ("expand", 0), ("qkv", 0, 0)]
    talk = []
    for n in range(TILES):
        talk.append([("scores", n)])
        if n % ET == 0 and n // ET + 1 < TILES // ET:
            talk[-1].append(("expand", n // ET + 1))
        if n % CT == LAG and n >= CT:
            talk[-1].append(("values", n // CT - 1))
        if n >= LAG:
            talk[-1].append(("mix", n - LAG))
        if n % (2 * CT) == 5 and n >= CT:
            talk[-1].append(("project", n // (2 * CT) - 1))
    for n in range(TILES - LAG, TILES):
        talk.append([("mix", n)])
    talk.append([("values", CHUNKS - 1)])
    talk.append([("project", TW - 1)])

    REST = []
    gate = []
    for l in range(LAYERS):
        if l:
            gate.append([("x_turn", l)])
        for t in range(TW):
            if l or t:
                gate.append([("qkv", l, t)])
            if t:
                gate.append([("q_turn", l, t - 1)])
                gate.append([("k_turn", l, t - 1)])
        gate += [REST] * 2
        gate.append([("q_turn", l, TW - 1)])
        gate.append([("k_turn", l, TW - 1)])
        units = TW * QUADS
        for u in range(units + 4):
            if u < units:
                gate.append([("local_scores", l, u)])
            if u >= 4 and u % QUADS == 0:
                gate.append([("o_turn", l, u // QUADS - 2)])
            if 1 <= u <= units:
                gate.append([("p_turn", l, u - 1)])
            if 2 <= u <= units + 1:
                gate[-1].append(("local_values", l, u - 2))
            if u >= 5 and u % QUADS == 1:
                gate.append([("out_proj", l, u // QUADS - 2)])
        gate += [[("half_turn", l)], [("shift_turn", l)], REST, [("h_scale", l)], REST, [("h_turn", l)]]
        gate += [[("up", l, c)] for c in range(HC)]
        if l == LAYERS - 1:
            gate[-3:-3] = [[("norm",)]]
            gate[-1:-1] = [[("scale",)]]
            gate.append([("x_turn", 0)])
        gate += [[("down", l, t)] for t in range(TW)]

    order, done = list(head), 0
    for i, steps in enumerate(talk):
        order += steps
        upto = (i + 1) * len(gate) // len(talk)
        for g in gate[done:upto]:
            order += g
        done = upto
        if i == 1:
            order += [("gated",), ("keep",)]
    return order


def banks_of(step):
    kind = step[0]
    if kind == "scores":
        return [f"S{step[1] % 2}"]
    if kind in ("mix", "project"):
        return ["M"]
    if kind in ("values", "local_values"):
        return ["V"]
    if kind == "talk_qk":
        return ["S0", "S1", "M", "V"]
    if kind == "talk_v":
        return ["S0", "S1"]
    if kind == "up":
        return ["F0", "F1"] if step[2] % 2 == 0 else ["F2", "F3"]
    if kind == "down":
        return [f"F{step[2]}"]
    return {
        "x_turn": ["F0", "F1"], "qkv": ["F0", "F1", "F2"], "q_turn": ["F3"], "k_turn": ["F3"],
        "local_scores": ["F0", "F1"], "p_turn": ["F2", "F3"], "o_turn": ["F2"], "out_proj": ["F3"],
        "half_turn": ["F0"], "shift_turn": ["F1"], "h_turn": ["F2", "F3"],
    }.get(kind, [])


BANKS = ["S0", "S1", "M", "V", "F0", "F1", "F2", "F3"]


def gate_network_kernel(nc, a, out):
    order = step_order()
    ahead = {k: 1 if k in banks_of(("x_turn", 0)) else 0 for k in BANKS}
    filling, fillings = {}, {k: 0 for k in BANKS}
    for step in order:
        for k in banks_of(step):
            fillings[k] += 1
            filling[step, k] = fillings[k]

    with ExitStack() as ctx:
        def sb(name, shape, dt=F32):
            return ctx.enter_context(nc.sbuf_tensor(name, [P, *shape], dt))

        ident = sb("ident", [P])
        ident_bf = sb("ident_bf", [P], BF16)
        mask_bf = sb("mask_bf", [2, 2 * P], BF16)
        rope_cos = sb("rope_cos", [N])
        rope_sin = sb("rope_sin", [N])
        delta = sb("delta", [RI])
        w_qk = sb("w_qk", [KC, 4, P])
        b_qk = sb("b_qk", [4])
        w_v = sb("w_v", [KC, D])
        b_v = sb("b_v", [D])
        w_pre = sb("w_pre", [GH])
        w_post = sb("w_post", [GH])
        w_out = sb("w_out", [GR, D])
        b_out = sb("b_out", [D])
        mixer = sb("mixer", [GH, RI])
        rot = [sb(f"rot{l}", [4, TW, HD]) for l in range(LAYERS)]
        w_qkv = sb("w_qkv", [KC, 3 * INNER])
        w_o = [sb(f"w_o{l}", [INNER // P, D]) for l in range(LAYERS)]
        w_1 = sb("w_1", [KC, 2 * HID])
        w_2 = [sb(f"w_2{l}", [HC, D]) for l in range(LAYERS)]
        b_1 = [sb(f"b_1{l}", [2 * HC]) for l in range(LAYERS)]
        b_2 = [sb(f"b_2{l}", [D]) for l in range(LAYERS)]
        ln_w = [sb(f"ln_w{l}", [2 * KC]) for l in range(LAYERS)]
        minus_half = sb("minus_half", [2 * H])
        opener = sb("opener", [1])
        eps = sb("eps", [TW])

        x_in = sb("x_in", [TW, D])
        x_keep = sb("x_keep", [TW, D])
        x_tok = sb("x_tok", [TW, D])
        xT = sb("xT", [KC, N + 1])
        stats = sb("stats", [TW, 2, 6])
        mean_var = sb("mean_var", [TW, 2])
        var_eps = sb("var_eps", [TW])
        rstd = sb("rstd", [TW])
        q_rope = sb("q_rope", [2, N])
        k_rope = sb("k_rope", [2, N])
        v_pad = sb("v_pad", [TW, GH, PAD])
        q_mix = sb("q_mix", [2, 2, ET, P])
        neg_max = sb("neg_max", [2])
        row_sum = sb("row_sum", [PB])
        row_inv = sb("row_inv", [2])
        probs = sb("probs", [PB, N])
        mixer_n = sb("mixer_n", [2, P])
        mixed = sb("mixed", [TW, GH, CI])
        before = mixed[:].rearrange("p j g i -> p (j g i)").rearrange("p (a n) -> p a n", n=N)
        raw_qk, t_q, t_k = before[:, 0:4], before[:, 4:6], before[:, 6:8]
        oT = sb("oT", [GR, P])
        s_tok = sb("s_tok", [TW, D])

        shared = sb("shared", [8, INNER])
        sq = shared[:, 0:2]
        rot_a, rot_b, qk_tok = shared[:, 2:4], shared[:, 4:6], shared[:, 6:8]
        x_mid_b, h_tok = (shared[:, j:j + 2].rearrange("p a (b f) -> p (a b) f", f=D) for j in (0, 2))
        hT, gelu = shared[:, 4:6], shared[:, 6:8]
        norms = sb("norms", [2 * H])
        norms_c = sb("norms_c", [2 * H])
        inv_norms = sb("inv_norms", [2 * H])
        att = sb("att", [3 * 4, N])
        qT = att[:, 0:4, :]
        kT = att[:, 4:8, :]
        v_loc = att[:, 8:12, :]
        hidden = att[:, 0:HC, :]
        l_max = sb("l_max", [2, 4])
        l_sum = sb("l_sum", [2, 4])
        l_inv = sb("l_inv", [2, 4])
        l_probs = sb("l_probs", [2, 4, 2 * P])
        pT = sb("pT", [2, 4, P])
        o_tok = sb("o_tok", [H, HD])
        o_locT = sb("o_locT", [4, P])
        x_mid = sb("x_mid", [TW, D])
        midT = sb("midT", [N + 1])
        o_fin = sb("o_fin", [TW, D])
        setup = l_probs[:].rearrange("p a h k -> p (a h k)")
        xpos = setup[:, 0:4 * TW * HD].rearrange("p (j t d) -> p j t d", j=4, t=TW)
        mask = setup[:, (4 * TW + 4 * LAYERS) * HD:]
        scales = [setup[:, (4 * TW + 4 * l) * HD:(4 * TW + 4 * l + 4) * HD].rearrange("p (j d) -> p j d", j=4)
                  for l in range(LAYERS)]

        bank = {k: ctx.enter_context(nc.psum_tensor(f"bank_{k}", [P, 512], F32)) for k in BANKS}

        per, base = {}, {}

        def sem(name, count, before=0):
            h = ctx.enter_context(nc.semaphore(name))
            per[id(h)] = count
            base[id(h)] = before
            return h

        filled = {k: sem(f"filled_{k}", fillings[k], ahead[k]) for k in BANKS}
        emptied = {k: sem(f"emptied_{k}", fillings[k], ahead[k]) for k in BANKS}
        QL = TW * QUADS * LAYERS
        WL = TW * LAYERS
        loads = sem("loads", 0)
        tables = sem("tables", 0)
        pads = sem("pads", 0)
        x_loaded = sem("x_loaded", 16, 16)
        keep_loaded = sem("keep_loaded", 16)
        qkv_loaded = sem("qkv_loaded", 16 * LAYERS)
        w_1_loaded = sem("w_1_loaded", 16 * LAYERS)
        stats_done = sem("stats_done", LAYERS * 2 * TW + TW, TW)
        aggr_done = sem("aggr_done", LAYERS + 1, 1)
        eps_done = sem("eps_done", LAYERS + 1, 1)
        rstd_done = sem("rstd_done", LAYERS + 1, 1)
        x_ready = sem("x_ready", TW, TW)
        k_parts = sem("k_parts", 2)
        k_roped = sem("k_roped", 1)
        q_parts = sem("q_parts", 2)
        q_roped = sem("q_roped", 1)
        q_mixed = sem("q_mixed", 2 * TILES // ET)
        max_done = sem("max_done", TILES)
        inv_done = sem("inv_done", TILES)
        mixer_done = sem("mixer_done", TILES)
        s_done = sem("s_done", TW)
        norm_done = sem("norm_done", 2 * WL)
        rot_done = sem("rot_done", 2 * WL)
        clip_done = sem("clip_done", WL)
        inv_norm_done = sem("inv_norm_done", WL)
        rot_added = sem("rot_added", 2 * WL)
        qk_ready = sem("qk_ready", 2 * WL)
        l_max_done = sem("l_max_done", QL)
        l_inv_done = sem("l_inv_done", QL)
        mid_b_ready = sem("mid_b_ready", LAYERS)
        h_ready = sem("h_ready", LAYERS * TW)
        gelu_done = sem("gelu_done", LAYERS * HC)
        bounded = sem("bounded", 1)
        exp_done = sem("exp_done", 1)
        one_plus = sem("one_plus", 1)
        sig_done = sem("sig_done", 1)
        silu_done = sem("silu_done", 1)
        gated_done = sem("gated_done", 1)
        o_ready = sem("o_ready", 1)
        stored = sem("stored", 16)

        once = [
            (ident[:], a["ident"]), (mask, a["mask"]),
            (rope_cos[:], a["rope_cos"]), (rope_sin[:], a["rope_sin"]), (delta[:], a["delta"]),
            (w_qk[:], a["w_qk"]), (b_qk[:], a["b_qk"]), (w_v[:], a["w_v"]), (b_v[:], a["b_v"]),
            (w_pre[:], a["w_pre"]), (w_post[:], a["w_post"]), (w_out[:], a["w_out"]),
            (b_out[:], a["b_out"]), (xpos, a["xpos"]),
        ]
        for l in range(LAYERS):
            once += [
                (scales[l], a["scales"][l]), (w_o[l][:], a["w_o"][l]),
                (w_2[l][:], a["w_2"][l]), (b_1[l][:], a["b_1"][l]),
                (b_2[l][:], a["b_2"][l]), (ln_w[l][:], a["ln_w"][l]),
            ]
        LOADED = 16 * len(once)
        TABLES = 4 + 4 * LAYERS

        class Counts:
            def __init__(self):
                self.b, self.first, self.ahead = -1, True, True

            def past(self, k):
                return k > 0 or not self.first

            def at(self, sem, k):
                return self.b * per[id(sem)] + base[id(sem)] + k

            def fill(self, step, k, ago=0):
                if self.ahead:
                    return ahead[k]
                return self.b * fillings[k] + ahead[k] + filling[step, k] - ago * fillings[k]

            def was_filled(self, step, k):
                return not self.ahead and self.past(ahead[k] + filling[step, k] - 1)

            def x_turned(self, l, k):
                return ahead[k] if self.first and not l else self.fill(("x_turn", l), k, ago=not l)

            def run(self, eng, steps):
                def go(list_of_steps):
                    for step in list_of_steps:
                        if step[0] in steps and not (step in BEHIND and self.first):
                            steps[step[0]](step, *step[1:])
                go(AHEAD)
                self.b, self.ahead = 0, False
                go(order)
                self.first = False
                with eng.Fori(1, B) as b:
                    self.b = b
                    go(order)
                self.b = B
                go(BEHIND)

        def window_before(l, t):
            return (l, t - 1) if t else ((l - 1) % LAYERS, TW - 1)

        def unit_before(l, u, by):
            n = (TW * QUADS * l + u - by) % (LAYERS * TW * QUADS)
            return n // (TW * QUADS), n % (TW * QUADS)

        def stream_ready(eng, now, l, ago=0):
            if l == 0:
                eng.wait_ge(x_ready, now.at(x_ready, TW))
            else:
                for t in range(TW):
                    eng.wait_ge(emptied[f"F{t}"], now.fill(("down", l - 1, t), f"F{t}", ago=ago))

        def store_mixed(eng, copy, now, n):
            c, m = n // CT, n % CT
            if c:
                eng.wait_ge(filled["V"], now.fill(("values", c - 1), "V"))
            else:
                eng.wait_ge(q_roped, now.at(q_roped, 1))
                eng.wait_ge(k_roped, now.at(k_roped, 1))
            copy(mixed[:, :, :, m * RI:(m + 1) * RI],
                 bank["M"][:].rearrange("p (j g i) -> p j g i", j=TW, g=GH)).then_inc(emptied["M"], 1)

        block = ctx.enter_context(nc.Block())

        @block.sync
        def _(sp):
            now = Counts()
            for dst, src in once:
                sp.dma_start(dst, src).then_inc(loads, 16)
            sp.dma_start(w_qkv[:], a["w_qkv"][0]).then_inc(qkv_loaded, 16)
            sp.dma_start(w_1[:], a["w_1"][0]).then_inc(w_1_loaded, 16)

            def qkv(step, l, t):
                if t == TW - 1:
                    sp.wait_ge(filled["F2"], now.fill(step, "F2"))
                    sp.dma_start(w_qkv[:], a["w_qkv"][(l + 1) % LAYERS]).then_inc(qkv_loaded, 16)

            def up(step, l, i):
                if i == HC - 1:
                    k = banks_of(step)[1]
                    sp.wait_ge(filled[k], now.fill(step, k))
                    sp.dma_start(w_1[:], a["w_1"][(l + 1) % LAYERS]).then_inc(w_1_loaded, 16)

            now.run(sp, {"qkv": qkv, "up": up})
            sp.wait_ge(keep_loaded, 16 * B)
            sp.wait_ge(x_loaded, 16 * (B + 1))
            sp.wait_ge(qkv_loaded, 16 * (LAYERS * B + 1))
            sp.wait_ge(w_1_loaded, 16 * (LAYERS * B + 1))
            sp.wait_ge(stored, 16 * B)

        @block.tensor
        def _(pe):
            now = Counts()
            mm = nc.tensor.matmul
            turn = nc.tensor.transpose
            pe.wait_ge(loads, LOADED)
            pe.wait_ge(tables, TABLES)
            pe.wait_ge(pads, 5)

            def x_turn(step, l):
                stream_ready(pe, now, l)
                for c in range(KC):
                    if now.was_filled(step, f"F{c}"):
                        pe.wait_ge(emptied[f"F{c}"], now.fill(step, f"F{c}") - 1)
                    x = x_tok if l else x_in
                    for t in range(TW):
                        last = turn(bank[f"F{c}"][:, t * P:(t + 1) * P], x[:, t, c * P:(c + 1) * P], ident[:])
                    last.then_inc(filled[f"F{c}"], 1)

            def talk_qk(step):
                for c in range(KC):
                    pe.wait_ge(emptied[f"F{c}"], now.x_turned(0, f"F{c}"))
                for j, k in enumerate(["S0", "S1", "M", "V"]):
                    if now.was_filled(step, k):
                        pe.wait_ge(emptied[k], now.fill(step, k) - 1)
                    for c in range(KC):
                        last = mm(bank[k][:], w_qk[:, c, j, :], xT[:, c, 1:N + 1], start=(c == 0), stop=(c == KC - 1))
                    last.then_inc(filled[k], 1)

            def talk_v(step):
                for t in range(TW):
                    k = f"S{t // 2}"
                    if t % 2 == 0:
                        if now.was_filled(step, k):
                            pe.wait_ge(emptied[k], now.fill(step, k) - 1)
                    for c in range(KC):
                        last = mm(bank[k][:, (t % 2) * D:(t % 2 + 1) * D], xT[:, c, 1 + t * P:1 + (t + 1) * P],
                                  w_v[:, c, :], start=(c == 0), stop=(c == KC - 1))
                    if t % 2:
                        last.then_inc(filled[k], 1)

            def scores(step, n):
                k = f"S{n % 2}"
                if n == 0:
                    pe.wait_ge(k_roped, now.at(k_roped, 1))
                if n % ET == 0:
                    pe.wait_ge(q_mixed, now.at(q_mixed, 2 * (n // ET + 1)))
                if now.was_filled(step, k):
                    pe.wait_ge(emptied[k], now.fill(step, k) - 1)
                for s in range(2):
                    last = mm(bank[k][:], q_mix[:, (n // ET) % 2, s, n % ET, :], k_rope[:, s, :],
                              start=(s == 0), stop=(s == 1))
                last.then_inc(filled[k], 1)

            def mix(step, n):
                pe.wait_ge(mixer_done, now.at(mixer_done, n + 1))
                if now.was_filled(step, "M"):
                    pe.wait_ge(emptied["M"], now.fill(step, "M") - 1)
                for j in range(TW):
                    last = mm(bank["M"][:, j * P:(j + 1) * P], probs[:, n % PB, j * P:(j + 1) * P],
                              mixer_n[:, n % 2, :], start=True, stop=True)
                last.then_inc(filled["M"], 1)

            def values(step, c):
                pe.wait_ge(emptied["M"], now.fill(("mix", (c + 1) * CT - 1), "M"))
                for j in range(2):
                    pe.wait_ge(emptied[f"S{j}"], now.fill(("talk_v",), f"S{j}"))
                if now.was_filled(step, "V"):
                    pe.wait_ge(emptied["V"], now.fill(step, "V") - 1)
                for r in range(GH // GR):
                    for j in range(TW):
                        for q in range(GR):
                            g = GR * r + q
                            last = mm(bank["V"][PAD * q:PAD * (q + 1), r * CI:(r + 1) * CI], v_pad[:, j, g, :],
                                      mixed[:, j, g, :], start=(j == 0), stop=(j == TW - 1))
                last.then_inc(filled["V"], 1)

            def project(step, t):
                pe.wait_ge(emptied["V"], now.fill(("values", 2 * t + 1), "V"))
                if now.was_filled(step, "M"):
                    pe.wait_ge(emptied["M"], now.fill(step, "M") - 1)
                for r in range(GH // GR):
                    last = mm(bank["M"][:, 0:D], oT[:, r, :], w_out[:, r, :], start=(r == 0), stop=(r == GH // GR - 1))
                last.then_inc(filled["M"], 1)

            def qkv(step, l, t):
                for c in range(KC):
                    pe.wait_ge(emptied[f"F{c}"], now.x_turned(l, f"F{c}"))
                pe.wait_ge(qkv_loaded, now.at(qkv_loaded, 16 * (l + 1)))
                for j in range(3):
                    k = f"F{j}"
                    if now.was_filled(step, k):
                        pe.wait_ge(emptied[k], now.fill(step, k) - 1)
                    for c in range(KC):
                        at = 1 - c + t * P
                        last = mm(bank[k][:], xT[:, c, at:at + P], w_qkv[:, c, j * INNER:(j + 1) * INNER],
                                  start=(c == 0), stop=(c == KC - 1))
                    last.then_inc(filled[k], 1)

            def qk_turn(step, l, t, j):
                pe.wait_ge(qk_ready, now.at(qk_ready, 2 * (TW * l + t) + j + 1))
                if now.was_filled(step, "F3"):
                    pe.wait_ge(emptied["F3"], now.fill(step, "F3") - 1)
                for c in range(4):
                    last = turn(bank["F3"][:, c * P:(c + 1) * P], qk_tok[:, j, c * P:(c + 1) * P], ident[:])
                last.then_inc(filled["F3"], 1)

            def local_scores(step, l, u):
                t, quad = u // QUADS, u % QUADS
                pe.wait_ge(emptied["F3"], now.fill(("k_turn", l, TW - 1), "F3"))
                for parity in range(2):
                    k = f"F{parity}"
                    if now.was_filled(step, k):
                        pe.wait_ge(emptied[k], now.fill(step, k) - 1)
                    mm(bank[k][:], ident_bf[:], mask_bf[:].rearrange("p a j -> p (a j)"), start=True, stop=False,
                       skip_group_check=True)
                    for pair in range(2):
                        hp = 2 * quad + pair
                        lo = P if t == 0 else 0
                        rows = slice(HD * parity, HD * (parity + 1))
                        last = mm(bank[k][:, pair * 2 * P + lo:(pair + 1) * 2 * P],
                                  qT[rows, hp, t * P:(t + 1) * P],
                                  kT[rows, hp, (t - 1) * P + lo:(t + 1) * P],
                                  start=False, stop=(pair == 1), skip_group_check=True)
                    last.then_inc(filled[k], 1)

            def p_turn(step, l, u):
                for parity in range(2):
                    pe.wait_ge(emptied[f"F{parity}"], now.fill(("local_scores", l, u), f"F{parity}"))
                lo = 1 if u // QUADS == 0 else 0
                for pair in range(2):
                    k = f"F{2 + pair}"
                    if now.was_filled(step, k):
                        pe.wait_ge(emptied[k], now.fill(step, k) - 1)
                    for parity in range(2):
                        for j in range(lo, 2):
                            last = turn(bank[k][:, (2 * parity + j) * P:(2 * parity + j + 1) * P],
                                        l_probs[:, u % 2, 2 * parity + pair, j * P:(j + 1) * P], ident[:])
                    last.then_inc(filled[k], 1)

            def local_values(step, l, u):
                t, quad = u // QUADS, u % QUADS
                for pair in range(2):
                    pe.wait_ge(emptied[f"F{2 + pair}"], now.fill(("p_turn", l, u), f"F{2 + pair}"))
                if now.was_filled(step, "V"):
                    pe.wait_ge(emptied["V"], now.fill(step, "V") - 1)
                lo = 1 if t == 0 else 0
                for pair in range(2):
                    for parity in range(2):
                        h = 4 * quad + 2 * pair + parity
                        for j in range(lo, 2):
                            last = mm(bank["V"][:, (2 * pair + parity) * HD:(2 * pair + parity + 1) * HD],
                                      pT[:, pair, 2 * parity + j, :], v_loc[:, t - 1 + j, h * HD:(h + 1) * HD],
                                      start=(j == lo), stop=(j == 1))
                last.then_inc(filled["V"], 1)

            def o_turn(step, l, t):
                pe.wait_ge(emptied["V"], now.fill(("local_values", l, QUADS * t + QUADS - 1), "V"))
                if now.was_filled(step, "F2"):
                    pe.wait_ge(emptied["F2"], now.fill(step, "F2") - 1)
                flat = o_tok[:].rearrange("p h d -> p (h d)")
                for c in range(4):
                    last = turn(bank["F2"][:, c * P:(c + 1) * P], flat[:, c * P:(c + 1) * P], ident[:])
                last.then_inc(filled["F2"], 1)

            def out_proj(step, l, t):
                pe.wait_ge(emptied["F2"], now.fill(("o_turn", l, t), "F2"))
                if now.was_filled(step, "F3"):
                    pe.wait_ge(emptied["F3"], now.fill(step, "F3") - 1)
                for c in range(4):
                    last = mm(bank["F3"][:, 0:D], o_locT[:, c, :], w_o[l][:, c, :], start=(c == 0), stop=(c == 3))
                last.then_inc(filled["F3"], 1)

            def half_turn(step, l):
                pe.wait_ge(emptied["F3"], now.fill(("out_proj", l, TW - 1), "F3"))
                if now.was_filled(step, "F0"):
                    pe.wait_ge(emptied["F0"], now.fill(step, "F0") - 1)
                for t in range(TW):
                    last = turn(bank["F0"][:, t * P:(t + 1) * P], x_mid[:, t, P:D], ident[:])
                last.then_inc(filled["F0"], 1)

            def shift_turn(step, l):
                pe.wait_ge(emptied["F0"], now.fill(("half_turn", l), "F0"))
                if now.was_filled(step, "F1"):
                    pe.wait_ge(emptied["F1"], now.fill(step, "F1") - 1)
                for t in range(TW):
                    last = turn(bank["F1"][:, t * P:(t + 1) * P], midT[:, t * P:(t + 1) * P], ident[:])
                last.then_inc(filled["F1"], 1)

            def h_turn(step, l):
                pe.wait_ge(h_ready, now.at(h_ready, TW * (l + 1)))
                pe.wait_ge(emptied["F1"], now.fill(("shift_turn", l), "F1"))
                for c in range(KC):
                    k = f"F{2 + c}"
                    if now.was_filled(step, k):
                        pe.wait_ge(emptied[k], now.fill(step, k) - 1)
                    for t in range(TW):
                        last = turn(bank[k][:, t * P:(t + 1) * P], h_tok[:, t, c * P:(c + 1) * P], ident[:])
                    last.then_inc(filled[k], 1)

            def up(step, l, i):
                for c in range(KC):
                    pe.wait_ge(emptied[f"F{2 + c}"], now.fill(("h_turn", l), f"F{2 + c}"))
                pe.wait_ge(w_1_loaded, now.at(w_1_loaded, 16 * (l + 1)))
                m = hidden_rows(i)
                for j, k in enumerate(banks_of(step)):
                    if now.was_filled(step, k):
                        pe.wait_ge(emptied[k], now.fill(step, k) - 1)
                    for c in range(KC):
                        at = j * HID + i * P
                        last = mm(bank[k][0:m, :], w_1[:, c, at:at + m], hT[:, c, :], start=(c == 0), stop=(c == KC - 1))
                    last.then_inc(filled[k], 1)

            def down(step, l, t):
                pe.wait_ge(emptied[banks_of(("up", l, HC - 1))[0]], now.fill(("up", l, HC - 1), banks_of(("up", l, HC - 1))[0]))
                k = f"F{t}"
                if now.was_filled(step, k):
                    pe.wait_ge(emptied[k], now.fill(step, k) - 1)
                for i in range(HC):
                    m = hidden_rows(i)
                    last = mm(bank[k][:, 0:D], hidden[0:m, i, t * P:(t + 1) * P], w_2[l][0:m, i, :],
                              start=(i == 0), stop=(i == HC - 1))
                last.then_inc(filled[k], 1)

            steps = {
                "x_turn": x_turn, "talk_qk": talk_qk, "talk_v": talk_v, "scores": scores, "mix": mix,
                "values": values, "project": project, "qkv": qkv,
                "q_turn": lambda step, l, t: qk_turn(step, l, t, 0),
                "k_turn": lambda step, l, t: qk_turn(step, l, t, 1),
                "local_scores": local_scores, "p_turn": p_turn, "local_values": local_values,
                "o_turn": o_turn, "out_proj": out_proj, "half_turn": half_turn, "shift_turn": shift_turn,
                "h_turn": h_turn, "up": up, "down": down,
            }

            now.run(pe, steps)

        @block.scalar
        def _(act):
            now = Counts()
            fn = nc.scalar.activation
            act.wait_ge(loads, LOADED)

            def x_turn(step, l):
                if not now.ahead:
                    act.wait_ge(filled["F2"], now.fill(("qkv", (l - 1) % LAYERS, TW - 1), "F2"))
                    act.wait_ge(filled["S1"], now.fill(("talk_v",), "S1"))
                for c in range(KC):
                    k = f"F{c}"
                    act.wait_ge(filled[k], now.fill(step, k))
                    fn(xT[:, c, 1:N + 1], bank[k][:], ACT.Copy).then_inc(emptied[k], 1)

            def talk_qk(step):
                if not now.first:
                    act.wait_ge(filled["V"], now.fill(("values", CHUNKS - 1), "V", ago=1))
                for j, k in enumerate(["S0", "S1", "M", "V"]):
                    act.wait_ge(filled[k], now.fill(step, k))
                    fn(raw_qk[:, j, :], bank[k][:], ACT.Identity, bias=b_qk[:, j:j + 1]).then_inc(emptied[k], 1)

            def scores(step, n):
                k = f"S{n % 2}"
                act.wait_ge(max_done, now.at(max_done, n + 1))
                if n >= PB:
                    act.wait_ge(filled["M"], now.fill(("mix", n - PB), "M"))
                elif not now.first:
                    act.wait_ge(filled["M"], now.fill(("mix", TILES - 1), "M", ago=1))
                fn(probs[:, n % PB, :], bank[k][:], ACT.Exp, bias=neg_max[:, n % 2:n % 2 + 1],
                   accum_out=row_sum[:, n % PB:n % PB + 1]).then_inc(emptied[k], 1)

            def mix(step, n):
                if n % 2:
                    return
                act.wait_ge(filled["M"], now.fill(step, "M"))
                store_mixed(act, nc.scalar.copy, now, n)

            def values(step, c):
                act.wait_ge(filled["V"], now.fill(step, "V"))
                if c % 2 == 0:
                    if now.past(not (c < 2)):
                        act.wait_ge(filled["M"], now.fill(("project", (c // 2 - 1) % TW), "M", ago=c < 2))
                at = (c % 2) * CI
                fn(oT[:, :, at:at + CI], bank["V"][:, 0:GR * CI].rearrange("p (r i) -> p r i", r=GR), ACT.Copy)\
                    .then_inc(emptied["V"], 1)

            def qkv(step, l, t):
                w = TW * l + t
                for j in range(2):
                    if now.past(2 * (w - 1) + j + 1):
                        act.wait_ge(norm_done, now.at(norm_done, 2 * (w - 1) + j + 1))
                    act.wait_ge(rot_done, now.at(rot_done, 2 * w + j + 1))
                    fn(sq[:, j, :], bank[f"F{j}"][:], ACT.Square).then_inc(emptied[f"F{j}"], 1)
                if t == 0:
                    if now.past(not (not l)):
                        act.wait_ge(filled["V"], now.fill(("local_values", (l - 1) % LAYERS, TW * QUADS - 1), "V", ago=not l))
                act.wait_ge(filled["F2"], now.fill(step, "F2"))
                fn(v_loc[:, t, :], bank["F2"][:], ACT.Copy).then_inc(emptied["F2"], 1)

            def q_turn(step, l, t):
                if t == 0:
                    if now.past(not (not l)):
                        act.wait_ge(filled["F3"], now.fill(("down", (l - 1) % LAYERS, TW - 1), "F3", ago=not l))
                act.wait_ge(filled["F3"], now.fill(step, "F3"))
                fn(qT[:, :, t * P:(t + 1) * P], bank["F3"][:].rearrange("p (c i) -> p c i", c=4), ACT.Copy)\
                    .then_inc(emptied["F3"], 1)

            def local_scores(step, l, u):
                n = TW * QUADS * l + u
                lo = P if u // QUADS == 0 else 0
                act.wait_ge(l_max_done, now.at(l_max_done, n + 1))
                if now.past(not (n < 2)):
                    act.wait_ge(filled["F3"], now.fill(("p_turn", *unit_before(l, u, 2)), "F3", ago=n < 2))
                if now.past(n - 1):
                    act.wait_ge(l_inv_done, now.at(l_inv_done, n - 1))
                for parity in range(2):
                    for pair in range(2):
                        j = 2 * parity + pair
                        ins = fn(l_probs[:, u % 2, j, lo:], bank[f"F{parity}"][:, pair * 2 * P + lo:(pair + 1) * 2 * P],
                                 ACT.Exp, bias=l_max[:, u % 2, j:j + 1], accum_out=l_sum[:, u % 2, j:j + 1])
                    ins.then_inc(emptied[f"F{parity}"], 1)

            def p_turn(step, l, u):
                act.wait_ge(filled["F3"], now.fill(step, "F3"))
                if now.past(not (not l and not u)):
                    act.wait_ge(filled["V"], now.fill(("local_values", *unit_before(l, u, 1)), "V", ago=not l and not u))
                lo = 1 if u // QUADS == 0 else 0
                fn(pT[:, 1, :, :].rearrange("p (a j) i -> p a j i", a=2)[:, :, lo:, :],
                   bank["F3"][:].rearrange("p (a j i) -> p a j i", a=2, j=2)[:, :, lo:, :], ACT.Copy)\
                    .then_inc(emptied["F3"], 1)

            def o_turn(step, l, t):
                act.wait_ge(filled["F2"], now.fill(step, "F2"))
                if now.past(not (not l and not t)):
                    act.wait_ge(filled["F3"], now.fill(("out_proj", *window_before(l, t)), "F3", ago=not l and not t))
                fn(o_locT[:], bank["F2"][:].rearrange("p (c i) -> p c i", c=4), ACT.Copy).then_inc(emptied["F2"], 1)

            def half_turn(step, l):
                act.wait_ge(filled["F0"], now.fill(step, "F0"))
                if now.past(not (not l)):
                    act.wait_ge(filled["F1"], now.fill(("shift_turn", (l - 1) % LAYERS), "F1", ago=not l))
                fn(midT[:, 1:N + 1], bank["F0"][:], ACT.Copy).then_inc(emptied["F0"], 1)

            def h_turn(step, l):
                act.wait_ge(rot_added, now.at(rot_added, 2 * TW * (l + 1)))
                for c in range(KC):
                    k = f"F{2 + c}"
                    act.wait_ge(filled[k], now.fill(step, k))
                    fn(hT[:, c, :], bank[k][:], ACT.Identity, bias=ln_w[l][:, KC + c:KC + c + 1],
                       scale=ln_w[l][:, c:c + 1]).then_inc(emptied[k], 1)

            def up(step, l, i):
                k = banks_of(step)[1]
                m = hidden_rows(i)
                act.wait_ge(filled[k], now.fill(step, k))
                if i >= 2:
                    act.wait_ge(emptied[banks_of(("up", l, i - 2))[0]], now.fill(("up", l, i - 2), banks_of(("up", l, i - 2))[0]))
                else:
                    act.wait_ge(filled["F3"], now.fill(("k_turn", l, TW - 1), "F3"))
                fn(gelu[0:m, i % 2, :], bank[k][0:m, :], ACT.Gelu, bias=b_1[l][0:m, HC + i:HC + i + 1])\
                    .then_inc(emptied[k], 1)

            def gated(step):
                act.wait_ge(bounded, now.at(bounded, 0))
                fn(o_fin[:], o_fin[:], ACT.Exp, scale=-1.0).then_inc(exp_done, 1)

            steps = {
                "x_turn": x_turn, "talk_qk": talk_qk, "scores": scores, "mix": mix, "values": values, "qkv": qkv,
                "q_turn": q_turn, "local_scores": local_scores, "p_turn": p_turn, "o_turn": o_turn,
                "half_turn": half_turn, "h_turn": h_turn, "up": up, "gated": gated,
            }

            now.run(act, steps)

        @block.vector
        def _(dve):
            now = Counts()
            v = nc.vector
            v.memset(xT[:, :, 0:1], 0.0).then_inc(pads, 1)
            v.memset(midT[:, 0:1], 0.0).then_inc(pads, 1)
            v.memset(v_pad[:], 0.0).then_inc(pads, 1)
            v.memset(minus_half[:], -0.5).then_inc(pads, 1)
            v.memset(eps[:], 1e-5).then_inc(pads, 1)
            dve.wait_ge(pads, 5)
            dve.wait_ge(loads, LOADED)
            v.tensor_copy(mask_bf[:].rearrange("p a j -> p (a j)"), mask).then_inc(tables, 1)
            v.tensor_copy(ident_bf[:], ident[:]).then_inc(tables, 1)
            v.tensor_scalar(w_pre[:], w_pre[:], float(GD) ** -0.5, None, ALU.mult).then_inc(tables, 1)
            v.tensor_tensor(mixer[:], w_post[:, :, None].to_broadcast([P, GH, RI]),
                            delta[:, None, :].to_broadcast([P, GH, RI]), ALU.mult).then_inc(tables, 1)
            for l in range(LAYERS):
                for j in range(4):
                    v.tensor_tensor(rot[l][:, j], xpos[:, j], scales[l][:, j, None, :].to_broadcast([P, TW, HD]),
                                    ALU.mult).then_inc(tables, 1)
            dve.wait_ge(tables, TABLES)

            def norm(step):
                dve.wait_ge(x_loaded, now.at(x_loaded, 16))
                if not now.ahead:
                    dve.wait_ge(aggr_done, now.at(aggr_done, LAYERS))
                for t in range(TW):
                    v.bn_stats(stats[:, t, 0, :], x_in[:, t, :]).then_inc(stats_done, 1)
                if not now.ahead:
                    dve.wait_ge(emptied["F1"], now.fill(("shift_turn", LAYERS - 1), "F1"))
                    dve.wait_ge(h_ready, now.at(h_ready, LAYERS * TW))
                dve.wait_ge(stats_done, now.at(stats_done, LAYERS * 2 * TW + TW))
                v.memset(opener[:], 0.0)
                for t in range(TW):
                    ins = v.bn_aggr(mean_var[:, t, :], stats[:, t, 0, :])
                ins.then_inc(aggr_done, 1)

            def scale(step):
                dve.wait_ge(rstd_done, now.at(rstd_done, LAYERS + 1))
                for t in range(TW):
                    v.tensor_scalar(x_in[:, t, :], x_in[:, t, :], mean_var[:, t, 0:1], rstd[:, t:t + 1],
                                    ALU.subtract, ALU.mult).then_inc(x_ready, 1)

            def talk_qk(step):
                dve.wait_ge(emptied["V"], now.at(emptied["V"], filling[step, "V"]))
                if not now.first:
                    dve.wait_ge(filled["S1"], now.fill(("scores", TILES - 1), "S1", ago=1))
                v.tensor_tensor(k_rope[:], raw_qk[:, 2:4, :], rope_cos[:, None, :].to_broadcast([P, 2, N]),
                                ALU.mult).then_inc(k_parts, 1)
                v.tensor_tensor(t_k, raw_qk[:, 2:4, :][:, ::-1, :], rope_sin[:, None, :].to_broadcast([P, 2, N]),
                                ALU.mult).then_inc(k_parts, 1)
                dve.wait_ge(k_parts, now.at(k_parts, 2))
                v.tensor_tensor(k_rope[:, 0], k_rope[:, 0], t_k[:, 0], ALU.subtract)
                v.tensor_tensor(k_rope[:, 1], k_rope[:, 1], t_k[:, 1], ALU.add).then_inc(k_roped, 1)

            def talk_v(step):
                if not now.first:
                    dve.wait_ge(filled["V"], now.fill(("values", CHUNKS - 1), "V", ago=1))
                for t in range(TW):
                    k = f"S{t // 2}"
                    if t % 2 == 0:
                        dve.wait_ge(filled[k], now.fill(step, k))
                    ins = v.tensor_tensor(v_pad[:, t, :, 0:GD],
                                          bank[k][:, (t % 2) * D:(t % 2 + 1) * D].rearrange("p (g d) -> p g d", d=GD),
                                          b_v[:].rearrange("p (g d) -> p g d", d=GD), ALU.add)
                    if t % 2:
                        ins.then_inc(emptied[k], 1)

            def mixers(n):
                k = f"S{n % 2}"
                dve.wait_ge(emptied[k], now.fill(("scores", n), k))
                if now.past(n - 1):
                    dve.wait_ge(mixer_done, now.at(mixer_done, n - 1))
                v.reciprocal(row_inv[:, n % 2:n % 2 + 1], row_sum[:, n % PB:n % PB + 1]).then_inc(inv_done, 1)
                if now.past(not (n < 2)):
                    dve.wait_ge(filled["M"], now.fill(("mix", (n - 2) % TILES), "M", ago=n < 2))
                dve.wait_ge(inv_done, now.at(inv_done, n + 1))
                v.tensor_scalar(mixer_n[:, n % 2, :], mixer[:].rearrange("p g i -> p (g i)"),
                                row_inv[:, n % 2:n % 2 + 1], None, ALU.mult).then_inc(mixer_done, 1)

            def scores(step, n):
                k = f"S{n % 2}"
                dve.wait_ge(filled[k], now.fill(step, k))
                if now.past(not (n < 2)):
                    dve.wait_ge(emptied[k], now.fill(("scores", (n - 2) % TILES), k, ago=n < 2))
                v.tensor_reduce(neg_max[:, n % 2:n % 2 + 1], bank[k][:], AX.X, ALU.max, negate=True)\
                    .then_inc(max_done, 1)
                if n:
                    mixers(n - 1)

            def mix(step, n):
                if n == TILES - LAG:
                    mixers(TILES - 1)
                if n % 2:
                    dve.wait_ge(filled["M"], now.fill(step, "M"))
                    store_mixed(dve, v.tensor_copy, now, n)

            def project(step, t):
                dve.wait_ge(filled["M"], now.fill(step, "M"))
                if t == 0:
                    if now.past(0):
                        dve.wait_ge(gated_done, now.at(gated_done, 0))
                v.tensor_tensor(s_tok[:, t, :], bank["M"][:, 0:D], b_out[:], ALU.add).then_inc(emptied["M"], 1)

            def qkv(step, l, t):
                w = TW * l + t
                if now.past(2 * w):
                    dve.wait_ge(rot_added, now.at(rot_added, 2 * w))
                for j in range(2):
                    dve.wait_ge(filled[f"F{j}"], now.fill(step, f"F{j}"))
                    src = bank[f"F{j}"][:].rearrange("p (h s d) -> p h s d", h=H, s=2)
                    for k, (dst, x) in enumerate([(rot_a, src), (rot_b, src[:, :, ::-1, :])]):
                        tab = rot[l][:, 2 * j + k, t, :].rearrange("p (s d) -> p s d", s=2)
                        ins = v.tensor_tensor(dst[:, j, :].rearrange("p (h s d) -> p h s d", h=H, s=2), x,
                                              tab[:, None, :, :].to_broadcast([P, H, 2, HD // 2]), ALU.mult)
                    ins.then_inc(rot_done, 1)
                if now.past(w):
                    dve.wait_ge(clip_done, now.at(clip_done, w))
                for j in range(2):
                    dve.wait_ge(emptied[f"F{j}"], now.fill(step, f"F{j}"))
                    v.tensor_reduce(norms[:, j * H:(j + 1) * H], sq[:, j, :].rearrange("p (h d) -> p h d", h=H),
                                    AX.X, ALU.add).then_inc(norm_done, 1)
                dve.wait_ge(norm_done, now.at(norm_done, 2 * w + 2))
                if now.past(w):
                    dve.wait_ge(inv_norm_done, now.at(inv_norm_done, w))
                v.tensor_scalar(norms_c[:], norms[:], 1e-24, None, ALU.max).then_inc(clip_done, 1)

            def k_turn(step, l, t):
                if t == 0:
                    if now.past(not (not l)):
                        dve.wait_ge(filled["F3"], now.fill(("down", (l - 1) % LAYERS, TW - 1), "F3", ago=not l))
                dve.wait_ge(filled["F3"], now.fill(step, "F3"))
                v.tensor_copy(kT[:, :, t * P:(t + 1) * P], bank["F3"][:].rearrange("p (c i) -> p c i", c=4))\
                    .then_inc(emptied["F3"], 1)

            def local_scores(step, l, u):
                n = TW * QUADS * l + u
                lo = P if u // QUADS == 0 else 0
                if now.past(not (n < 2)):
                    dve.wait_ge(emptied["F1"], now.fill(("local_scores", *unit_before(l, u, 2)), "F1", ago=n < 2))
                for parity in range(2):
                    k = f"F{parity}"
                    dve.wait_ge(filled[k], now.fill(step, k))
                    ins = v.tensor_reduce(l_max[:, u % 2, 2 * parity:2 * parity + 2],
                                          bank[k][:].rearrange("p (a j) -> p a j", a=2)[:, :, lo:], AX.X, ALU.max,
                                          negate=True)
                ins.then_inc(l_max_done, 1)

            def p_turn(step, l, u):
                n = TW * QUADS * l + u
                lo = 1 if u // QUADS == 0 else 0
                if now.past(not (not l and not u)):
                    dve.wait_ge(filled["V"], now.fill(("local_values", *unit_before(l, u, 1)), "V", ago=not l and not u))
                dve.wait_ge(filled["F2"], now.fill(step, "F2"))
                v.tensor_copy(pT[:, 0, :, :].rearrange("p (a j) i -> p a j i", a=2)[:, :, lo:, :],
                              bank["F2"][:].rearrange("p (a j i) -> p a j i", a=2, j=2)[:, :, lo:, :])\
                    .then_inc(emptied["F2"], 1)
                dve.wait_ge(emptied["F1"], now.fill(("local_scores", l, u), "F1"))
                if now.past(not (n < 2)):
                    dve.wait_ge(emptied["V"], now.fill(("local_values", *unit_before(l, u, 2)), "V", ago=n < 2))
                v.reciprocal(l_inv[:, u % 2, :], l_sum[:, u % 2, :]).then_inc(l_inv_done, 1)

            def local_values(step, l, u):
                t, quad = u // QUADS, u % QUADS
                dve.wait_ge(filled["V"], now.fill(step, "V"))
                dve.wait_ge(l_inv_done, now.at(l_inv_done, TW * QUADS * l + u + 1))
                if quad == 0:
                    if now.past(not (not l and not t)):
                        dve.wait_ge(filled["F2"], now.fill(("o_turn", *window_before(l, t)), "F2", ago=not l and not t))
                v.tensor_tensor(
                    o_tok[:, 4 * quad:4 * quad + 4, :].rearrange("p (a b) d -> p a b d", a=2),
                    bank["V"][:, 0:4 * HD].rearrange("p (a b d) -> p a b d", a=2, b=2),
                    l_inv[:, u % 2, :].rearrange("p (b a) -> p a b", b=2)[:, :, :, None].to_broadcast([P, 2, 2, HD]),
                    ALU.mult).then_inc(emptied["V"], 1)

            def out_proj(step, l, t):
                dve.wait_ge(filled["F3"], now.fill(step, "F3"))
                if not l and not t and not now.first:
                    dve.wait_ge(gated_done, now.at(gated_done, 0))
                if t == 0:
                    if now.past(l):
                        dve.wait_ge(mid_b_ready, now.at(mid_b_ready, l))
                    if now.past(TW * l):
                        dve.wait_ge(h_ready, now.at(h_ready, TW * l))
                x = x_tok if l else x_in
                v.tensor_tensor(x_mid[:, t, :], bank["F3"][:, 0:D], x[:, t, :], ALU.add)\
                    .then_inc(emptied["F3"], 1)

            def shift_turn(step, l):
                dve.wait_ge(filled["F1"], now.fill(step, "F1"))
                dve.wait_ge(emptied["F3"], now.fill(("out_proj", l, TW - 1), "F3"))
                dve.wait_ge(aggr_done, now.at(aggr_done, l))
                for t in range(TW):
                    v.bn_stats(stats[:, t, 0, :], x_mid[:, t, 0:P]).then_inc(stats_done, 1)
                    v.bn_stats(stats[:, t, 1, :], bank["F1"][:, t * P:(t + 1) * P]).then_inc(stats_done, 1)
                dve.wait_ge(stats_done, now.at(stats_done, 2 * TW * (l + 1)))
                dve.wait_ge(eps_done, now.at(eps_done, l))
                v.memset(opener[:], 0.0)
                for t in range(TW):
                    ins = v.bn_aggr(mean_var[:, t, :], stats[:, t, :, :].rearrange("p a s -> p (a s)"))
                ins.then_inc(aggr_done, 1)

            def h_scale(step, l):
                dve.wait_ge(rstd_done, now.at(rstd_done, 1 + l))
                dve.wait_ge(rot_added, now.at(rot_added, 2 * TW * (l + 1)))
                dve.wait_ge(qk_ready, now.at(qk_ready, 2 * TW * (l + 1)))
                for t in range(TW):
                    v.tensor_scalar(h_tok[:, t, 0:P], x_mid[:, t, 0:P], mean_var[:, t, 0:1], rstd[:, t:t + 1],
                                    ALU.subtract, ALU.mult).then_inc(h_ready, 1)
                for t in range(TW):
                    ins = v.tensor_scalar(h_tok[:, t, P:D], bank["F1"][:, t * P:(t + 1) * P], mean_var[:, t, 0:1],
                                          rstd[:, t:t + 1], ALU.subtract, ALU.mult)
                ins.then_inc(emptied["F1"], 1)

            def up(step, l, i):
                ka, kg = banks_of(step)
                m = hidden_rows(i)
                dve.wait_ge(filled[ka], now.fill(step, ka))
                dve.wait_ge(emptied[kg], now.fill(step, kg))
                v.scalar_tensor_tensor(hidden[0:m, i, :], bank[ka][0:m, :], b_1[l][0:m, i:i + 1], gelu[0:m, i % 2, :],
                                       op0=ALU.add, op1=ALU.mult).then_inc(emptied[ka], 1)

            def down(step, l, t):
                k = f"F{t}"
                dve.wait_ge(filled[k], now.fill(step, k))
                dve.wait_ge(mid_b_ready, now.at(mid_b_ready, l + 1))
                if not l and not t and not now.first:
                    dve.wait_ge(silu_done, now.at(silu_done, 0))
                v.tensor_tensor(x_tok[:, t, :], bank[k][:, 0:D], x_mid_b[:, t, :], ALU.add)\
                    .then_inc(emptied[k], 1)

            def gated(step):
                stream_ready(dve, now, LAYERS, ago=1)
                dve.wait_ge(stored, now.at(stored, -16))
                v.tensor_scalar(o_fin[:], x_tok[:], LEAST, None, ALU.max).then_inc(bounded, 1)
                dve.wait_ge(exp_done, now.at(exp_done, 0))
                v.tensor_scalar(o_fin[:], o_fin[:], 1.0, None, ALU.add).then_inc(one_plus, 1)
                dve.wait_ge(one_plus, now.at(one_plus, 0))
                v.reciprocal(x_mid[:], o_fin[:]).then_inc(sig_done, 1)

            steps = {
                "norm": norm, "scale": scale, "talk_qk": talk_qk, "talk_v": talk_v, "scores": scores, "mix": mix,
                "project": project, "h_scale": h_scale,
                "qkv": qkv, "k_turn": k_turn, "local_scores": local_scores, "p_turn": p_turn,
                "local_values": local_values, "out_proj": out_proj, "shift_turn": shift_turn, "up": up, "down": down,
                "gated": gated,
            }

            now.run(dve, steps)

        @block.gpsimd
        def _(pool):
            now = Counts()
            g = nc.gpsimd
            pool.dma_start(x_in[:], a["x"][0]).then_inc(x_loaded, 16)
            pool.wait_ge(pads, 5)
            pool.wait_ge(loads, LOADED)
            pool.wait_ge(tables, TABLES)

            def inverse_std(n):
                pool.wait_ge(aggr_done, now.at(aggr_done, n))
                g.tensor_tensor(var_eps[:], mean_var[:, :, 1], eps[:], ALU.add).then_inc(eps_done, 1)
                pool.wait_ge(eps_done, now.at(eps_done, n))
                if n == LAYERS + 1:
                    if not now.ahead:
                        pool.wait_ge(emptied["F1"], now.fill(("shift_turn", LAYERS - 1), "F1"))
                elif n == 1:
                    pool.wait_ge(x_ready, now.at(x_ready, 0))
                else:
                    pool.wait_ge(emptied["F1"], now.fill(("shift_turn", n - 2), "F1"))
                g.tensor_tensor(rstd[:], var_eps[:], minus_half[:, 0:TW], ALU.pow).then_inc(rstd_done, 1)

            def norm(step):
                inverse_std(LAYERS + 1)

            def talk_qk(step):
                pool.wait_ge(emptied["S1"], now.fill(step, "S1"))
                if now.past(0):
                    pool.wait_ge(q_mixed, now.at(q_mixed, 0))
                g.tensor_tensor(q_rope[:], raw_qk[:, 0:2, :], rope_cos[:, None, :].to_broadcast([P, 2, N]),
                                ALU.mult).then_inc(q_parts, 1)
                for s in range(2):
                    ins = g.tensor_tensor(t_q[:, s, :], raw_qk[:, 1 - s, :], rope_sin[:], ALU.mult)
                ins.then_inc(q_parts, 1)
                pool.wait_ge(q_parts, now.at(q_parts, 2))
                g.tensor_tensor(q_rope[:, 0], q_rope[:, 0], t_q[:, 0], ALU.subtract)
                g.tensor_tensor(q_rope[:, 1], q_rope[:, 1], t_q[:, 1], ALU.add).then_inc(q_roped, 1)

            def expand(step, c):
                pool.wait_ge(q_roped, now.at(q_roped, 1))
                n = (c - 2) * ET + ET - 1
                if now.past(not (n < 0)):
                    pool.wait_ge(filled[f"S{n % 2}"], now.fill(("scores", n % TILES), f"S{n % 2}", ago=n < 0))
                shape = [P, ET, GH, RI]
                for s in range(2):
                    q = q_rope[:, s, c * ET * RI:(c + 1) * ET * RI].rearrange("p (m i) -> p m i", m=ET)
                    g.tensor_tensor(q_mix[:, c % 2, s].rearrange("p m (g i) -> p m g i", g=GH),
                                    q[:, :, None, :].to_broadcast(shape),
                                    w_pre[:, None, :, None].to_broadcast(shape), ALU.mult).then_inc(q_mixed, 1)

            def qkv(step, l, t):
                w = TW * l + t
                if now.past(not (not w)):
                    pool.wait_ge(filled["F3"], now.fill(("k_turn", *window_before(l, t)), "F3", ago=not w))
                if not t:
                    c = ("up", (l - 1) % LAYERS, HC - 1)
                    if now.past(not (not l)):
                        pool.wait_ge(emptied[banks_of(c)[0]], now.fill(c, banks_of(c)[0], ago=not l))
                for j in range(2):
                    pool.wait_ge(rot_done, now.at(rot_done, 2 * w + j + 1))
                    g.tensor_tensor(qk_tok[:, j, :], rot_a[:, j, :], rot_b[:, j, :], ALU.add).then_inc(rot_added, 1)
                pool.wait_ge(clip_done, now.at(clip_done, w + 1))
                if now.past(2 * w):
                    pool.wait_ge(qk_ready, now.at(qk_ready, 2 * w))
                g.tensor_tensor(inv_norms[:], norms_c[:], minus_half[:], ALU.pow).then_inc(inv_norm_done, 1)
                pool.wait_ge(inv_norm_done, now.at(inv_norm_done, w + 1))
                pool.wait_ge(rot_added, now.at(rot_added, 2 * w + 2))
                for j in range(2):
                    g.tensor_tensor(qk_tok[:, j, :].rearrange("p (h d) -> p h d", h=H),
                                    qk_tok[:, j, :].rearrange("p (h d) -> p h d", h=H),
                                    inv_norms[:, j * H:(j + 1) * H, None].to_broadcast([P, H, HD]), ALU.mult)\
                        .then_inc(qk_ready, 1)

            def half_turn(step, l):
                pool.wait_ge(emptied["F3"], now.fill(("out_proj", l, TW - 1), "F3"))
                g.tensor_tensor(x_mid_b, x_mid[:], b_2[l][:, None, :].to_broadcast([P, TW, D]), ALU.add)\
                    .then_inc(mid_b_ready, 1)
                if not l:
                    pool.dma_start(x_in[:], a["x_next"][bass.ds(now.b + 1, 1)].rearrange("a p t f -> (a p) t f"))\
                        .then_inc(x_loaded, 16)

            def shift_turn(step, l):
                inverse_std(1 + l)

            def gated(step):
                pool.wait_ge(sig_done, now.at(sig_done, 0))
                pool.wait_ge(emptied["M"], now.fill(("project", TW - 1), "M", ago=1))
                g.tensor_tensor(x_mid[:], x_mid[:], x_tok[:], ALU.mult).then_inc(silu_done, 1)
                pool.wait_ge(silu_done, now.at(silu_done, 0))
                g.tensor_tensor(s_tok[:], s_tok[:], x_mid[:], ALU.mult).then_inc(gated_done, 1)
                pool.wait_ge(gated_done, now.at(gated_done, 0))
                pool.wait_ge(keep_loaded, now.at(keep_loaded, 0))
                g.tensor_tensor(o_fin[:], s_tok[:], x_keep[:], ALU.add).then_inc(o_ready, 1)
                pool.wait_ge(o_ready, now.at(o_ready, 0))
                pool.dma_start(out[bass.ds(now.b - 1, 1)].rearrange("a (t p) f -> (a p) t f", p=P), o_fin[:])\
                    .then_inc(stored, 16)

            def keep(step):
                pool.dma_start(x_keep[:], a["x_next"][bass.ds(now.b, 1)].rearrange("a p t f -> (a p) t f"))\
                    .then_inc(keep_loaded, 16)

            steps = {
                "norm": norm, "talk_qk": talk_qk, "expand": expand, "qkv": qkv, "half_turn": half_turn,
                "shift_turn": shift_turn, "gated": gated, "keep": keep,
            }

            now.run(pool, steps)


def shape_constants():
    f = np.float32
    c = {"ident": np.eye(P, dtype=f)}
    i, j = np.arange(P)[:, None], np.arange(P)[None, :]
    prev, cur = np.where(i > j, MASKED, 0.0), np.where(i < j, MASKED, 0.0)
    c["mask"] = np.tile(np.concatenate([prev, cur], 1), (1, 2)).astype(f)
    c["delta"] = (np.arange(P)[:, None] % RI == np.arange(RI)[None, :]).astype(f)
    inv = f(1.0) / f(10000.0) ** (np.arange(0, GD, 2, dtype=f) / f(GD))
    fr = (np.arange(N, dtype=f)[:, None] * inv[None, :]).astype(f)
    cos, sin = np.tile(np.cos(fr).T, (GH, 1)), np.tile(np.sin(fr).T, (GH, 1))
    c["rope_cos"] = cos.astype(f)
    c["rope_sin"] = sin.astype(f)
    half = np.arange(0, HD, 2, dtype=f)
    inv = f(1.0) / f(10000.0) ** (half / f(HD))
    t = np.arange(N, dtype=f)
    fr = (t[:, None] * inv[None, :]).astype(f)
    base = (half + f(0.4 * HD)) / f(1.4 * HD)
    power = (t - N // 2) / f(P // 2)
    sc = (base[None, :] ** power[:, None]).astype(f)
    two = lambda x: np.concatenate([x, x], 1)
    cos, sin, sc = two(np.cos(fr)), two(np.sin(fr)), two(sc)
    sin[:, :HD // 2] *= -1
    tab = np.stack([cos * sc * f(8), sin * sc * f(8), cos / sc, sin / sc]).astype(f)
    c["xpos"] = np.ascontiguousarray(tab.reshape(4, TW, P, HD).transpose(2, 0, 1, 3))
    return c


def laid_out(i):
    i = {k: np.asarray(v) for k, v in i.items()}
    bc = lambda x: np.ascontiguousarray(np.broadcast_to(x, (P, *x.shape)))
    kp = lambda w: np.ascontiguousarray(w.reshape(-1, P, w.shape[-1]).transpose(1, 0, 2))
    o = {}
    x = i["L0_attn_x"].reshape(B, TW, P, D).transpose(0, 2, 1, 3)
    o["x_next"] = np.ascontiguousarray(np.concatenate([x, x[:1]]))
    w = i["L0_attn_Wqkv"]
    qk = w[:2 * D].reshape(2, GH, 2, HALF, KC, P).transpose(5, 4, 0, 2, 1, 3)
    o["w_qk"] = np.ascontiguousarray(qk.reshape(P, KC, 4, P))
    bias = i["L0_attn_bqkv"]
    o["b_qk"] = np.ascontiguousarray(bias[:2 * D].reshape(2, GH, 2, HALF).transpose(1, 3, 0, 2).reshape(P, 4))
    o["w_v"] = kp(w[2 * D:].T)
    o["b_v"] = bc(bias[2 * D:])
    o["w_pre"] = np.repeat(i["L0_attn_Wpre"].T, RI, axis=0)
    o["w_post"] = np.repeat(i["L0_attn_Wpost"].T, RI, axis=0)
    wo = np.zeros((GR, PAD, GH // GR, D), w.dtype)
    wo[:, :GD] = i["L0_attn_Wout"].T.reshape(GH // GR, GR, GD, D).transpose(1, 2, 0, 3)
    o["w_out"] = wo.reshape(P, GH // GR, D)
    o["b_out"] = bc(i["L0_attn_bout"])
    qs, ks = i["L0_ffn_q_scale"], i["L0_ffn_k_scale"]
    sw = lambda s: np.concatenate([s[:, HD // 2:], s[:, :HD // 2]], 1)
    sc = np.stack([qs, sw(qs), ks, sw(ks)], 1)
    o["scales"] = np.ascontiguousarray(np.broadcast_to(sc[:, None], (LAYERS, P, 4, HD)))
    per = lambda f: np.stack([f(l) for l in range(LAYERS)])
    o["w_qkv"] = per(lambda l: kp(i["L0_ffn_wqkv"][l]))
    o["w_o"] = per(lambda l: kp(i["L0_ffn_wo"][l]))
    o["w_1"] = per(lambda l: kp(i["L0_ffn_w1"][l]))

    def padded(v):
        z = np.zeros((HC * P, *v.shape[1:]), v.dtype)
        z[:HID] = v
        return z
    o["w_2"] = per(lambda l: kp(padded(i["L0_ffn_w2"][l])))
    b1 = i["L0_ffn_b1"]
    o["b_1"] = per(lambda l: np.concatenate([padded(b1[l][:HID]).reshape(HC, P).T, padded(b1[l][HID:]).reshape(HC, P).T], 1))
    o["b_2"] = per(lambda l: bc(i["L0_ffn_b2"][l]))
    o["ln_w"] = per(lambda l: np.concatenate([i["L0_ffn_ln_g"][l].reshape(KC, P).T, i["L0_ffn_ln_b"][l].reshape(KC, P).T], 1))
    return {k: np.ascontiguousarray(v) for k, v in o.items()}


def kernel(**inputs):
    import concourse.bacc as bacc
    from concourse.bass_utils import run_bass_kernel_spmd

    arrays = {**laid_out(inputs), **shape_constants()}
    nc = bacc.Bacc("TRN2", target_bir_lowering=False, num_devices=1)
    a = {k: nc.dram_tensor(f"in_{k}", v.shape, mybir.dt.from_np(v.dtype), kind="ExternalInput").ap()
         for k, v in arrays.items()}
    a["x"] = a["x_next"]
    out = nc.dram_tensor("out_y", (B, N, D), F32, kind="ExternalOutput").ap()
    gate_network_kernel(nc, a, out)
    r = run_bass_kernel_spmd(nc, [{f"in_{k}": v for k, v in arrays.items()}], core_ids=[0])
    return r.results[0]["out_y"]
```

```python
from contextlib import ExitStack

import numpy as np

import concourse.bass as bass
from concourse import mybir

ALU = mybir.AluOpType
ACT = mybir.ActivationFunctionType
AX = mybir.AxisListType
F32 = mybir.dt.float32
F32R = mybir.dt.float32r
BF16 = mybir.dt.bfloat16

P = 128
B, N, D = 16, 512, 256
TW = N // P
KC = D // P

GH, GD = 16, 16
HALF = GD // 2
RI = P // GH
TILES = N // RI
CT = 8
ET = 2
QB = 3
CI = CT * RI
CHUNKS = TILES // CT
LAG = 2
PB = LAG + 1
GR = 4
PAD = 32

LAYERS = 2
H, HD = 8, 64
INNER = H * HD
HID = D * 4 * 2 // 3
HC = -(-HID // P)
QUADS = 2
LB = 3
MASKED = -1e30
LEAST = -87.5


def hidden_rows(c):
    return min(P, HID - c * P)


WEIGHTS = {
    "qkv": 1.5, "q_turn": 1, "k_turn": 0.3, "join": 0.3, "local_scores": 1, "weigh": 0.5, "local_values": 1,
    "p_turn": 0.7, "out_proj": 1.5, "h_turn": 2, "up": 1.6, "down": 1, "rest": 1.5,
}
AHEAD = [("norm",), ("scale",), ("x_turn", 0)]
BEHIND = [("bound",), ("sigmoid",), ("silu",), ("gated",), ("store",)]


def step_order():
    head = [("talk_qk",), ("talk_v",), ("expand", 0), ("part", 0), ("expand", 1), ("part", 1), ("expand", 2),
            ("qkv", 0, 0)]
    talk = []
    for n in range(TILES):
        talk.append([("scores", n)])
        if n % ET == 0:
            c = n // ET + QB - 1
            talk[-1] += [(kind, d) for kind, d in (("part", c), ("expand", c + 1)) if d < TILES // ET]
        if n % CT == LAG and n >= CT:
            talk[-1].append(("values", n // CT - 1))
        if n >= LAG:
            talk[-1].append(("mix", n - LAG))
        if n % (2 * CT) == 5 and n >= CT:
            talk[-1].append(("project", n // (2 * CT) - 1))
    for n in range(TILES - LAG, TILES):
        talk.append([("mix", n)])
    talk.append([("values", CHUNKS - 1)])
    talk.append([("project", TW - 1)])

    REST = []
    gate = []
    for l in range(LAYERS):
        if l:
            gate.append([("x_turn", l)])
        for t in range(TW):
            if l or t:
                gate.append([("qkv", l, t)])
            if t:
                gate.append([("q_turn", l, t - 1)])
                gate.append([("k_turn", l, t - 1)])
            gate.append([("join", l, t)])
        gate += [REST, REST]
        gate.append([("q_turn", l, TW - 1)])
        gate.append([("k_turn", l, TW - 1)])
        units = TW * QUADS
        for u in range(units + 3):
            if u < units:
                gate.append([("local_scores", l, u)])
            if 1 <= u <= units:
                gate.append([("weigh", l, u - 1)])
            if u >= 3 and u % QUADS == 1 and u > QUADS + 1:
                gate.append([("out_proj", l, u // QUADS - 2)])
            if 3 <= u <= units + 2:
                gate.append([("local_values", l, u - 3)])
            if 2 <= u <= units + 1:
                gate.append([("p_turn", l, u - 2)])
        gate += [[("out_proj", l, TW - 1)]]
        gate += [[("half_turn", l)], [("shift_turn", l)], REST, REST, [("h_scale", l)], REST, REST, [("h_turn", l)]]
        gate += [[("up", l, c)] for c in range(HC)]
        if l == LAYERS - 1:
            gate[-3:-3] = [[("norm",)]]
            gate[-1:-1] = [[("scale",)]]
            gate.append([("x_turn", 0)])
        gate += [[("down", l, t)] for t in range(TW)]

    weight = [sum(WEIGHTS.get(step[0], 1) for step in g) if g else WEIGHTS["rest"] for g in gate]
    order, done = list(head), 0
    for i, steps in enumerate(talk):
        order += steps
        while done < len(gate) and sum(weight[:done + 1]) * len(talk) <= sum(weight) * (i + 1):
            order += gate[done]
            done += 1
        if i % 2 == 0 and i < 2 * (len(BEHIND) + 1):
            order.append([*BEHIND, ("keep",)][i // 2])
    return order


def banks_of(step):
    kind = step[0]
    if kind == "scores":
        return [f"S{step[1] % 2}"]
    if kind == "mix":
        return ["M"]
    if kind in ("values", "project", "local_values", "k_turn"):
        return ["V"]
    if kind == "talk_qk":
        return ["S0", "S1", "M", "V"]
    if kind == "talk_v":
        return ["S0", "S1"]
    if kind == "up":
        return ["F0", "F1"] if step[2] % 2 == 0 else ["F2", "F3"]
    if kind == "down":
        return [f"F{step[2]}"]
    return {
        "x_turn": ["F0", "F1"], "qkv": ["F0", "F1", "F2"], "q_turn": ["F3"],
        "local_scores": ["F0", "F1"], "p_turn": ["F2", "F3"], "out_proj": ["F3"],
        "half_turn": ["F0"], "shift_turn": ["F1"], "h_turn": ["F2", "F3"],
    }.get(kind, [])


BANKS = ["S0", "S1", "M", "V", "F0", "F1", "F2", "F3"]


def gate_network_kernel(nc, a, out):
    order = step_order()
    ahead = {k: 1 if k in banks_of(("x_turn", 0)) else 0 for k in BANKS}
    filling, fillings = {}, {k: 0 for k in BANKS}
    for step in order:
        for k in banks_of(step):
            fillings[k] += 1
            filling[step, k] = fillings[k]

    with ExitStack() as ctx:
        def sb(name, shape, dt=F32):
            return ctx.enter_context(nc.sbuf_tensor(name, [P, *shape], dt))

        ident = sb("ident", [P])
        ident_bf = sb("ident_bf", [P], BF16)
        mask_bf = sb("mask_bf", [2, 2 * P], BF16)
        rope_cos = sb("rope_cos", [N])
        rope_sin = sb("rope_sin", [N])
        delta = sb("delta", [RI])
        w_qk = sb("w_qk", [KC, 4, P])
        b_qk = sb("b_qk", [4])
        w_v = sb("w_v", [KC, D])
        b_v = sb("b_v", [D])
        w_pre = sb("w_pre", [GH])
        w_post = sb("w_post", [GH])
        w_out = sb("w_out", [GR, D])
        b_out = sb("b_out", [D])
        mixer = sb("mixer", [GH, RI])
        rot = [sb(f"rot{l}", [4, TW, HD]) for l in range(LAYERS)]
        w_qkv = sb("w_qkv", [KC, 3 * INNER])
        w_o = sb("w_o", [INNER // P, D])
        w_1 = sb("w_1", [KC, 2 * HID])
        w_2 = sb("w_2", [HC, D])
        b_1 = [sb(f"b_1{l}", [2 * HC]) for l in range(LAYERS)]
        b_2 = [sb(f"b_2{l}", [D]) for l in range(LAYERS)]
        ln_w = [sb(f"ln_w{l}", [2 * KC]) for l in range(LAYERS)]
        minus_half = sb("minus_half", [2 * H])
        opener = sb("opener", [1])
        opener_p = sb("opener_p", [1])
        eps = sb("eps", [TW])

        x_in = sb("x_in", [TW, D])
        x_keep = sb("x_keep", [TW, D])
        x_tok = sb("x_tok", [TW, D])
        xT = sb("xT", [KC, N + 1])
        stats = sb("stats", [TW, 2, 6])
        mean_var = sb("mean_var", [TW, 2])
        var_eps = sb("var_eps", [TW])
        rstd = sb("rstd", [TW])
        q_rope = sb("q_rope", [2, N])
        k_hi = sb("k_hi", [2, N], F32R)
        k_lo = sb("k_lo", [2, N], F32R)
        v_pad = sb("v_pad", [TW, GH, PAD])
        q_mix = sb("q_mix", [2, ET, P])
        q_hi = sb("q_hi", [QB, 2, ET, P], F32R)
        q_lo = sb("q_lo", [QB, 2, ET, P], F32R)
        neg_max = sb("neg_max", [2])
        row_sum = sb("row_sum", [PB])
        row_inv = sb("row_inv", [2])
        probs = sb("probs", [PB, N])
        mixer_n = sb("mixer_n", [2, P])
        mixed = sb("mixed", [TW, GH, CI])
        before = mixed[:].rearrange("p j g i -> p (j g i)").rearrange("p (a n) -> p a n", n=N)
        raw_qk, t_q, t_k = before[:, 0:4], before[:, 4:6], before[:, 6:8]
        k_rope = raw_qk[:, 2:4]
        oT = sb("oT", [GR, P])
        s_tok = sb("s_tok", [TW, D])

        shared = sb("shared", [8, INNER])
        sq = shared[:, 0:2]
        rot_a, rot_b, qk_tok = shared[:, 2:4], shared[:, 4:6], shared[:, 6:8]
        x_mid_b, h_tok = (shared[:, j:j + 2].rearrange("p a (b f) -> p (a b) f", f=D) for j in (0, 2))
        hT, gelu = shared[:, 4:6], shared[:, 6:8]
        norms = sb("norms", [2 * H])
        norms_c = sb("norms_c", [2 * H])
        inv_norms = sb("inv_norms", [2 * H])
        att = sb("att", [3 * 4, N])
        qT = att[:, 0:4, :]
        kT = att[:, 4:8, :]
        v_loc = att[:, 8:12, :]
        hidden = att[:, 0:HC, :]
        l_max = sb("l_max", [2, 4])
        l_sum = sb("l_sum", [2, 4])
        l_inv = sb("l_inv", [2, 4])
        l_probs = sb("l_probs", [LB, 4, 2 * P])
        pT = sb("pT", [2, 4, P])
        o_locT = sb("o_locT", [4, P])
        x_mid = sb("x_mid", [TW, D])
        midT = sb("midT", [N + 1])
        setup = l_probs[:].rearrange("p a h k -> p (a h k)")
        xpos = setup[:, 0:4 * TW * HD].rearrange("p (j t d) -> p j t d", j=4, t=TW)
        mask = setup[:, (4 * TW + 4 * LAYERS) * HD:(4 * TW + 4 * LAYERS) * HD + 4 * P]
        scales = [setup[:, (4 * TW + 4 * l) * HD:(4 * TW + 4 * l + 4) * HD].rearrange("p (j d) -> p j d", j=4)
                  for l in range(LAYERS)]

        bank = {k: ctx.enter_context(nc.psum_tensor(f"bank_{k}", [P, 512], F32)) for k in BANKS}

        per, base = {}, {}

        def sem(name, count, before=0):
            h = ctx.enter_context(nc.semaphore(name))
            per[id(h)] = count
            base[id(h)] = before
            return h

        filled = {k: sem(f"filled_{k}", fillings[k], ahead[k]) for k in BANKS}
        emptied = {k: sem(f"emptied_{k}", fillings[k], ahead[k]) for k in BANKS}
        QL = TW * QUADS * LAYERS
        WL = TW * LAYERS
        loads = sem("loads", 0)
        tables = sem("tables", 0)
        pads = sem("pads", 0)
        x_loaded = sem("x_loaded", 16, 16)
        keep_loaded = sem("keep_loaded", 16)
        qkv_loaded = sem("qkv_loaded", 16 * LAYERS)
        w_o_loaded = sem("w_o_loaded", 16 * LAYERS)
        w_1_loaded = sem("w_1_loaded", 16 * LAYERS)
        w_2_loaded = sem("w_2_loaded", 16 * LAYERS)
        stats_done = sem("stats_done", LAYERS * 2 * TW + TW, TW)
        aggr_done = sem("aggr_done", LAYERS + 1, 1)
        eps_done = sem("eps_done", LAYERS + 1, 1)
        rstd_done = sem("rstd_done", LAYERS + 1, 1)
        x_ready = sem("x_ready", TW, TW)
        k_parts = sem("k_parts", 2)
        k_roped = sem("k_roped", 1)
        q_parts = sem("q_parts", 2)
        q_roped = sem("q_roped", 1)
        k_hi_done = sem("k_hi_done", 1)
        k_lo_done = sem("k_lo_done", 1)
        q_mixed = sem("q_mixed", 2 * TILES // ET)
        q_hi_done = sem("q_hi_done", TILES // ET)
        q_lo_done = sem("q_lo_done", TILES // ET)
        max_done = sem("max_done", TILES)
        inv_done = sem("inv_done", TILES)
        mixer_done = sem("mixer_done", TILES)
        s_done = sem("s_done", TW)
        norm_done = sem("norm_done", 2 * WL)
        rot_done = sem("rot_done", 2 * WL)
        clip_done = sem("clip_done", WL)
        inv_norm_done = sem("inv_norm_done", WL)
        rot_added = sem("rot_added", WL)
        qk_ready = sem("qk_ready", 2 * WL)
        l_max_done = sem("l_max_done", QL)
        l_inv_done = sem("l_inv_done", QL)
        l_scaled = sem("l_scaled", QL)
        mid_b_ready = sem("mid_b_ready", LAYERS)
        h_ready = sem("h_ready", LAYERS * TW)
        gelu_done = sem("gelu_done", LAYERS * HC)
        bounded = sem("bounded", 1)
        exp_done = sem("exp_done", 1)
        one_plus = sem("one_plus", 1)
        sig_done = sem("sig_done", 1)
        silu_done = sem("silu_done", 1)
        gated_done = sem("gated_done", 1)
        o_ready = sem("o_ready", 1)
        stored = sem("stored", 16)

        once = [
            (ident[:], a["ident"]), (mask, a["mask"]),
            (rope_cos[:], a["rope_cos"]), (rope_sin[:], a["rope_sin"]), (delta[:], a["delta"]),
            (w_qk[:], a["w_qk"]), (b_qk[:], a["b_qk"]), (w_v[:], a["w_v"]), (b_v[:], a["b_v"]),
            (w_pre[:], a["w_pre"]), (w_post[:], a["w_post"]), (w_out[:], a["w_out"]),
            (b_out[:], a["b_out"]), (xpos, a["xpos"]),
        ]
        for l in range(LAYERS):
            once += [
                (scales[l], a["scales"][l]), (b_1[l][:], a["b_1"][l]),
                (b_2[l][:], a["b_2"][l]), (ln_w[l][:], a["ln_w"][l]),
            ]
        LOADED = 16 * len(once)
        TABLES = 4 + 4 * LAYERS

        class Counts:
            def __init__(self):
                self.b, self.first, self.ahead = -1, True, True

            def past(self, k):
                return k > 0 or not self.first

            def at(self, sem, k):
                return self.b * per[id(sem)] + base[id(sem)] + k

            def fill(self, step, k, ago=0):
                if self.ahead:
                    return ahead[k]
                return self.b * fillings[k] + ahead[k] + filling[step, k] - ago * fillings[k]

            def was_filled(self, step, k):
                return not self.ahead and self.past(ahead[k] + filling[step, k] - 1)

            def x_turned(self, l, k):
                return ahead[k] if self.first and not l else self.fill(("x_turn", l), k, ago=not l)

            def run(self, eng, steps):
                def go(list_of_steps):
                    for step in list_of_steps:
                        if step[0] in steps and not (step in BEHIND and self.first):
                            steps[step[0]](step, *step[1:])
                go(AHEAD)
                self.b, self.ahead = 0, False
                go(order)
                self.first = False
                with eng.Fori(1, B) as b:
                    self.b = b
                    go(order)
                self.b = B
                go(BEHIND)

        def window_before(l, t):
            return (l, t - 1) if t else ((l - 1) % LAYERS, TW - 1)

        def unit_before(l, u, by):
            n = (TW * QUADS * l + u - by) % (LAYERS * TW * QUADS)
            return n // (TW * QUADS), n % (TW * QUADS)

        def stream_ready(eng, now, l, ago=0):
            if l == 0:
                eng.wait_ge(x_ready, now.at(x_ready, TW))
            else:
                for t in range(TW):
                    eng.wait_ge(emptied[f"F{t}"], now.fill(("down", l - 1, t), f"F{t}", ago=ago))

        def store_mixed(eng, copy, now, n):
            c, m = n // CT, n % CT
            if c:
                eng.wait_ge(filled["V"], now.fill(("values", c - 1), "V"))
            else:
                eng.wait_ge(q_roped, now.at(q_roped, 1))
                eng.wait_ge(k_lo_done, now.at(k_lo_done, 1))
            copy(mixed[:, :, :, m * RI:(m + 1) * RI],
                 bank["M"][:].rearrange("p (j g i) -> p j g i", j=TW, g=GH)).then_inc(emptied["M"], 1)

        block = ctx.enter_context(nc.Block())

        @block.sync
        def _(sp):
            now = Counts()
            for dst, src in once:
                sp.dma_start(dst, src).then_inc(loads, 16)
            sp.dma_start(w_qkv[:], a["w_qkv"][0]).then_inc(qkv_loaded, 16)
            sp.dma_start(w_o[:], a["w_o"][0]).then_inc(w_o_loaded, 16)
            sp.dma_start(w_1[:], a["w_1"][0]).then_inc(w_1_loaded, 16)
            sp.dma_start(w_2[:], a["w_2"][0]).then_inc(w_2_loaded, 16)

            def qkv(step, l, t):
                if t == TW - 1:
                    sp.wait_ge(filled["F2"], now.fill(step, "F2"))
                    sp.dma_start(w_qkv[:], a["w_qkv"][(l + 1) % LAYERS]).then_inc(qkv_loaded, 16)

            def out_proj(step, l, t):
                if t == TW - 1:
                    sp.wait_ge(filled["F3"], now.fill(step, "F3"))
                    sp.dma_start(w_o[:], a["w_o"][(l + 1) % LAYERS]).then_inc(w_o_loaded, 16)

            def up(step, l, i):
                if i == HC - 1:
                    k = banks_of(step)[1]
                    sp.wait_ge(filled[k], now.fill(step, k))
                    sp.dma_start(w_1[:], a["w_1"][(l + 1) % LAYERS]).then_inc(w_1_loaded, 16)

            def down(step, l, t):
                if t == TW - 1:
                    sp.wait_ge(filled["F3"], now.fill(step, "F3"))
                    sp.dma_start(w_2[:], a["w_2"][(l + 1) % LAYERS]).then_inc(w_2_loaded, 16)

            now.run(sp, {"qkv": qkv, "out_proj": out_proj, "up": up, "down": down})
            sp.wait_ge(keep_loaded, 16 * B)
            sp.wait_ge(x_loaded, 16 * (B + 1))
            sp.wait_ge(qkv_loaded, 16 * (LAYERS * B + 1))
            sp.wait_ge(w_o_loaded, 16 * (LAYERS * B + 1))
            sp.wait_ge(w_1_loaded, 16 * (LAYERS * B + 1))
            sp.wait_ge(w_2_loaded, 16 * (LAYERS * B + 1))
            sp.wait_ge(stored, 16 * B)

        @block.tensor
        def _(pe):
            now = Counts()
            mm = nc.tensor.matmul
            turn = nc.tensor.transpose
            pe.wait_ge(loads, LOADED)
            pe.wait_ge(tables, TABLES)
            pe.wait_ge(pads, 5)

            def x_turn(step, l):
                stream_ready(pe, now, l)
                for c in range(KC):
                    if now.was_filled(step, f"F{c}"):
                        pe.wait_ge(emptied[f"F{c}"], now.fill(step, f"F{c}") - 1)
                    x = x_tok if l else x_in
                    for t in range(TW):
                        last = turn(bank[f"F{c}"][:, t * P:(t + 1) * P], x[:, t, c * P:(c + 1) * P], ident[:])
                    last.then_inc(filled[f"F{c}"], 1)

            def talk_qk(step):
                for c in range(KC):
                    pe.wait_ge(emptied[f"F{c}"], now.x_turned(0, f"F{c}"))
                for j, k in enumerate(["S0", "S1", "M", "V"]):
                    if now.was_filled(step, k):
                        pe.wait_ge(emptied[k], now.fill(step, k) - 1)
                    for c in range(KC):
                        last = mm(bank[k][:], w_qk[:, c, j, :], xT[:, c, 1:N + 1], start=(c == 0), stop=(c == KC - 1))
                    last.then_inc(filled[k], 1)

            def talk_v(step):
                for t in range(TW):
                    k = f"S{t // 2}"
                    if t % 2 == 0:
                        if now.was_filled(step, k):
                            pe.wait_ge(emptied[k], now.fill(step, k) - 1)
                    for c in range(KC):
                        last = mm(bank[k][:, (t % 2) * D:(t % 2 + 1) * D], xT[:, c, 1 + t * P:1 + (t + 1) * P],
                                  w_v[:, c, :], start=(c == 0), stop=(c == KC - 1))
                    if t % 2:
                        last.then_inc(filled[k], 1)

            def scores(step, n):
                k = f"S{n % 2}"
                if n == 0:
                    pe.wait_ge(k_lo_done, now.at(k_lo_done, 1))
                if n % ET == 0:
                    pe.wait_ge(q_lo_done, now.at(q_lo_done, n // ET + 1))
                if now.was_filled(step, k):
                    pe.wait_ge(emptied[k], now.fill(step, k) - 1)
                for s in range(2):
                    q = (slice(None), (n // ET) % QB, s, n % ET)
                    mm(bank[k][:], q_lo[q], k_hi[:, s, :], start=(s == 0), stop=False)
                    mm(bank[k][:], q_hi[q], k_lo[:, s, :], start=False, stop=False)
                    last = mm(bank[k][:], q_hi[q], k_hi[:, s, :], start=False, stop=(s == 1))
                last.then_inc(filled[k], 1)

            def mix(step, n):
                pe.wait_ge(mixer_done, now.at(mixer_done, n + 1))
                if now.was_filled(step, "M"):
                    pe.wait_ge(emptied["M"], now.fill(step, "M") - 1)
                for j in range(TW):
                    last = mm(bank["M"][:, j * P:(j + 1) * P], probs[:, n % PB, j * P:(j + 1) * P],
                              mixer_n[:, n % 2, :], start=True, stop=True)
                last.then_inc(filled["M"], 1)

            def values(step, c):
                pe.wait_ge(emptied["M"], now.fill(("mix", (c + 1) * CT - 1), "M"))
                for j in range(2):
                    pe.wait_ge(emptied[f"S{j}"], now.fill(("talk_v",), f"S{j}"))
                if now.was_filled(step, "V"):
                    pe.wait_ge(emptied["V"], now.fill(step, "V") - 1)
                for r in range(GH // GR):
                    for j in range(TW):
                        for q in range(GR):
                            g = GR * r + q
                            last = mm(bank["V"][PAD * q:PAD * (q + 1), r * CI:(r + 1) * CI], v_pad[:, j, g, :],
                                      mixed[:, j, g, :], start=(j == 0), stop=(j == TW - 1))
                last.then_inc(filled["V"], 1)

            def project(step, t):
                pe.wait_ge(emptied["V"], now.fill(step, "V") - 1)
                for r in range(GH // GR):
                    last = mm(bank["V"][:, 0:D], oT[:, r, :], w_out[:, r, :], start=(r == 0), stop=(r == GH // GR - 1))
                last.then_inc(filled["V"], 1)

            def qkv(step, l, t):
                for c in range(KC):
                    pe.wait_ge(emptied[f"F{c}"], now.x_turned(l, f"F{c}"))
                pe.wait_ge(qkv_loaded, now.at(qkv_loaded, 16 * (l + 1)))
                for j in range(3):
                    k = f"F{j}"
                    if now.was_filled(step, k):
                        pe.wait_ge(emptied[k], now.fill(step, k) - 1)
                    for c in range(KC):
                        at = 1 - c + t * P
                        last = mm(bank[k][:], xT[:, c, at:at + P], w_qkv[:, c, j * INNER:(j + 1) * INNER],
                                  start=(c == 0), stop=(c == KC - 1))
                    last.then_inc(filled[k], 1)

            def qk_turn(step, l, t, j):
                k, = banks_of(step)
                pe.wait_ge(qk_ready, now.at(qk_ready, 2 * (TW * l + t) + j + 1))
                if now.was_filled(step, k):
                    pe.wait_ge(emptied[k], now.fill(step, k) - 1)
                for c in range(4):
                    last = turn(bank[k][:, c * P:(c + 1) * P], qk_tok[:, j, c * P:(c + 1) * P], ident[:])
                last.then_inc(filled[k], 1)

            def local_scores(step, l, u):
                t, quad = u // QUADS, u % QUADS
                pe.wait_ge(emptied["F3"], now.fill(("q_turn", l, TW - 1), "F3"))
                pe.wait_ge(emptied["V"], now.fill(("k_turn", l, TW - 1), "V"))
                for parity in range(2):
                    k = f"F{parity}"
                    if now.was_filled(step, k):
                        pe.wait_ge(emptied[k], now.fill(step, k) - 1)
                    mm(bank[k][:], ident_bf[:], mask_bf[:].rearrange("p a j -> p (a j)"), start=True, stop=False,
                       skip_group_check=True)
                    for pair in range(2):
                        hp = 2 * quad + pair
                        lo = P if t == 0 else 0
                        rows = slice(HD * parity, HD * (parity + 1))
                        last = mm(bank[k][:, pair * 2 * P + lo:(pair + 1) * 2 * P],
                                  qT[rows, hp, t * P:(t + 1) * P],
                                  kT[rows, hp, (t - 1) * P + lo:(t + 1) * P],
                                  start=False, stop=(pair == 1), skip_group_check=True)
                    last.then_inc(filled[k], 1)

            def p_turn(step, l, u):
                pe.wait_ge(l_scaled, now.at(l_scaled, TW * QUADS * l + u + 1))
                lo = 1 if u // QUADS == 0 else 0
                for pair in range(2):
                    k = f"F{2 + pair}"
                    if now.was_filled(step, k):
                        pe.wait_ge(emptied[k], now.fill(step, k) - 1)
                    for parity in range(2):
                        for j in range(lo, 2):
                            last = turn(bank[k][:, (2 * parity + j) * P:(2 * parity + j + 1) * P],
                                        l_probs[:, u % LB, 2 * parity + pair, j * P:(j + 1) * P], ident[:])
                    last.then_inc(filled[k], 1)

            def local_values(step, l, u):
                t, quad = u // QUADS, u % QUADS
                for pair in range(2):
                    pe.wait_ge(emptied[f"F{2 + pair}"], now.fill(("p_turn", l, u), f"F{2 + pair}"))
                if now.was_filled(step, "V"):
                    pe.wait_ge(emptied["V"], now.fill(step, "V") - 1)
                lo = 1 if t == 0 else 0
                for pair in range(2):
                    for j in range(lo, 2):
                        for parity in range(2):
                            h = 4 * quad + 2 * pair + parity
                            last = mm(bank["V"][HD * parity:HD * (parity + 1), pair * P:(pair + 1) * P],
                                      v_loc[:, t - 1 + j, h * HD:(h + 1) * HD], pT[:, pair, 2 * parity + j, :],
                                      start=(j == lo), stop=(j == 1))
                last.then_inc(filled["V"], 1)

            def out_proj(step, l, t):
                for quad in range(QUADS):
                    pe.wait_ge(emptied["V"], now.fill(("local_values", l, QUADS * t + quad), "V"))
                if now.was_filled(step, "F3"):
                    pe.wait_ge(emptied["F3"], now.fill(step, "F3") - 1)
                pe.wait_ge(w_o_loaded, now.at(w_o_loaded, 16 * (l + 1)))
                for c in range(4):
                    last = mm(bank["F3"][:, 0:D], o_locT[:, c, :], w_o[:, c, :], start=(c == 0), stop=(c == 3))
                last.then_inc(filled["F3"], 1)

            def half_turn(step, l):
                pe.wait_ge(emptied["F3"], now.fill(("out_proj", l, TW - 1), "F3"))
                if now.was_filled(step, "F0"):
                    pe.wait_ge(emptied["F0"], now.fill(step, "F0") - 1)
                for t in range(TW):
                    last = turn(bank["F0"][:, t * P:(t + 1) * P], x_mid[:, t, P:D], ident[:])
                last.then_inc(filled["F0"], 1)

            def shift_turn(step, l):
                pe.wait_ge(emptied["F0"], now.fill(("half_turn", l), "F0"))
                if now.was_filled(step, "F1"):
                    pe.wait_ge(emptied["F1"], now.fill(step, "F1") - 1)
                for t in range(TW):
                    last = turn(bank["F1"][:, t * P:(t + 1) * P], midT[:, t * P:(t + 1) * P], ident[:])
                last.then_inc(filled["F1"], 1)

            def h_turn(step, l):
                pe.wait_ge(h_ready, now.at(h_ready, TW * (l + 1)))
                pe.wait_ge(emptied["F1"], now.fill(("shift_turn", l), "F1"))
                for c in range(KC):
                    k = f"F{2 + c}"
                    if now.was_filled(step, k):
                        pe.wait_ge(emptied[k], now.fill(step, k) - 1)
                    for t in range(TW):
                        last = turn(bank[k][:, t * P:(t + 1) * P], h_tok[:, t, c * P:(c + 1) * P], ident[:])
                    last.then_inc(filled[k], 1)

            def up(step, l, i):
                for c in range(KC):
                    pe.wait_ge(emptied[f"F{2 + c}"], now.fill(("h_turn", l), f"F{2 + c}"))
                pe.wait_ge(w_1_loaded, now.at(w_1_loaded, 16 * (l + 1)))
                m = hidden_rows(i)
                for j, k in enumerate(banks_of(step)):
                    if now.was_filled(step, k):
                        pe.wait_ge(emptied[k], now.fill(step, k) - 1)
                    for c in range(KC):
                        at = j * HID + i * P
                        last = mm(bank[k][0:m, :], w_1[:, c, at:at + m], hT[:, c, :], start=(c == 0), stop=(c == KC - 1))
                    last.then_inc(filled[k], 1)

            def down(step, l, t):
                pe.wait_ge(emptied[banks_of(("up", l, HC - 1))[0]], now.fill(("up", l, HC - 1), banks_of(("up", l, HC - 1))[0]))
                k = f"F{t}"
                if now.was_filled(step, k):
                    pe.wait_ge(emptied[k], now.fill(step, k) - 1)
                pe.wait_ge(w_2_loaded, now.at(w_2_loaded, 16 * (l + 1)))
                for i in range(HC):
                    m = hidden_rows(i)
                    last = mm(bank[k][:, 0:D], hidden[0:m, i, t * P:(t + 1) * P], w_2[0:m, i, :],
                              start=(i == 0), stop=(i == HC - 1))
                last.then_inc(filled[k], 1)

            steps = {
                "x_turn": x_turn, "talk_qk": talk_qk, "talk_v": talk_v, "scores": scores, "mix": mix,
                "values": values, "project": project, "qkv": qkv,
                "q_turn": lambda step, l, t: qk_turn(step, l, t, 0),
                "k_turn": lambda step, l, t: qk_turn(step, l, t, 1),
                "local_scores": local_scores, "p_turn": p_turn, "local_values": local_values,
                "out_proj": out_proj, "half_turn": half_turn, "shift_turn": shift_turn,
                "h_turn": h_turn, "up": up, "down": down,
            }

            now.run(pe, steps)

        @block.scalar
        def _(act):
            now = Counts()
            fn = nc.scalar.activation
            act.wait_ge(loads, LOADED)

            def x_turn(step, l):
                if not now.ahead:
                    act.wait_ge(filled["F2"], now.fill(("qkv", (l - 1) % LAYERS, TW - 1), "F2"))
                    act.wait_ge(filled["S1"], now.fill(("talk_v",), "S1"))
                for c in range(KC):
                    k = f"F{c}"
                    act.wait_ge(filled[k], now.fill(step, k))
                    fn(xT[:, c, 1:N + 1], bank[k][:], ACT.Copy).then_inc(emptied[k], 1)

            def talk_qk(step):
                if not now.first:
                    act.wait_ge(filled["V"], now.fill(("values", CHUNKS - 1), "V", ago=1))
                for j, k in enumerate(["S0", "S1", "M", "V"]):
                    act.wait_ge(filled[k], now.fill(step, k))
                    fn(raw_qk[:, j, :], bank[k][:], ACT.Identity, bias=b_qk[:, j:j + 1]).then_inc(emptied[k], 1)

            def part(step, c):
                act.wait_ge(q_mixed, now.at(q_mixed, 2 * (c + 1)))
                if c >= QB:
                    act.wait_ge(filled["S1"], now.fill(("scores", (c - QB + 1) * ET - 1), "S1"))
                elif not now.first:
                    act.wait_ge(filled["S1"], now.fill(("scores", TILES - 1), "S1", ago=1))
                fn(q_hi[:, c % QB], q_mix[:], ACT.Copy).then_inc(q_hi_done, 1)

            def scores(step, n):
                k = f"S{n % 2}"
                act.wait_ge(max_done, now.at(max_done, n + 1))
                if n >= PB:
                    act.wait_ge(filled["M"], now.fill(("mix", n - PB), "M"))
                elif not now.first:
                    act.wait_ge(filled["M"], now.fill(("mix", TILES - 1), "M", ago=1))
                fn(probs[:, n % PB, :], bank[k][:], ACT.Exp, bias=neg_max[:, n % 2:n % 2 + 1],
                   accum_out=row_sum[:, n % PB:n % PB + 1]).then_inc(emptied[k], 1)

            def mix(step, n):
                if n % 2:
                    return
                act.wait_ge(filled["M"], now.fill(step, "M"))
                store_mixed(act, nc.scalar.copy, now, n)

            def values(step, c):
                act.wait_ge(filled["V"], now.fill(step, "V"))
                if c % 2 == 0:
                    if now.past(not (c < 2)):
                        act.wait_ge(filled["V"], now.fill(("project", (c // 2 - 1) % TW), "V", ago=c < 2))
                at = (c % 2) * CI
                fn(oT[:, :, at:at + CI], bank["V"][:, 0:GR * CI].rearrange("p (r i) -> p r i", r=GR), ACT.Copy)\
                    .then_inc(emptied["V"], 1)

            def qkv(step, l, t):
                w = TW * l + t
                for j in range(2):
                    if now.past(2 * (w - 1) + j + 1):
                        act.wait_ge(norm_done, now.at(norm_done, 2 * (w - 1) + j + 1))
                    act.wait_ge(rot_done, now.at(rot_done, 2 * w + j + 1))
                    fn(sq[:, j, :], bank[f"F{j}"][:], ACT.Square).then_inc(emptied[f"F{j}"], 1)
                if t == 0:
                    if now.past(not (not l)):
                        act.wait_ge(filled["V"], now.fill(("local_values", (l - 1) % LAYERS, TW * QUADS - 1), "V", ago=not l))
                act.wait_ge(filled["F2"], now.fill(step, "F2"))
                fn(v_loc[:, t, :], bank["F2"][:], ACT.Copy).then_inc(emptied["F2"], 1)

            def q_turn(step, l, t):
                if t == 0:
                    if now.past(not (not l)):
                        act.wait_ge(filled["F3"], now.fill(("down", (l - 1) % LAYERS, TW - 1), "F3", ago=not l))
                act.wait_ge(filled["F3"], now.fill(step, "F3"))
                fn(qT[:, :, t * P:(t + 1) * P], bank["F3"][:].rearrange("p (c i) -> p c i", c=4), ACT.Copy)\
                    .then_inc(emptied["F3"], 1)

            def local_scores(step, l, u):
                n = TW * QUADS * l + u
                lo = P if u // QUADS == 0 else 0
                act.wait_ge(l_max_done, now.at(l_max_done, n + 1))
                if u >= LB:
                    act.wait_ge(filled["F3"], now.fill(("p_turn", l, u - LB), "F3"))
                elif now.past(l):
                    act.wait_ge(filled["F3"], now.fill(("p_turn", (l - 1) % LAYERS, TW * QUADS - 1), "F3", ago=not l))
                if now.past(n - 1):
                    act.wait_ge(l_inv_done, now.at(l_inv_done, n - 1))
                for parity in range(2):
                    for pair in range(2):
                        j = 2 * parity + pair
                        ins = fn(l_probs[:, u % LB, j, lo:], bank[f"F{parity}"][:, pair * 2 * P + lo:(pair + 1) * 2 * P],
                                 ACT.Exp, bias=l_max[:, u % 2, j:j + 1], accum_out=l_sum[:, u % 2, j:j + 1])
                    ins.then_inc(emptied[f"F{parity}"], 1)

            def p_turn(step, l, u):
                act.wait_ge(filled["F3"], now.fill(step, "F3"))
                if now.past(not (not l and not u)):
                    act.wait_ge(filled["V"], now.fill(("local_values", *unit_before(l, u, 1)), "V", ago=not l and not u))
                lo = 1 if u // QUADS == 0 else 0
                fn(pT[:, 1, :, :].rearrange("p (a j) i -> p a j i", a=2)[:, :, lo:, :],
                   bank["F3"][:].rearrange("p (a j i) -> p a j i", a=2, j=2)[:, :, lo:, :], ACT.Copy)\
                    .then_inc(emptied["F3"], 1)

            def half_turn(step, l):
                act.wait_ge(filled["F0"], now.fill(step, "F0"))
                if now.past(not (not l)):
                    act.wait_ge(filled["F1"], now.fill(("shift_turn", (l - 1) % LAYERS), "F1", ago=not l))
                fn(midT[:, 1:N + 1], bank["F0"][:], ACT.Copy).then_inc(emptied["F0"], 1)

            def h_turn(step, l):
                act.wait_ge(rot_added, now.at(rot_added, TW * (l + 1)))
                for c in range(KC):
                    k = f"F{2 + c}"
                    act.wait_ge(filled[k], now.fill(step, k))
                    fn(hT[:, c, :], bank[k][:], ACT.Identity, bias=ln_w[l][:, KC + c:KC + c + 1],
                       scale=ln_w[l][:, c:c + 1]).then_inc(emptied[k], 1)

            def up(step, l, i):
                k = banks_of(step)[1]
                m = hidden_rows(i)
                act.wait_ge(filled[k], now.fill(step, k))
                if i >= 2:
                    act.wait_ge(emptied[banks_of(("up", l, i - 2))[0]], now.fill(("up", l, i - 2), banks_of(("up", l, i - 2))[0]))
                else:
                    act.wait_ge(filled["V"], now.fill(("k_turn", l, TW - 1), "V"))
                fn(gelu[0:m, i % 2, :], bank[k][0:m, :], ACT.Gelu, bias=b_1[l][0:m, HC + i:HC + i + 1])\
                    .then_inc(emptied[k], 1)

            def bound(step):
                act.wait_ge(bounded, now.at(bounded, 0))
                fn(x_mid[:], x_mid[:], ACT.Exp, scale=-1.0).then_inc(exp_done, 1)

            steps = {
                "x_turn": x_turn, "talk_qk": talk_qk, "part": part, "scores": scores, "mix": mix, "values": values,
                "qkv": qkv, "q_turn": q_turn, "local_scores": local_scores, "p_turn": p_turn,
                "half_turn": half_turn, "h_turn": h_turn, "up": up, "bound": bound,
            }

            now.run(act, steps)

        @block.vector
        def _(dve):
            now = Counts()
            v = nc.vector
            v.memset(xT[:, :, 0:1], 0.0).then_inc(pads, 1)
            v.memset(midT[:, 0:1], 0.0).then_inc(pads, 1)
            v.memset(v_pad[:], 0.0).then_inc(pads, 1)
            v.memset(minus_half[:], -0.5).then_inc(pads, 1)
            v.memset(eps[:], 1e-5).then_inc(pads, 1)
            dve.wait_ge(pads, 5)
            dve.wait_ge(loads, LOADED)
            v.tensor_copy(mask_bf[:].rearrange("p a j -> p (a j)"), mask).then_inc(tables, 1)
            v.tensor_copy(ident_bf[:], ident[:]).then_inc(tables, 1)
            v.tensor_scalar(w_pre[:], w_pre[:], float(GD) ** -0.5, None, ALU.mult).then_inc(tables, 1)
            v.tensor_tensor(mixer[:], w_post[:, :, None].to_broadcast([P, GH, RI]),
                            delta[:, None, :].to_broadcast([P, GH, RI]), ALU.mult).then_inc(tables, 1)
            for l in range(LAYERS):
                for j in range(4):
                    v.tensor_tensor(rot[l][:, j], xpos[:, j], scales[l][:, j, None, :].to_broadcast([P, TW, HD]),
                                    ALU.mult).then_inc(tables, 1)
            dve.wait_ge(tables, TABLES)

            def norm(step):
                dve.wait_ge(x_loaded, now.at(x_loaded, 16))
                if not now.ahead:
                    dve.wait_ge(aggr_done, now.at(aggr_done, LAYERS))
                for t in range(TW):
                    v.bn_stats(stats[:, t, 0, :], x_in[:, t, :]).then_inc(stats_done, 1)
                if not now.ahead:
                    dve.wait_ge(emptied["F1"], now.fill(("shift_turn", LAYERS - 1), "F1"))
                    dve.wait_ge(h_ready, now.at(h_ready, LAYERS * TW))
                dve.wait_ge(stats_done, now.at(stats_done, LAYERS * 2 * TW + TW))
                v.memset(opener[:], 0.0)
                for t in range(TW):
                    ins = v.bn_aggr(mean_var[:, t, :], stats[:, t, 0, :])
                ins.then_inc(aggr_done, 1)

            def scale(step):
                dve.wait_ge(rstd_done, now.at(rstd_done, LAYERS + 1))
                for t in range(TW):
                    v.tensor_scalar(x_in[:, t, :], x_in[:, t, :], mean_var[:, t, 0:1], rstd[:, t:t + 1],
                                    ALU.subtract, ALU.mult).then_inc(x_ready, 1)

            def talk_qk(step):
                dve.wait_ge(emptied["V"], now.at(emptied["V"], filling[step, "V"]))
                if not now.first:
                    dve.wait_ge(filled["S1"], now.fill(("scores", TILES - 1), "S1", ago=1))
                v.tensor_tensor(t_k, k_rope[:, ::-1, :], rope_sin[:, None, :].to_broadcast([P, 2, N]),
                                ALU.mult).then_inc(k_parts, 1)
                dve.wait_ge(k_parts, now.at(k_parts, 1))
                v.tensor_tensor(k_rope, k_rope, rope_cos[:, None, :].to_broadcast([P, 2, N]),
                                ALU.mult).then_inc(k_parts, 1)
                dve.wait_ge(k_parts, now.at(k_parts, 2))
                v.tensor_tensor(k_rope[:, 0], k_rope[:, 0], t_k[:, 0], ALU.subtract)
                v.tensor_tensor(k_rope[:, 1], k_rope[:, 1], t_k[:, 1], ALU.add).then_inc(k_roped, 1)
                dve.wait_ge(k_roped, now.at(k_roped, 1))
                v.tensor_copy(k_hi[:], k_rope).then_inc(k_hi_done, 1)
                dve.wait_ge(k_hi_done, now.at(k_hi_done, 1))
                v.tensor_tensor(k_lo[:], k_rope, k_hi[:].bitcast(F32), ALU.subtract).then_inc(k_lo_done, 1)

            def talk_v(step):
                if not now.first:
                    dve.wait_ge(filled["V"], now.fill(("values", CHUNKS - 1), "V", ago=1))
                for t in range(TW):
                    k = f"S{t // 2}"
                    if t % 2 == 0:
                        dve.wait_ge(filled[k], now.fill(step, k))
                    ins = v.tensor_tensor(v_pad[:, t, :, 0:GD],
                                          bank[k][:, (t % 2) * D:(t % 2 + 1) * D].rearrange("p (g d) -> p g d", d=GD),
                                          b_v[:].rearrange("p (g d) -> p g d", d=GD), ALU.add)
                    if t % 2:
                        ins.then_inc(emptied[k], 1)

            def mixers(n):
                k = f"S{n % 2}"
                dve.wait_ge(emptied[k], now.fill(("scores", n), k))
                if now.past(n - 1):
                    dve.wait_ge(mixer_done, now.at(mixer_done, n - 1))
                v.reciprocal(row_inv[:, n % 2:n % 2 + 1], row_sum[:, n % PB:n % PB + 1]).then_inc(inv_done, 1)
                if now.past(not (n < 2)):
                    dve.wait_ge(filled["M"], now.fill(("mix", (n - 2) % TILES), "M", ago=n < 2))
                dve.wait_ge(inv_done, now.at(inv_done, n + 1))
                v.tensor_scalar(mixer_n[:, n % 2, :], mixer[:].rearrange("p g i -> p (g i)"),
                                row_inv[:, n % 2:n % 2 + 1], None, ALU.mult).then_inc(mixer_done, 1)

            def scores(step, n):
                k = f"S{n % 2}"
                dve.wait_ge(filled[k], now.fill(step, k))
                if now.past(not (n < 2)):
                    dve.wait_ge(emptied[k], now.fill(("scores", (n - 2) % TILES), k, ago=n < 2))
                v.tensor_reduce(neg_max[:, n % 2:n % 2 + 1], bank[k][:], AX.X, ALU.max, negate=True)\
                    .then_inc(max_done, 1)
                if n:
                    mixers(n - 1)

            def mix(step, n):
                if n == TILES - LAG:
                    mixers(TILES - 1)
                if n % 2:
                    dve.wait_ge(filled["M"], now.fill(step, "M"))
                    store_mixed(dve, v.tensor_copy, now, n)

            def project(step, t):
                dve.wait_ge(filled["V"], now.fill(step, "V"))
                if t == 0:
                    if now.past(0):
                        dve.wait_ge(gated_done, now.at(gated_done, 0))
                v.tensor_tensor(s_tok[:, t, :], bank["V"][:, 0:D], b_out[:], ALU.add).then_inc(emptied["V"], 1)

            def qkv(step, l, t):
                w = TW * l + t
                if now.past(w):
                    dve.wait_ge(rot_added, now.at(rot_added, w))
                for j in range(2):
                    dve.wait_ge(filled[f"F{j}"], now.fill(step, f"F{j}"))
                    src = bank[f"F{j}"][:].rearrange("p (h s d) -> p h s d", h=H, s=2)
                    for k, (dst, x) in enumerate([(rot_a, src), (rot_b, src[:, :, ::-1, :])]):
                        tab = rot[l][:, 2 * j + k, t, :].rearrange("p (s d) -> p s d", s=2)
                        ins = v.tensor_tensor(dst[:, j, :].rearrange("p (h s d) -> p h s d", h=H, s=2), x,
                                              tab[:, None, :, :].to_broadcast([P, H, 2, HD // 2]), ALU.mult)
                    ins.then_inc(rot_done, 1)
                if now.past(w):
                    dve.wait_ge(clip_done, now.at(clip_done, w))
                for j in range(2):
                    dve.wait_ge(emptied[f"F{j}"], now.fill(step, f"F{j}"))
                    v.tensor_reduce(norms[:, j * H:(j + 1) * H], sq[:, j, :].rearrange("p (h d) -> p h d", h=H),
                                    AX.X, ALU.add).then_inc(norm_done, 1)
                dve.wait_ge(norm_done, now.at(norm_done, 2 * w + 2))
                if now.past(w):
                    dve.wait_ge(inv_norm_done, now.at(inv_norm_done, w))
                v.tensor_scalar(norms_c[:], norms[:], 1e-24, None, ALU.max).then_inc(clip_done, 1)

            def join(step, l, t):
                w = TW * l + t
                if now.past(w):
                    for k, step_k in (("F3", "q_turn"), ("V", "k_turn")):
                        dve.wait_ge(filled[k], now.fill((step_k, *window_before(l, t)), k, ago=not w))
                if not t and (l or not now.first):
                    c = ("up", (l - 1) % LAYERS, HC - 1)
                    dve.wait_ge(emptied[banks_of(c)[0]], now.fill(c, banks_of(c)[0], ago=not l))
                dve.wait_ge(rot_done, now.at(rot_done, 2 * w + 2))
                v.tensor_tensor(qk_tok, rot_a, rot_b, ALU.add).then_inc(rot_added, 1)

            def k_turn(step, l, t):
                if t == 0:
                    if now.past(not (not l)):
                        dve.wait_ge(filled["F3"], now.fill(("down", (l - 1) % LAYERS, TW - 1), "F3", ago=not l))
                dve.wait_ge(filled["V"], now.fill(step, "V"))
                v.tensor_copy(kT[:, :, t * P:(t + 1) * P], bank["V"][:].rearrange("p (c i) -> p c i", c=4))\
                    .then_inc(emptied["V"], 1)

            def local_scores(step, l, u):
                n = TW * QUADS * l + u
                lo = P if u // QUADS == 0 else 0
                if now.past(not (n < 2)):
                    dve.wait_ge(emptied["F1"], now.fill(("local_scores", *unit_before(l, u, 2)), "F1", ago=n < 2))
                for parity in range(2):
                    k = f"F{parity}"
                    dve.wait_ge(filled[k], now.fill(step, k))
                    ins = v.tensor_reduce(l_max[:, u % 2, 2 * parity:2 * parity + 2],
                                          bank[k][:].rearrange("p (a j) -> p a j", a=2)[:, :, lo:], AX.X, ALU.max,
                                          negate=True)
                ins.then_inc(l_max_done, 1)

            def p_turn(step, l, u):
                n = TW * QUADS * l + u
                lo = 1 if u // QUADS == 0 else 0
                if now.past(not (not l and not u)):
                    dve.wait_ge(filled["V"], now.fill(("local_values", *unit_before(l, u, 1)), "V", ago=not l and not u))
                dve.wait_ge(filled["F2"], now.fill(step, "F2"))
                v.tensor_copy(pT[:, 0, :, :].rearrange("p (a j) i -> p a j i", a=2)[:, :, lo:, :],
                              bank["F2"][:].rearrange("p (a j i) -> p a j i", a=2, j=2)[:, :, lo:, :])\
                    .then_inc(emptied["F2"], 1)
            def weigh(step, l, u):
                n = TW * QUADS * l + u
                dve.wait_ge(emptied["F1"], now.fill(("local_scores", l, u), "F1"))
                if now.past(n - 1):
                    dve.wait_ge(l_scaled, now.at(l_scaled, n - 1))
                v.reciprocal(l_inv[:, u % 2, :], l_sum[:, u % 2, :]).then_inc(l_inv_done, 1)

            def local_values(step, l, u):
                t, quad = u // QUADS, u % QUADS
                dve.wait_ge(filled["V"], now.fill(step, "V"))
                if quad == 0:
                    if now.past(not (not l and not t)):
                        dve.wait_ge(filled["F3"], now.fill(("out_proj", *window_before(l, t)), "F3", ago=not l and not t))
                v.tensor_copy(o_locT[:, 2 * quad:2 * quad + 2, :],
                              bank["V"][:, 0:2 * P].rearrange("p (c i) -> p c i", c=2)).then_inc(emptied["V"], 1)

            def out_proj(step, l, t):
                dve.wait_ge(filled["F3"], now.fill(step, "F3"))
                if not l and not t and not now.first:
                    dve.wait_ge(gated_done, now.at(gated_done, 0))
                if t == 0:
                    if now.past(l):
                        dve.wait_ge(mid_b_ready, now.at(mid_b_ready, l))
                    if now.past(TW * l):
                        dve.wait_ge(h_ready, now.at(h_ready, TW * l))
                x = x_tok if l else x_in
                v.tensor_tensor(x_mid[:, t, :], bank["F3"][:, 0:D], x[:, t, :], ALU.add)\
                    .then_inc(emptied["F3"], 1)

            def shift_turn(step, l):
                dve.wait_ge(filled["F1"], now.fill(step, "F1"))
                dve.wait_ge(emptied["F3"], now.fill(("out_proj", l, TW - 1), "F3"))
                dve.wait_ge(aggr_done, now.at(aggr_done, l))
                for t in range(TW):
                    v.bn_stats(stats[:, t, 0, :], x_mid[:, t, 0:P]).then_inc(stats_done, 1)
                    v.bn_stats(stats[:, t, 1, :], bank["F1"][:, t * P:(t + 1) * P]).then_inc(stats_done, 1)
                dve.wait_ge(stats_done, now.at(stats_done, 2 * TW * (l + 1)))
                dve.wait_ge(eps_done, now.at(eps_done, l))
                v.memset(opener[:], 0.0)
                for t in range(TW):
                    ins = v.bn_aggr(mean_var[:, t, :], stats[:, t, :, :].rearrange("p a s -> p (a s)"))
                ins.then_inc(aggr_done, 1)

            def h_scale(step, l):
                dve.wait_ge(rstd_done, now.at(rstd_done, 1 + l))
                dve.wait_ge(rot_added, now.at(rot_added, TW * (l + 1)))
                dve.wait_ge(qk_ready, now.at(qk_ready, 2 * TW * (l + 1)))
                for t in range(TW):
                    v.tensor_scalar(h_tok[:, t, 0:P], x_mid[:, t, 0:P], mean_var[:, t, 0:1], rstd[:, t:t + 1],
                                    ALU.subtract, ALU.mult).then_inc(h_ready, 1)
                for t in range(TW):
                    ins = v.tensor_scalar(h_tok[:, t, P:D], bank["F1"][:, t * P:(t + 1) * P], mean_var[:, t, 0:1],
                                          rstd[:, t:t + 1], ALU.subtract, ALU.mult)
                ins.then_inc(emptied["F1"], 1)

            def up(step, l, i):
                ka, kg = banks_of(step)
                m = hidden_rows(i)
                dve.wait_ge(filled[ka], now.fill(step, ka))
                dve.wait_ge(emptied[kg], now.fill(step, kg))
                v.scalar_tensor_tensor(hidden[0:m, i, :], bank[ka][0:m, :], b_1[l][0:m, i:i + 1], gelu[0:m, i % 2, :],
                                       op0=ALU.add, op1=ALU.mult).then_inc(emptied[ka], 1)

            def down(step, l, t):
                k = f"F{t}"
                dve.wait_ge(filled[k], now.fill(step, k))
                dve.wait_ge(mid_b_ready, now.at(mid_b_ready, l + 1))
                if not l and not t and not now.first:
                    dve.wait_ge(silu_done, now.at(silu_done, 0))
                v.tensor_tensor(x_tok[:, t, :], bank[k][:, 0:D], x_mid_b[:, t, :], ALU.add)\
                    .then_inc(emptied[k], 1)

            def bound(step):
                stream_ready(dve, now, LAYERS, ago=1)
                dve.wait_ge(mid_b_ready, now.at(mid_b_ready, 0))
                dve.wait_ge(h_ready, now.at(h_ready, 0))
                v.tensor_scalar(x_mid[:], x_tok[:], LEAST, None, ALU.max).then_inc(bounded, 1)

            def sigmoid(step):
                dve.wait_ge(exp_done, now.at(exp_done, 0))
                v.tensor_scalar(x_mid[:], x_mid[:], 1.0, None, ALU.add).then_inc(one_plus, 1)
                dve.wait_ge(one_plus, now.at(one_plus, 0))
                v.reciprocal(x_mid[:], x_mid[:]).then_inc(sig_done, 1)

            steps = {
                "norm": norm, "scale": scale, "talk_qk": talk_qk, "talk_v": talk_v, "scores": scores, "mix": mix,
                "project": project, "h_scale": h_scale,
                "qkv": qkv, "join": join, "k_turn": k_turn, "local_scores": local_scores, "weigh": weigh, "p_turn": p_turn,
                "local_values": local_values, "out_proj": out_proj, "shift_turn": shift_turn, "up": up, "down": down,
                "bound": bound, "sigmoid": sigmoid,
            }

            now.run(dve, steps)

        @block.gpsimd
        def _(pool):
            now = Counts()
            g = nc.gpsimd
            pool.dma_start(x_in[:], a["x"][0]).then_inc(x_loaded, 16)
            pool.wait_ge(pads, 5)
            pool.wait_ge(loads, LOADED)
            pool.wait_ge(tables, TABLES)

            def inverse_std(n):
                pool.wait_ge(aggr_done, now.at(aggr_done, n))
                g.tensor_tensor(var_eps[:], mean_var[:, :, 1], eps[:], ALU.add).then_inc(eps_done, 1)
                pool.wait_ge(eps_done, now.at(eps_done, n))
                if n == LAYERS + 1:
                    if not now.ahead:
                        pool.wait_ge(emptied["F1"], now.fill(("shift_turn", LAYERS - 1), "F1"))
                elif n == 1:
                    pool.wait_ge(x_ready, now.at(x_ready, 0))
                else:
                    pool.wait_ge(emptied["F1"], now.fill(("shift_turn", n - 2), "F1"))
                g.tensor_tensor(rstd[:], var_eps[:], minus_half[:, 0:TW], ALU.pow).then_inc(rstd_done, 1)

            def norm(step):
                inverse_std(LAYERS + 1)

            def talk_qk(step):
                pool.wait_ge(emptied["S1"], now.fill(step, "S1"))
                if now.past(0):
                    pool.wait_ge(q_mixed, now.at(q_mixed, 0))
                g.tensor_tensor(q_rope[:], raw_qk[:, 0:2, :], rope_cos[:, None, :].to_broadcast([P, 2, N]),
                                ALU.mult).then_inc(q_parts, 1)
                for s in range(2):
                    ins = g.tensor_tensor(t_q[:, s, :], raw_qk[:, 1 - s, :], rope_sin[:], ALU.mult)
                ins.then_inc(q_parts, 1)
                pool.wait_ge(q_parts, now.at(q_parts, 2))
                g.tensor_tensor(q_rope[:, 0], q_rope[:, 0], t_q[:, 0], ALU.subtract)
                g.tensor_tensor(q_rope[:, 1], q_rope[:, 1], t_q[:, 1], ALU.add).then_inc(q_roped, 1)

            def expand(step, c):
                pool.wait_ge(q_roped, now.at(q_roped, 1))
                if now.past(c):
                    pool.wait_ge(q_lo_done, now.at(q_lo_done, c))
                shape = [P, ET, GH, RI]
                for s in range(2):
                    q = q_rope[:, s, c * ET * RI:(c + 1) * ET * RI].rearrange("p (m i) -> p m i", m=ET)
                    g.tensor_tensor(q_mix[:, s].rearrange("p m (g i) -> p m g i", g=GH),
                                    q[:, :, None, :].to_broadcast(shape),
                                    w_pre[:, None, :, None].to_broadcast(shape), ALU.mult).then_inc(q_mixed, 1)

            def part(step, c):
                pool.wait_ge(q_hi_done, now.at(q_hi_done, c + 1))
                g.tensor_tensor(q_lo[:, c % QB], q_mix[:], q_hi[:, c % QB].bitcast(F32), ALU.subtract)\
                    .then_inc(q_lo_done, 1)

            def qkv(step, l, t):
                w = TW * l + t
                pool.wait_ge(clip_done, now.at(clip_done, w + 1))
                if now.past(2 * w):
                    pool.wait_ge(qk_ready, now.at(qk_ready, 2 * w))
                g.tensor_tensor(inv_norms[:], norms_c[:], minus_half[:], ALU.pow).then_inc(inv_norm_done, 1)

            def join(step, l, t):
                w = TW * l + t
                pool.wait_ge(inv_norm_done, now.at(inv_norm_done, w + 1))
                pool.wait_ge(rot_added, now.at(rot_added, w + 1))
                for j in range(2):
                    g.tensor_tensor(qk_tok[:, j, :].rearrange("p (h d) -> p h d", h=H),
                                    qk_tok[:, j, :].rearrange("p (h d) -> p h d", h=H),
                                    inv_norms[:, j * H:(j + 1) * H, None].to_broadcast([P, H, HD]), ALU.mult)\
                        .then_inc(qk_ready, 1)

            def weigh(step, l, u):
                n = TW * QUADS * l + u
                lo = P if u // QUADS == 0 else 0
                pool.wait_ge(l_inv_done, now.at(l_inv_done, n + 1))
                g.tensor_tensor(l_probs[:, u % LB, :, lo:], l_probs[:, u % LB, :, lo:],
                                l_inv[:, u % 2, :, None].to_broadcast([P, 4, 2 * P - lo]), ALU.mult)\
                    .then_inc(l_scaled, 1)

            def half_turn(step, l):
                pool.wait_ge(emptied["F3"], now.fill(("out_proj", l, TW - 1), "F3"))
                g.tensor_tensor(x_mid_b, x_mid[:], b_2[l][:, None, :].to_broadcast([P, TW, D]), ALU.add)\
                    .then_inc(mid_b_ready, 1)
                if not l:
                    pool.dma_start(x_in[:], a["x_next"][bass.ds(now.b + 1, 1)].rearrange("a p t f -> (a p) t f"))\
                        .then_inc(x_loaded, 16)

            def shift_turn(step, l):
                inverse_std(1 + l)

            def silu(step):
                pool.wait_ge(sig_done, now.at(sig_done, 0))
                g.tensor_tensor(x_mid[:], x_mid[:], x_tok[:], ALU.mult).then_inc(silu_done, 1)

            def gated(step):
                pool.wait_ge(emptied["V"], now.fill(("project", TW - 1), "V", ago=1))
                pool.wait_ge(silu_done, now.at(silu_done, 0))
                g.tensor_tensor(s_tok[:], s_tok[:], x_mid[:], ALU.mult).then_inc(gated_done, 1)

            def store(step):
                pool.wait_ge(gated_done, now.at(gated_done, 0))
                pool.wait_ge(keep_loaded, now.at(keep_loaded, 0))
                g.tensor_tensor(x_keep[:], s_tok[:], x_keep[:], ALU.add).then_inc(o_ready, 1)
                pool.wait_ge(o_ready, now.at(o_ready, 0))
                pool.dma_start(out[bass.ds(now.b - 1, 1)].rearrange("a (t p) f -> (a p) t f", p=P), x_keep[:])\
                    .then_inc(stored, 16)

            def keep(step):
                if not now.first:
                    pool.wait_ge(stored, now.at(stored, 0))
                    g.tensor_tensor(opener_p[:], eps[:, 0:1], eps[:, 0:1], ALU.add)
                pool.dma_start(x_keep[:], a["x_next"][bass.ds(now.b, 1)].rearrange("a p t f -> (a p) t f"))\
                    .then_inc(keep_loaded, 16)

            steps = {
                "norm": norm, "talk_qk": talk_qk, "expand": expand, "part": part, "qkv": qkv, "join": join,
                "weigh": weigh, "half_turn": half_turn,
                "shift_turn": shift_turn, "silu": silu, "gated": gated, "store": store,
                "keep": keep,
            }

            now.run(pool, steps)


def shape_constants():
    f = np.float32
    c = {"ident": np.eye(P, dtype=f)}
    i, j = np.arange(P)[:, None], np.arange(P)[None, :]
    prev, cur = np.where(i > j, MASKED, 0.0), np.where(i < j, MASKED, 0.0)
    c["mask"] = np.tile(np.concatenate([prev, cur], 1), (1, 2)).astype(f)
    c["delta"] = (np.arange(P)[:, None] % RI == np.arange(RI)[None, :]).astype(f)
    inv = f(1.0) / f(10000.0) ** (np.arange(0, GD, 2, dtype=f) / f(GD))
    fr = (np.arange(N, dtype=f)[:, None] * inv[None, :]).astype(f)
    cos, sin = np.tile(np.cos(fr).T, (GH, 1)), np.tile(np.sin(fr).T, (GH, 1))
    c["rope_cos"] = cos.astype(f)
    c["rope_sin"] = sin.astype(f)
    half = np.arange(0, HD, 2, dtype=f)
    inv = f(1.0) / f(10000.0) ** (half / f(HD))
    t = np.arange(N, dtype=f)
    fr = (t[:, None] * inv[None, :]).astype(f)
    base = (half + f(0.4 * HD)) / f(1.4 * HD)
    power = (t - N // 2) / f(P // 2)
    sc = (base[None, :] ** power[:, None]).astype(f)
    two = lambda x: np.concatenate([x, x], 1)
    cos, sin, sc = two(np.cos(fr)), two(np.sin(fr)), two(sc)
    sin[:, :HD // 2] *= -1
    tab = np.stack([cos * sc * f(8), sin * sc * f(8), cos / sc, sin / sc]).astype(f)
    c["xpos"] = np.ascontiguousarray(tab.reshape(4, TW, P, HD).transpose(2, 0, 1, 3))
    return c


def laid_out(i):
    i = {k: np.asarray(v) for k, v in i.items()}
    bc = lambda x: np.ascontiguousarray(np.broadcast_to(x, (P, *x.shape)))
    kp = lambda w: np.ascontiguousarray(w.reshape(-1, P, w.shape[-1]).transpose(1, 0, 2))
    o = {}
    x = i["L0_attn_x"].reshape(B, TW, P, D).transpose(0, 2, 1, 3)
    o["x_next"] = np.ascontiguousarray(np.concatenate([x, x[:1]]))
    w = i["L0_attn_Wqkv"]
    qk = w[:2 * D].reshape(2, GH, 2, HALF, KC, P).transpose(5, 4, 0, 2, 1, 3)
    o["w_qk"] = np.ascontiguousarray(qk.reshape(P, KC, 4, P))
    bias = i["L0_attn_bqkv"]
    o["b_qk"] = np.ascontiguousarray(bias[:2 * D].reshape(2, GH, 2, HALF).transpose(1, 3, 0, 2).reshape(P, 4))
    o["w_v"] = kp(w[2 * D:].T)
    o["b_v"] = bc(bias[2 * D:])
    o["w_pre"] = np.repeat(i["L0_attn_Wpre"].T, RI, axis=0)
    o["w_post"] = np.repeat(i["L0_attn_Wpost"].T, RI, axis=0)
    wo = np.zeros((GR, PAD, GH // GR, D), w.dtype)
    wo[:, :GD] = i["L0_attn_Wout"].T.reshape(GH // GR, GR, GD, D).transpose(1, 2, 0, 3)
    o["w_out"] = wo.reshape(P, GH // GR, D)
    o["b_out"] = bc(i["L0_attn_bout"])
    qs, ks = i["L0_ffn_q_scale"], i["L0_ffn_k_scale"]
    sw = lambda s: np.concatenate([s[:, HD // 2:], s[:, :HD // 2]], 1)
    sc = np.stack([qs, sw(qs), ks, sw(ks)], 1)
    o["scales"] = np.ascontiguousarray(np.broadcast_to(sc[:, None], (LAYERS, P, 4, HD)))
    per = lambda f: np.stack([f(l) for l in range(LAYERS)])
    o["w_qkv"] = per(lambda l: kp(i["L0_ffn_wqkv"][l]))
    o["w_o"] = per(lambda l: kp(i["L0_ffn_wo"][l]))
    o["w_1"] = per(lambda l: kp(i["L0_ffn_w1"][l]))

    def padded(v):
        z = np.zeros((HC * P, *v.shape[1:]), v.dtype)
        z[:HID] = v
        return z
    o["w_2"] = per(lambda l: kp(padded(i["L0_ffn_w2"][l])))
    b1 = i["L0_ffn_b1"]
    o["b_1"] = per(lambda l: np.concatenate([padded(b1[l][:HID]).reshape(HC, P).T, padded(b1[l][HID:]).reshape(HC, P).T], 1))
    o["b_2"] = per(lambda l: bc(i["L0_ffn_b2"][l]))
    o["ln_w"] = per(lambda l: np.concatenate([i["L0_ffn_ln_g"][l].reshape(KC, P).T, i["L0_ffn_ln_b"][l].reshape(KC, P).T], 1))
    return {k: np.ascontiguousarray(v) for k, v in o.items()}


def kernel(**inputs):
    import concourse.bacc as bacc
    from concourse.bass_utils import run_bass_kernel_spmd

    arrays = {**laid_out(inputs), **shape_constants()}
    nc = bacc.Bacc("TRN2", target_bir_lowering=False, num_devices=1)
    a = {k: nc.dram_tensor(f"in_{k}", v.shape, mybir.dt.from_np(v.dtype), kind="ExternalInput").ap()
         for k, v in arrays.items()}
    a["x"] = a["x_next"]
    out = nc.dram_tensor("out_y", (B, N, D), F32, kind="ExternalOutput").ap()
    gate_network_kernel(nc, a, out)
    r = run_bass_kernel_spmd(nc, [{f"in_{k}": v for k, v in arrays.items()}], core_ids=[0])
    return r.results[0]["out_y"]
```
